# Optimizing a Trainium2 kernel written in Bass

```python
import numpy as np
import jax
import jax.numpy as jnp

def _softmax(x, axis=-1):
    return jax.nn.softmax(x, axis=axis)

def _gelu(x):
    return jax.nn.gelu(x, approximate=True)

def _silu(x):
    return jax.nn.silu(x)

def _sigmoid(x):
    return jax.nn.sigmoid(x)

def _layernorm(x, axis=-1, eps=1e-05):
    m = jnp.mean(x, axis=axis, keepdims=True)
    v = jnp.var(x, axis=axis, keepdims=True)
    return (x - m) / jnp.sqrt(v + eps)

def _scatter_add(tgt, idx, src, axis=0):
    return tgt.at[idx].add(src)

def _segment_sum(src, seg, n):
    return jax.ops.segment_sum(src, seg, n)
kernel_name = 'mk_gps_d4_gnn_r32_333f6f'

def setup_inputs(seed: int=0):
    np.random.seed(seed)
    _w = jnp.asarray

    def _rec_inputs():
        import jax
        import jax.numpy as jnp
        _gk = jax.random.key(seed)
        x = -8.776e-05 + 1 * jax.random.normal(jax.random.fold_in(_gk, 1), (625, 256), jnp.float32)
        src = jax.random.randint(jax.random.fold_in(_gk, 2), (20000,), 0, 625, jnp.int32)
        dst = jnp.minimum((625 * jax.random.uniform(jax.random.fold_in(_gk, 3), (20000,)) ** 2.0).astype(jnp.int32), 19999)
        _o = jnp.argsort(dst, stable=True)
        src = src[_o]
        dst = dst[_o]
        return (x, src, dst)
    x, src, dst = _rec_inputs()

    def _L0_gnn_setup():
        import jax, jax.numpy as jnp
        import numpy as np
        N_NODES = 625
        key = jax.random.key(seed)
        k1, k2, k3, k4 = jax.random.split(key, 4)
        d = 256
        E = 10000
        x = jax.random.normal(k1, (N_NODES, d), dtype=jnp.float32)
        edge_index = jax.random.randint(k2, (2, E), 0, N_NODES, dtype=jnp.int64)
        limit = float(np.sqrt(6.0 / (d + d)))
        W_l = jax.random.uniform(k3, (d, d), dtype=jnp.float32, minval=-limit, maxval=limit)
        W_r = jax.random.uniform(k4, (d, d), dtype=jnp.float32, minval=-limit, maxval=limit)
        b_r = jnp.zeros((d,), dtype=jnp.float32)
        return {'x': x, 'edge_index': edge_index, 'W_l': W_l, 'W_r': W_r, 'b_r': b_r}
    _L0_gnn_all = _L0_gnn_setup()
    _L0_gnn_in = {k: v for k, v in _L0_gnn_all.items() if k in ('W_l', 'W_r', 'b_r')}
    del _L0_gnn_all

    def _L0_mix_setup():
        import jax, jax.numpy as jnp
        import numpy as np
        EPS = 1e-05

        def _layernorm(x, weight, bias):
            mean = jnp.mean(x, axis=-1, keepdims=True)
            std = jnp.std(x, axis=-1, keepdims=True, ddof=1)
            out = (x - mean) / (std + EPS)
            return weight * out + bias
        key = jax.random.key(seed)
        B, N, C = (4, 1024, 256)
        H, hc = (8, C // 8)
        kx, = jax.random.split(key, 1)
        x = jax.random.normal(kx, (B, N, C), dtype=jnp.float32)
        return {'x': x, 'kln_weight': jnp.ones((H, 1, hc), dtype=jnp.float32), 'kln_bias': jnp.zeros((H, 1, hc), dtype=jnp.float32), 'vln_weight': jnp.ones((H, 1, hc), dtype=jnp.float32), 'vln_bias': jnp.zeros((H, 1, hc), dtype=jnp.float32)}
    _L0_mix_all = _L0_mix_setup()
    _L0_mix_in = {k: v for k, v in _L0_mix_all.items() if k in ('kln_weight', 'kln_bias', 'vln_weight', 'vln_bias')}
    del _L0_mix_all

    def _L0_ffn_setup():
        import jax, jax.numpy as jnp
        import numpy as np
        B, T, D, H, E = (16, 128, 256, 512, 8)
        key = jax.random.key(seed)
        ks = jax.random.split(key, 5)
        x = jax.random.normal(ks[0], (B, T, D), dtype=jnp.float32)
        gate_w = jax.random.normal(ks[1], (D, E), dtype=jnp.float32) * 0.02
        gate_b = jnp.zeros((E,), dtype=jnp.float32)
        W1 = jax.random.normal(ks[2], (E, D, H), dtype=jnp.float32) * 0.02
        b1 = jnp.zeros((E, H), dtype=jnp.float32)
        W2 = jax.random.normal(ks[3], (E, H, D), dtype=jnp.float32) * 0.02
        b2 = jnp.zeros((E, D), dtype=jnp.float32)
        return {'x': x, 'gate_w': gate_w, 'gate_b': gate_b, 'W1': W1, 'b1': b1, 'W2': W2, 'b2': b2}
    _L0_ffn_all = _L0_ffn_setup()
    _L0_ffn_in = {k: v for k, v in _L0_ffn_all.items() if k in ('gate_w', 'gate_b', 'W1', 'b1', 'W2', 'b2')}
    del _L0_ffn_all

    def _L1_gnn_setup():
        import jax, jax.numpy as jnp
        import numpy as np
        N_NODES = 50000
        N_EDGES = 25000
        D_IN = 256
        D_HID = 256
        D_OUT = 256
        GAMMA = 0.0
        K_STEPS = 6

        def _spmm(h, src, dst, inv_deg):
            msg = h[src]
            agg = jax.ops.segment_sum(msg, dst, num_segments=h.shape[0])
            return agg * inv_deg[:, None]

        def _linear_diffusion(h, src, dst, gamma=GAMMA, k=K_STEPS):
            n = h.shape[0]
            deg = jax.ops.segment_sum(jnp.ones((src.shape[0],), h.dtype), dst, num_segments=n)
            inv_deg = 1.0 / jnp.clip(deg, 1.0)
            out = h
            term = h
            for i in range(1, k + 1):
                term = (_spmm(term, src, dst, inv_deg) + gamma * term) / float(i)
                out = out + term
            return out
        key = jax.random.key(seed)
        ks = jax.random.split(key, 8)
        h = jax.random.normal(ks[0], (N_NODES, D_IN), dtype=jnp.float32)
        src = jax.random.randint(ks[1], (N_EDGES,), 0, N_NODES, dtype=jnp.int64)
        dst = jax.random.randint(ks[2], (N_EDGES,), 0, N_NODES, dtype=jnp.int64)
        s_in = 1.0 / np.sqrt(D_IN)
        s_hid = 1.0 / np.sqrt(D_HID)
        W_in = jax.random.uniform(ks[3], (D_HID, D_IN), jnp.float32, -s_in, s_in)
        b_in = jax.random.uniform(ks[4], (D_HID,), jnp.float32, -s_in, s_in)
        W_out = jax.random.uniform(ks[5], (D_OUT, D_HID), jnp.float32, -s_hid, s_hid)
        b_out = jax.random.uniform(ks[6], (D_OUT,), jnp.float32, -s_hid, s_hid)
        return {'h': h, 'src': src, 'dst': dst, 'W_in': W_in, 'b_in': b_in, 'W_out': W_out, 'b_out': b_out}
    _L1_gnn_all = _L1_gnn_setup()
    _L1_gnn_in = {k: v for k, v in _L1_gnn_all.items() if k in ('W_in', 'b_in', 'W_out', 'b_out')}
    del _L1_gnn_all

    def _L1_mix_setup():
        import jax, jax.numpy as jnp
        import numpy as np
        N, F, C, H = (32, 128, 256, 8)
        D = C // H
        EPS_ATTN = 1e-06
        EPS_LN = 1e-05

        def layer_norm(x, g, b):
            mu = jnp.mean(x, axis=-1, keepdims=True)
            var = jnp.var(x, axis=-1, keepdims=True)
            return (x - mu) * jax.lax.rsqrt(var + EPS_LN) * g + b
        key = jax.random.key(seed)
        ks = jax.random.split(key, 8)
        s = 1.0 / np.sqrt(C)
        return {'x': jax.random.normal(ks[0], (N, F, C), jnp.float32), 'Wqkv': jax.random.uniform(ks[1], (3 * C, C), jnp.float32, -s, s), 'ln1_g': jnp.ones((C,), jnp.float32), 'ln1_b': jnp.zeros((C,), jnp.float32), 'W1': jax.random.uniform(ks[2], (C, C), jnp.float32, -s, s), 'b1': jax.random.uniform(ks[3], (C,), jnp.float32, -s, s), 'W2': jax.random.uniform(ks[4], (C, C), jnp.float32, -s, s), 'b2': jax.random.uniform(ks[5], (C,), jnp.float32, -s, s), 'ln2_g': jnp.ones((C,), jnp.float32), 'ln2_b': jnp.zeros((C,), jnp.float32)}
    _L1_mix_all = _L1_mix_setup()
    _L1_mix_in = {k: v for k, v in _L1_mix_all.items() if k in ('Wqkv', 'ln1_g', 'ln1_b', 'W1', 'b1', 'W2', 'b2', 'ln2_g', 'ln2_b')}
    del _L1_mix_all

    def _L1_ffn_setup():
        import jax, jax.numpy as jnp
        import numpy as np
        BN_EPS = 0.001

        def _bn(h, g, b, m, v):
            return g * (h - m) * jax.lax.rsqrt(v + BN_EPS) + b
        key = jax.random.key(seed)
        ks = jax.random.split(key, 8)
        B, F, Df = (256, 64, 256)
        E, H, D = (8, 256, 256)
        s1 = 1.0 / np.sqrt(Df)
        s2 = 1.0 / np.sqrt(H)
        return {'x': jax.random.normal(ks[0], (B, F, Df), jnp.float32), 'Wr': jax.random.normal(ks[1], (Df, E), jnp.float32) * s1, 'br': jnp.zeros((E,), jnp.float32), 'W1': jax.random.normal(ks[2], (E, Df, H), jnp.float32) * s1, 'b1': jnp.zeros((E, H), jnp.float32), 'g1': jnp.ones((E, H), jnp.float32), 'be1': jnp.zeros((E, H), jnp.float32), 'm1': jnp.zeros((E, H), jnp.float32), 'v1': jnp.ones((E, H), jnp.float32), 'W2': jax.random.normal(ks[3], (E, H, H), jnp.float32) * s2, 'b2': jnp.zeros((E, H), jnp.float32), 'g2': jnp.ones((E, H), jnp.float32), 'be2': jnp.zeros((E, H), jnp.float32), 'm2': jnp.zeros((E, H), jnp.float32), 'v2': jnp.ones((E, H), jnp.float32), 'Wo': jax.random.normal(ks[4], (E, H, D), jnp.float32) * s2, 'bo': jnp.zeros((E, D), jnp.float32)}
    _L1_ffn_all = _L1_ffn_setup()
    _L1_ffn_in = {k: v for k, v in _L1_ffn_all.items() if k in ('Wr', 'br', 'W1', 'b1', 'g1', 'be1', 'm1', 'v1', 'W2', 'b2', 'g2', 'be2', 'm2', 'v2', 'Wo', 'bo')}
    del _L1_ffn_all

    def _L2_gnn_setup():
        import jax, jax.numpy as jnp
        import numpy as np
        N_NODES = 50000
        N_EDGES = 50000
        H_SIZE = 256
        HEADS = 8
        HEAD_DIM = H_SIZE // HEADS
        NEG_SLOPE = 0.2
        key = jax.random.key(seed)
        k_x, k_e, k_w, k_as, k_ad, k_b = jax.random.split(key, 6)
        x = jax.random.normal(k_x, (N_NODES, H_SIZE), dtype=jnp.float32)
        edge_index = jax.random.randint(k_e, (2, N_EDGES), 0, N_NODES, dtype=jnp.int64)
        scale = 1.0 / np.sqrt(H_SIZE)
        W = jax.random.normal(k_w, (H_SIZE, HEADS, HEAD_DIM), dtype=jnp.float32) * scale
        att_src = jax.random.normal(k_as, (HEADS, HEAD_DIM), dtype=jnp.float32) * scale
        att_dst = jax.random.normal(k_ad, (HEADS, HEAD_DIM), dtype=jnp.float32) * scale
        bias = jnp.zeros((H_SIZE,), dtype=jnp.float32)
        return {'x': x, 'edge_index': edge_index, 'W': W, 'att_src': att_src, 'att_dst': att_dst, 'bias': bias}
    _L2_gnn_all = _L2_gnn_setup()
    _L2_gnn_in = {k: v for k, v in _L2_gnn_all.items() if k in ('W', 'att_src', 'att_dst', 'bias')}
    del _L2_gnn_all

    def _L2_mix_setup():
        import jax, jax.numpy as jnp
        import numpy as np
        HEADS = 4
        DIM_HEAD = 32
        key = jax.random.key(seed)
        k1, k2, k3 = jax.random.split(key, 3)
        B, L, D = (16, 256, 256)
        hidden = HEADS * DIM_HEAD
        x = jax.random.normal(k1, (B, L, D), dtype=jnp.float32)
        W_qkv = jax.random.normal(k2, (D, 3 * hidden), dtype=jnp.float32) * D ** (-0.5)
        W_out = jax.random.normal(k3, (hidden, D), dtype=jnp.float32) * hidden ** (-0.5)
        b_out = jnp.zeros((D,), dtype=jnp.float32)
        return {'x': x, 'W_qkv': W_qkv, 'W_out': W_out, 'b_out': b_out}
    _L2_mix_all = _L2_mix_setup()
    _L2_mix_in = {k: v for k, v in _L2_mix_all.items() if k in ('W_qkv', 'W_out', 'b_out')}
    del _L2_mix_all

    def _L2_ffn_setup():
        import jax, jax.numpy as jnp
        import numpy as np
        IN_CH = 256
        OUT_CH = 256
        key = jax.random.key(seed)
        kx, kw, kb = jax.random.split(key, 3)
        x = jax.random.normal(kx, (8, 128, IN_CH), dtype=jnp.float32)
        bound = 1.0 / np.sqrt(IN_CH)
        weight = jax.random.uniform(kw, (OUT_CH, IN_CH), dtype=jnp.float32, minval=-bound, maxval=bound)
        bias = jax.random.uniform(kb, (OUT_CH,), dtype=jnp.float32, minval=-bound, maxval=bound)
        return {'x': x, 'weight': weight, 'bias': bias}
    _L2_ffn_all = _L2_ffn_setup()
    _L2_ffn_in = {k: v for k, v in _L2_ffn_all.items() if k in ('weight', 'bias')}
    del _L2_ffn_all

    def _L3_gnn_setup():
        import jax, jax.numpy as jnp
        import numpy as np
        N_NODES = 50000
        N_EDGES = 25000
        D_IN = 256
        D_OUT = 256
        key = jax.random.key(seed)
        k1, k2, k3, k4 = jax.random.split(key, 4)
        bound = 1.0 / np.sqrt(D_IN)
        vertex_features = jax.random.normal(k1, (N_NODES, D_IN), dtype=jnp.float32)
        edge_index = jax.random.randint(k2, (2, N_EDGES), 0, N_NODES, dtype=jnp.int32)
        w0 = jax.random.uniform(k3, (D_IN, D_OUT), minval=-bound, maxval=bound, dtype=jnp.float32)
        w1 = jax.random.uniform(k4, (D_IN, D_OUT), minval=-bound, maxval=bound, dtype=jnp.float32)
        return {'vertex_features': vertex_features, 'edge_index': edge_index, 'w0': w0, 'w1': w1}
    _L3_gnn_all = _L3_gnn_setup()
    _L3_gnn_in = {k: v for k, v in _L3_gnn_all.items() if k in ('w0', 'w1')}
    del _L3_gnn_all

    def _L3_mix_setup():
        import math
        import jax, jax.numpy as jnp
        import numpy as np
        EPS_DIV = 1e-07
        EPS_NORM = 1e-12

        def _l2_normalize(x, axis):
            n = jnp.sqrt(jnp.sum(x * x, axis=axis, keepdims=True))
            return x / jnp.maximum(n, EPS_NORM)
        key = jax.random.key(seed)
        ks = jax.random.split(key, 5)
        b, N, C = (8, 128, 256)
        x = jax.random.normal(ks[0], (b, N, C), dtype=jnp.float32)
        W_qkv = jax.random.normal(ks[1], (C, 3 * C), dtype=jnp.float32) * (1.0 / math.sqrt(C))
        b_qkv = jax.random.normal(ks[2], (3 * C,), dtype=jnp.float32) * 0.02
        W_out = jax.random.normal(ks[3], (C, C), dtype=jnp.float32) * (1.0 / math.sqrt(C))
        b_out = jax.random.normal(ks[4], (C,), dtype=jnp.float32) * 0.02
        return {'x': x, 'W_qkv': W_qkv, 'b_qkv': b_qkv, 'W_out': W_out, 'b_out': b_out}
    _L3_mix_all = _L3_mix_setup()
    _L3_mix_in = {k: v for k, v in _L3_mix_all.items() if k in ('W_qkv', 'b_qkv', 'W_out', 'b_out')}
    del _L3_mix_all

    def _L3_ffn_setup():
        import jax, jax.numpy as jnp
        import numpy as np
        TOP_K = 2
        LN_EPS = 1e-05
        key = jax.random.key(seed)
        ks = jax.random.split(key, 8)
        B, S, D, E, H = (16, 1024, 256, 8, 1024)
        x = jax.random.normal(ks[0], (B, S, D), dtype=jnp.float32)
        Wr = jax.random.normal(ks[1], (D, E), dtype=jnp.float32) * 0.1
        br = jnp.zeros((E,), dtype=jnp.float32)
        ln_g = jnp.ones((E, D), dtype=jnp.float32)
        ln_b = jnp.zeros((E, D), dtype=jnp.float32)
        W1 = jax.random.normal(ks[2], (E, D, H), dtype=jnp.float32) * (1.0 / np.sqrt(D))
        b1 = jnp.zeros((E, H), dtype=jnp.float32)
        W2 = jax.random.normal(ks[3], (E, H, D), dtype=jnp.float32) * (1.0 / np.sqrt(H))
        b2 = jnp.zeros((E, D), dtype=jnp.float32)
        return {'x': x, 'Wr': Wr, 'br': br, 'ln_g': ln_g, 'ln_b': ln_b, 'W1': W1, 'b1': b1, 'W2': W2, 'b2': b2}
    _L3_ffn_all = _L3_ffn_setup()
    _L3_ffn_in = {k: v for k, v in _L3_ffn_all.items() if k in ('Wr', 'br', 'ln_g', 'ln_b', 'W1', 'b1', 'W2', 'b2')}
    del _L3_ffn_all
    return {'x': x, 'src': src, 'dst': dst, 'L0_gnn_W_l': _L0_gnn_in['W_l'], 'L0_gnn_W_r': _L0_gnn_in['W_r'], 'L0_gnn_b_r': _L0_gnn_in['b_r'], 'L0_mix_kln_weight': _L0_mix_in['kln_weight'], 'L0_mix_kln_bias': _L0_mix_in['kln_bias'], 'L0_mix_vln_weight': _L0_mix_in['vln_weight'], 'L0_mix_vln_bias': _L0_mix_in['vln_bias'], 'L0_ffn_gate_w': _L0_ffn_in['gate_w'], 'L0_ffn_gate_b': _L0_ffn_in['gate_b'], 'L0_ffn_W1': _L0_ffn_in['W1'], 'L0_ffn_b1': _L0_ffn_in['b1'], 'L0_ffn_W2': _L0_ffn_in['W2'], 'L0_ffn_b2': _L0_ffn_in['b2'], 'L1_gnn_W_in': _L1_gnn_in['W_in'], 'L1_gnn_b_in': _L1_gnn_in['b_in'], 'L1_gnn_W_out': _L1_gnn_in['W_out'], 'L1_gnn_b_out': _L1_gnn_in['b_out'], 'L1_mix_Wqkv': _L1_mix_in['Wqkv'], 'L1_mix_ln1_g': _L1_mix_in['ln1_g'], 'L1_mix_ln1_b': _L1_mix_in['ln1_b'], 'L1_mix_W1': _L1_mix_in['W1'], 'L1_mix_b1': _L1_mix_in['b1'], 'L1_mix_W2': _L1_mix_in['W2'], 'L1_mix_b2': _L1_mix_in['b2'], 'L1_mix_ln2_g': _L1_mix_in['ln2_g'], 'L1_mix_ln2_b': _L1_mix_in['ln2_b'], 'L1_ffn_Wr': _L1_ffn_in['Wr'], 'L1_ffn_br': _L1_ffn_in['br'], 'L1_ffn_W1': _L1_ffn_in['W1'], 'L1_ffn_b1': _L1_ffn_in['b1'], 'L1_ffn_g1': _L1_ffn_in['g1'], 'L1_ffn_be1': _L1_ffn_in['be1'], 'L1_ffn_m1': _L1_ffn_in['m1'], 'L1_ffn_v1': _L1_ffn_in['v1'], 'L1_ffn_W2': _L1_ffn_in['W2'], 'L1_ffn_b2': _L1_ffn_in['b2'], 'L1_ffn_g2': _L1_ffn_in['g2'], 'L1_ffn_be2': _L1_ffn_in['be2'], 'L1_ffn_m2': _L1_ffn_in['m2'], 'L1_ffn_v2': _L1_ffn_in['v2'], 'L1_ffn_Wo': _L1_ffn_in['Wo'], 'L1_ffn_bo': _L1_ffn_in['bo'], 'L2_gnn_W': _L2_gnn_in['W'], 'L2_gnn_att_src': _L2_gnn_in['att_src'], 'L2_gnn_att_dst': _L2_gnn_in['att_dst'], 'L2_gnn_bias': _L2_gnn_in['bias'], 'L2_mix_W_qkv': _L2_mix_in['W_qkv'], 'L2_mix_W_out': _L2_mix_in['W_out'], 'L2_mix_b_out': _L2_mix_in['b_out'], 'L2_ffn_weight': _L2_ffn_in['weight'], 'L2_ffn_bias': _L2_ffn_in['bias'], 'L3_gnn_w0': _L3_gnn_in['w0'], 'L3_gnn_w1': _L3_gnn_in['w1'], 'L3_mix_W_qkv': _L3_mix_in['W_qkv'], 'L3_mix_b_qkv': _L3_mix_in['b_qkv'], 'L3_mix_W_out': _L3_mix_in['W_out'], 'L3_mix_b_out': _L3_mix_in['b_out'], 'L3_ffn_Wr': _L3_ffn_in['Wr'], 'L3_ffn_br': _L3_ffn_in['br'], 'L3_ffn_ln_g': _L3_ffn_in['ln_g'], 'L3_ffn_ln_b': _L3_ffn_in['ln_b'], 'L3_ffn_W1': _L3_ffn_in['W1'], 'L3_ffn_b1': _L3_ffn_in['b1'], 'L3_ffn_W2': _L3_ffn_in['W2'], 'L3_ffn_b2': _L3_ffn_in['b2']}

def reference(x, src, dst, L0_gnn_W_l, L0_gnn_W_r, L0_gnn_b_r, L0_mix_kln_weight, L0_mix_kln_bias, L0_mix_vln_weight, L0_mix_vln_bias, L0_ffn_gate_w, L0_ffn_gate_b, L0_ffn_W1, L0_ffn_b1, L0_ffn_W2, L0_ffn_b2, L1_gnn_W_in, L1_gnn_b_in, L1_gnn_W_out, L1_gnn_b_out, L1_mix_Wqkv, L1_mix_ln1_g, L1_mix_ln1_b, L1_mix_W1, L1_mix_b1, L1_mix_W2, L1_mix_b2, L1_mix_ln2_g, L1_mix_ln2_b, L1_ffn_Wr, L1_ffn_br, L1_ffn_W1, L1_ffn_b1, L1_ffn_g1, L1_ffn_be1, L1_ffn_m1, L1_ffn_v1, L1_ffn_W2, L1_ffn_b2, L1_ffn_g2, L1_ffn_be2, L1_ffn_m2, L1_ffn_v2, L1_ffn_Wo, L1_ffn_bo, L2_gnn_W, L2_gnn_att_src, L2_gnn_att_dst, L2_gnn_bias, L2_mix_W_qkv, L2_mix_W_out, L2_mix_b_out, L2_ffn_weight, L2_ffn_bias, L3_gnn_w0, L3_gnn_w1, L3_mix_W_qkv, L3_mix_b_qkv, L3_mix_W_out, L3_mix_b_out, L3_ffn_Wr, L3_ffn_br, L3_ffn_ln_g, L3_ffn_ln_b, L3_ffn_W1, L3_ffn_b1, L3_ffn_W2, L3_ffn_b2):
    import jax
    import jax.numpy as jnp

    def _L0_gnn_ref(x, edge_index, W_l, W_r, b_r):
        import jax, jax.numpy as jnp
        import numpy as np
        N_NODES = 625
        src, dst = (edge_index[0], edge_index[1])
        messages = x[src]
        sums = jax.ops.segment_sum(messages, dst, num_segments=N_NODES)
        counts = jax.ops.segment_sum(jnp.ones_like(dst, dtype=x.dtype), dst, num_segments=N_NODES)
        aggr = sums / jnp.maximum(counts, 1.0)[:, None]
        out = aggr @ W_l.T + x @ W_r.T + b_r
        return out

    def _L0_mix_ref(x, kln_weight, kln_bias, vln_weight, vln_bias):
        import jax, jax.numpy as jnp
        import numpy as np
        EPS = 1e-05

        def _layernorm(x, weight, bias):
            mean = jnp.mean(x, axis=-1, keepdims=True)
            std = jnp.std(x, axis=-1, keepdims=True, ddof=1)
            out = (x - mean) / (std + EPS)
            return weight * out + bias
        B, N, C = x.shape
        H = kln_weight.shape[0]
        hc = C // H
        qkv = x.reshape(B, N, H, hc).transpose(0, 2, 1, 3)
        q = qkv
        k = _layernorm(qkv, kln_weight, kln_bias)
        v = _layernorm(qkv, vln_weight, vln_bias)
        kv = jnp.einsum('bhnd,bhne->bhde', k, v) / N
        out = jnp.einsum('bhnd,bhde->bhne', q, kv)
        out = out.transpose(0, 2, 1, 3).reshape(B, N, C)
        return out + x

    def _L0_ffn_ref(x, gate_w, gate_b, W1, b1, W2, b2):
        import jax, jax.numpy as jnp
        import numpy as np
        B, T, D, H, E = (16, 128, 256, 512, 8)
        Bb, Tt, Dd = x.shape
        Ee = gate_w.shape[1]
        xf = x.reshape(-1, Dd)
        N = xf.shape[0]
        logits = xf @ gate_w + gate_b
        probs = jax.nn.softmax(logits, axis=-1)
        top2_vals, top2_idx = jax.lax.top_k(probs, 2)
        cw = jnp.zeros((N, Ee), dtype=xf.dtype).at[jnp.arange(N)[:, None], top2_idx].add(top2_vals)

        def step(acc, params):
            w1, bb1, w2, bb2, we = params
            h = jax.nn.gelu(xf @ w1 + bb1, approximate=False)
            y = h @ w2 + bb2
            return (acc + we[:, None] * y, None)
        out, _ = jax.lax.scan(step, jnp.zeros_like(xf), (W1, b1, W2, b2, cw.T))
        return out.reshape(Bb, Tt, Dd)

    def _L1_gnn_ref(h, src, dst, W_in, b_in, W_out, b_out):
        import jax, jax.numpy as jnp
        import numpy as np
        N_NODES = 50000
        N_EDGES = 25000
        D_IN = 256
        D_HID = 256
        D_OUT = 256
        GAMMA = 0.0
        K_STEPS = 6

        def _spmm(h, src, dst, inv_deg):
            msg = h[src]
            agg = jax.ops.segment_sum(msg, dst, num_segments=h.shape[0])
            return agg * inv_deg[:, None]

        def _linear_diffusion(h, src, dst, gamma=GAMMA, k=K_STEPS):
            n = h.shape[0]
            deg = jax.ops.segment_sum(jnp.ones((src.shape[0],), h.dtype), dst, num_segments=n)
            inv_deg = 1.0 / jnp.clip(deg, 1.0)
            out = h
            term = h
            for i in range(1, k + 1):
                term = (_spmm(term, src, dst, inv_deg) + gamma * term) / float(i)
                out = out + term
            return out
        x = h @ W_in.T + b_in
        x = jax.nn.silu(x)
        x = _linear_diffusion(x, src, dst)
        x = x @ W_out.T + b_out
        return x

    def _L1_mix_ref(x, Wqkv, ln1_g, ln1_b, W1, b1, W2, b2, ln2_g, ln2_b):
        import jax, jax.numpy as jnp
        import numpy as np
        N, F, C, H = (32, 128, 256, 8)
        D = C // H
        EPS_ATTN = 1e-06
        EPS_LN = 1e-05

        def layer_norm(x, g, b):
            mu = jnp.mean(x, axis=-1, keepdims=True)
            var = jnp.var(x, axis=-1, keepdims=True)
            return (x - mu) * jax.lax.rsqrt(var + EPS_LN) * g + b
        n, f, c = x.shape
        qkv = jnp.einsum('nfc,oc->nfo', x, Wqkv)
        q, k, v = jnp.split(qkv, 3, axis=-1)
        q = q.reshape(n, f, H, D)
        k = k.reshape(n, f, H, D)
        v = v.reshape(n, f, H, D)
        q = jax.nn.elu(q) + 1.0
        k = jax.nn.elu(k) + 1.0
        kv = jnp.einsum('nshd,nshm->nhmd', k, v)
        ksum = jnp.sum(k, axis=1)
        z = 1.0 / (jnp.einsum('nlhd,nhd->nlh', q, ksum) + EPS_ATTN)
        t = jnp.einsum('nlhd,nhmd,nlh->nlhm', q, kv, z)
        t = t.reshape(n, f, c)
        x1 = layer_norm(t + x, ln1_g, ln1_b)
        h = jax.nn.gelu(jnp.einsum('nfc,oc->nfo', x1, W1) + b1, approximate=False)
        y = jnp.einsum('nfc,oc->nfo', h, W2) + b2
        return layer_norm(y + x1, ln2_g, ln2_b)

    def _L1_ffn_ref(x, Wr, br, W1, b1, g1, be1, m1, v1, W2, b2, g2, be2, m2, v2, Wo, bo):
        import jax, jax.numpy as jnp
        import numpy as np
        BN_EPS = 0.001

        def _bn(h, g, b, m, v):
            return g * (h - m) * jax.lax.rsqrt(v + BN_EPS) + b
        feat = jnp.mean(x, axis=0)
        w = jax.nn.softmax(feat @ Wr + br, axis=-1)
        h = jnp.einsum('bfd,edh->bfeh', x, W1) + b1
        h = jax.nn.relu(_bn(h, g1, be1, m1, v1))
        h = jnp.einsum('bfeh,ehk->bfek', h, W2) + b2
        h = jax.nn.relu(_bn(h, g2, be2, m2, v2))
        y = jnp.einsum('bfeh,ehd->bfed', h, Wo) + bo
        return jnp.einsum('bfed,fe->bfd', y, w)

    def _L2_gnn_ref(x, edge_index, W, att_src, att_dst, bias):
        import jax, jax.numpy as jnp
        import numpy as np
        N_NODES = 50000
        N_EDGES = 50000
        H_SIZE = 256
        HEADS = 8
        HEAD_DIM = H_SIZE // HEADS
        NEG_SLOPE = 0.2
        'GATConv (concat heads) -> relu -> dropout(eval=identity).\n\n            x: [N, F]; edge_index: [2, E] with (src=row0, dst=row1) meaning message j->i.\n            '
        N = x.shape[0]
        h = jnp.einsum('nf,fhd->nhd', x, W)
        a_src = jnp.sum(h * att_src, axis=-1)
        a_dst = jnp.sum(h * att_dst, axis=-1)
        src = edge_index[0]
        dst = edge_index[1]
        e = jax.nn.leaky_relu(a_src[src] + a_dst[dst], NEG_SLOPE)
        e_max = jax.ops.segment_max(e, dst, num_segments=N)
        e_exp = jnp.exp(e - e_max[dst])
        denom = jax.ops.segment_sum(e_exp, dst, num_segments=N)
        alpha = e_exp / (denom[dst] + 1e-16)
        msg = h[src] * alpha[:, :, None]
        out = jax.ops.segment_sum(msg, dst, num_segments=N)
        out = out.reshape(N, -1) + bias
        return jax.nn.relu(out)

    def _L2_mix_ref(x, W_qkv, W_out, b_out):
        import jax, jax.numpy as jnp
        import numpy as np
        HEADS = 4
        DIM_HEAD = 32
        B, L, D = x.shape
        scale = DIM_HEAD ** (-0.5)
        qkv = jnp.einsum('bld,df->blf', x, W_qkv)
        qkv = qkv.reshape(B, L, 3, HEADS, DIM_HEAD)
        q = jnp.transpose(qkv[:, :, 0], (0, 2, 1, 3)) * scale
        k = jax.nn.softmax(jnp.transpose(qkv[:, :, 1], (0, 2, 1, 3)), axis=2)
        v = jnp.transpose(qkv[:, :, 2], (0, 2, 1, 3))
        context = jnp.einsum('bhld,bhle->bhde', k, v)
        out = jnp.einsum('bhde,bhld->bhle', context, q)
        out = jnp.transpose(out, (0, 2, 1, 3)).reshape(B, L, HEADS * DIM_HEAD)
        return jnp.einsum('blf,fd->bld', out, W_out) + b_out

    def _L2_ffn_ref(x, weight, bias):
        import jax, jax.numpy as jnp
        import numpy as np
        IN_CH = 256
        OUT_CH = 256
        return jnp.einsum('bsi,oi->bso', x, weight) + bias

    def _L3_gnn_ref(vertex_features, edge_index, w0, w1):
        import jax, jax.numpy as jnp
        import numpy as np
        N_NODES = 50000
        N_EDGES = 25000
        D_IN = 256
        D_OUT = 256
        w0_features = vertex_features @ w0
        w1_features = vertex_features @ w1
        dst, src = (edge_index[0], edge_index[1])
        messages = w1_features[src]
        neighbours = jax.ops.segment_sum(messages, dst, num_segments=vertex_features.shape[0])
        return jax.nn.relu(w0_features + neighbours)

    def _L3_mix_ref(x, W_qkv, b_qkv, W_out, b_out):
        import math
        import jax, jax.numpy as jnp
        import numpy as np
        EPS_DIV = 1e-07
        EPS_NORM = 1e-12

        def _l2_normalize(x, axis):
            n = jnp.sqrt(jnp.sum(x * x, axis=axis, keepdims=True))
            return x / jnp.maximum(n, EPS_NORM)
        b, N, C = x.shape
        qkv = x @ W_qkv + b_qkv
        q, k, v = jnp.split(qkv, 3, axis=2)
        q = q - jnp.mean(q, axis=2, keepdims=True)
        k = k - jnp.mean(k, axis=2, keepdims=True)
        q2 = q * q
        k2 = k * k
        q2s = jnp.sum(q2, axis=2, keepdims=True)
        k2s = jnp.sum(k2, axis=2, keepdims=True)
        k2 = _l2_normalize(k2 / (k2s + EPS_DIV), axis=-2)
        q2 = _l2_normalize(q2 / (q2s + EPS_DIV), axis=-1)
        kv = jnp.einsum('bnc,bnd->bcd', k2, v)
        t2 = jnp.einsum('bnc,bcd->bnd', q2, kv) / math.sqrt(N)
        attn = v + t2
        return attn @ W_out + b_out

    def _L3_ffn_ref(x, Wr, br, ln_g, ln_b, W1, b1, W2, b2):
        import jax, jax.numpy as jnp
        import numpy as np
        TOP_K = 2
        LN_EPS = 1e-05
        B, S, D = x.shape
        N = B * S
        xt = x.reshape(N, D)
        logits = xt @ Wr + br
        probs = jax.nn.softmax(logits, axis=-1)
        top_p, top_idx = jax.lax.top_k(probs, TOP_K)
        weights = top_p / top_p.sum(axis=-1, keepdims=True)
        mu = xt.mean(axis=-1, keepdims=True)
        var = ((xt - mu) ** 2).mean(axis=-1, keepdims=True)
        xn = (xt - mu) * jax.lax.rsqrt(var + LN_EPS)
        xe = xn[None, :, :] * ln_g[:, None, :] + ln_b[:, None, :]
        h = jax.nn.gelu(jnp.einsum('end,edh->enh', xe, W1) + b1[:, None, :], approximate=False)
        y = jnp.einsum('enh,ehd->end', h, W2) + b2[:, None, :]
        y_tok = jnp.transpose(y, (1, 0, 2))
        sel = jnp.take_along_axis(y_tok, top_idx[:, :, None], axis=1)
        out = (weights[:, :, None] * sel).sum(axis=1)
        return out.reshape(B, S, D)
    edge_index = jnp.stack([src, dst])
    xn = _layernorm(x, axis=-1)
    x = x + _L0_gnn_ref(xn, edge_index, L0_gnn_W_l, L0_gnn_W_r, L0_gnn_b_r) + _L0_mix_ref(xn[None], L0_mix_kln_weight, L0_mix_kln_bias, L0_mix_vln_weight, L0_mix_vln_bias)[0]
    x = x + _L0_ffn_ref(_layernorm(x, axis=-1)[None], L0_ffn_gate_w, L0_ffn_gate_b, L0_ffn_W1, L0_ffn_b1, L0_ffn_W2, L0_ffn_b2)[0]
    xn = _layernorm(x, axis=-1)
    x = x + _L1_gnn_ref(xn, src, dst, L1_gnn_W_in, L1_gnn_b_in, L1_gnn_W_out, L1_gnn_b_out) + _L1_mix_ref(xn[None], L1_mix_Wqkv, L1_mix_ln1_g, L1_mix_ln1_b, L1_mix_W1, L1_mix_b1, L1_mix_W2, L1_mix_b2, L1_mix_ln2_g, L1_mix_ln2_b)[0]
    x = x + _L1_ffn_ref(_layernorm(x, axis=-1)[None], L1_ffn_Wr, L1_ffn_br, L1_ffn_W1, L1_ffn_b1, L1_ffn_g1, L1_ffn_be1, L1_ffn_m1, L1_ffn_v1, L1_ffn_W2, L1_ffn_b2, L1_ffn_g2, L1_ffn_be2, L1_ffn_m2, L1_ffn_v2, L1_ffn_Wo, L1_ffn_bo)[0]
    xn = _layernorm(x, axis=-1)
    x = x + _L2_gnn_ref(xn, edge_index, L2_gnn_W, L2_gnn_att_src, L2_gnn_att_dst, L2_gnn_bias) + _L2_mix_ref(xn[None], L2_mix_W_qkv, L2_mix_W_out, L2_mix_b_out)[0]
    x = x + _L2_ffn_ref(_layernorm(x, axis=-1)[None], L2_ffn_weight, L2_ffn_bias)[0]
    xn = _layernorm(x, axis=-1)
    x = x + _L3_gnn_ref(xn, edge_index, L3_gnn_w0, L3_gnn_w1) + _L3_mix_ref(xn[None], L3_mix_W_qkv, L3_mix_b_qkv, L3_mix_W_out, L3_mix_b_out)[0]
    x = x + _L3_ffn_ref(_layernorm(x, axis=-1)[None], L3_ffn_Wr, L3_ffn_br, L3_ffn_ln_g, L3_ffn_ln_b, L3_ffn_W1, L3_ffn_b1, L3_ffn_W2, L3_ffn_b2)[0]
    return x

_drawn_inputs = setup_inputs


def setup_inputs(seed=0):
    import zlib

    import numpy as np

    out = dict(_drawn_inputs(seed))
    spreads = {'L0_gnn_b_r': (0.0, 0.1),
     'L0_mix_kln_weight': (1.0, 0.2),
     'L0_mix_kln_bias': (0.0, 0.455),
     'L0_mix_vln_weight': (1.0, 0.2),
     'L0_mix_vln_bias': (0.0, 0.436),
     'L0_ffn_gate_b': (0.0, 0.767),
     'L0_ffn_b1': (0.0, 0.8),
     'L0_ffn_b2': (0.0, 0.513),
     'L1_mix_ln1_g': (1.0, 0.2),
     'L1_mix_ln1_b': (0.0, 0.1),
     'L1_mix_ln2_g': (1.0, 0.2),
     'L1_mix_ln2_b': (0.0, 0.1),
     'L1_ffn_br': (0.0, 0.8),
     'L1_ffn_b1': (0.0, 0.71),
     'L1_ffn_g1': (1.0, 0.6),
     'L1_ffn_be1': (0.0, 0.767),
     'L1_ffn_m1': (0.0, 0.745),
     'L1_ffn_v1': (1.0, 0.6),
     'L1_ffn_b2': (0.0, 0.442),
     'L1_ffn_g2': (1.0, 0.6),
     'L1_ffn_be2': (0.0, 0.503),
     'L1_ffn_m2': (0.0, 0.451),
     'L1_ffn_v2': (1.0, 0.6),
     'L1_ffn_bo': (0.0, 0.285),
     'L2_gnn_bias': (0.0, 0.312),
     'L2_mix_b_out': (0.0, 0.1),
     'L3_ffn_br': (0.0, 0.467),
     'L3_ffn_ln_g': (1.0, 0.6),
     'L3_ffn_ln_b': (0.0, 0.8),
     'L3_ffn_b1': (0.0, 0.8),
     'L3_ffn_b2': (0.0, 0.558)}
    factors = {'L0_ffn_gate_w': 5.773,
     'L0_ffn_W1': 7.77,
     'L0_ffn_W2': 6.784,
     'L1_gnn_b_in': 2.717,
     'L1_mix_b1': 7.531,
     'L2_gnn_att_src': 3.16,
     'L2_gnn_att_dst': 34.88,
     'L3_mix_b_out': 8.0,
     'L1_gnn_b_out': 3.925,
     'L1_mix_b2': 3.419,
     'L2_ffn_bias': 3.535}
    for name, (base, spread) in spreads.items():
        noise = np.random.default_rng([zlib.crc32(name.encode()), seed]).standard_normal(out[name].shape)
        drawn = base * np.exp(spread * noise) if base else spread * noise
        out[name] = jnp.asarray(drawn.astype(out[name].dtype))
    for name, factor in factors.items():
        out[name] = (out[name] * factor).astype(out[name].dtype)
    return out
```

```python
from contextlib import ExitStack

import numpy as np

import concourse.bass as bass
from concourse import mybir

F32 = mybir.dt.float32
BF16 = mybir.dt.bfloat16
F16 = mybir.dt.float16
I32 = mybir.dt.int32
ALU = mybir.AluOpType
ACT = mybir.ActivationFunctionType
AX = mybir.AxisListType

N = 625
D = 256
P = 125
NT = N // P
KC = D // 128
TP = 628
TH = TP // 2
E = 8
NE = 20000
G, R = 40, 4
H8, HC = 8, 32
LN_EPS = 1e-5
NO_EDGE = -1e30

SMALL = {}
ROWS = {}
COLS = {}


def _place(table, parts):
    at = 0
    for name, n in parts:
        table[name] = (at, at + n)
        at += n
    table["end"] = at


SMALL_L0 = [("l0_wl", KC * D), ("l0_wr", KC * D), ("l0_gate", KC * E)]
SMALL_L1 = [("l1_win", KC * D), ("l1_qkv", KC * 3 * D), ("l1_w1", KC * D), ("l1_w2", KC * D),
            ("l1_wout", KC * D), ("l1_wr", KC * E)]
SMALL_L2 = [("l2_w", KC * D), ("l2_qkv", KC * 384), ("l2_wout", D), ("l2_ffn", KC * D)]
SMALL_L3 = [("l3_w0", KC * D), ("l3_w1", KC * D), ("l3_qkv", KC * 3 * D), ("l3_wout", KC * D), ("l3_wr", KC * E)]
_place(SMALL, SMALL_L0 + SMALL_L1 + SMALL_L2 + SMALL_L3)
_place(ROWS, [("l0_br", D), ("l0_kw", D), ("l0_kb", D), ("l0_vw", D), ("l0_vb", D), ("l0_gb", E),
              ("l1_bin", D), ("l1_bout", D), ("l1_g1", D), ("l1_b1", D), ("l1_b2", D), ("l1_g2", D),
              ("l1_be2", D), ("l1_br", E), ("l2_as", D), ("l2_ad", D), ("l2_bias", D), ("l2_bout", D),
              ("l2_ffnb", D), ("l3_bqk", 2 * D), ("l3_bv", D), ("l3_bout", D), ("l3_br", E)])
_place(COLS, [("l0_b1", E * 4), ("l1_mb1", KC), ("b1", 16), ("g1", 16), ("be1", 16), ("m1", 16), ("v1", 16),
              ("b2", 16), ("g2", 16), ("be2", 16), ("m2", 16), ("v2", 16), ("l3_bv", KC),
              ("l3_g", 16), ("l3_b", 16), ("l3_b1", E * 8)])
FFN0, FFN1, FFN3 = KC * 512 + 4 * D, 6 * D, KC * 1024 + 8 * D


class Count:

    def __init__(self, slots=1):
        self.n, self.more, self.slots = 0, None, slots

    def at(self, d=0):
        return self.n + d if self.more is None else self.more + (self.n + d)

    @property
    def slot(self):
        return self.n % self.slots

    def enter(self, i, per):
        assert per % self.slots == 0
        self.first, self.per, self.more = self.n, per, i * per

    def leave(self, times):
        assert self.n - self.first == self.per, (self.n - self.first, self.per)
        self.n, self.more = self.first + times * self.per, None


def gps_network(nc, x, src, dst, small, rows, cols, eb2, ffn0, ffn1, ffn3, out):
    with ExitStack() as ctx:
        def sb(name, shape, dt=F32):
            return ctx.enter_context(nc.sbuf_tensor(name, shape, dt))

        def sem(name):
            return ctx.enter_context(nc.semaphore(name))

        w_small = sb("w_small", [128, SMALL["end"]])
        w_rows = sb("w_rows", [P, ROWS["end"]])
        w_cols = sb("w_cols", [128, COLS["end"]])
        w_eb2 = sb("w_eb2", [E, 3, D])
        w_ffn = sb("w_ffn", [128, 2, FFN3])

        def W(name, k=KC):
            a, b = SMALL[name]
            return w_small[:, a:b].rearrange("p (c n) -> p c n", c=k)

        def row(name, tiles=NT):
            a, b = ROWS[name]
            return w_rows[:, a:b].unsqueeze(1).to_broadcast([P, tiles, b - a])

        def col(name):
            a, b = COLS[name]
            return w_cols[:, a:b]

        ident = sb("ident", [128, 128])
        headmask = sb("headmask", [128, 128])
        headcols = sb("headcols", [128, 4])
        pick = sb("pick", [E, H8, 128])
        ones = sb("ones", [128, 2])
        order = sb("order", [P, E])
        minus_half, half = sb("minus_half", [128, 16]), sb("half", [128, 16])
        group_no = sb("group_no", [1, 2, G])
        tile_start = sb("tile_start", [1, NT, G])

        ends = sb("ends", [G, 2])
        endsT = sb("endsT", [1, 2, G])
        last = sb("last", [1, NT])
        bounds = sb("bounds", [1, 3, NT])
        bounds_i = sb("bounds_i", [1, 3, NT], I32)
        a_mem = sb("a_mem", [128, NT * N])
        A = a_mem[0:P, :].rearrange("p (m n) -> p m n", n=N)
        at_mem = sb("at_mem", [128, NT * N])
        AT = at_mem[0:P, :].rearrange("p (m n) -> p m n", n=N)
        idx = at_mem[0:G, 0:1000].bitcast(I32).rearrange("g (w k) -> g w k", w=2)
        idxT = at_mem[0:P, 1000:1640].rearrange("p (w g r) -> p w g r", w=2, r=R)
        span = at_mem[0:1, 1640:2040].rearrange("p (m w g) -> p m w g", m=NT, w=2)
        hot_dst = at_mem[0:P, 2040:2296].bitcast(BF16).rearrange("p (r n) -> p r n", r=R)
        iota = at_mem[0:P, 2296:2616].bitcast(F16)
        zeros = at_mem[0:1, 2616:2872].bitcast(BF16)

        def tm(name, n=D):
            return sb(name, [P, NT, n])

        def fm(name):
            return sb(name, [128, KC, TP])

        X, XB, XN, ACC = tm("X"), tm("XB"), tm("XN", D + 1), tm("ACC")
        XT = fm("XT")
        big = sb("big", [128, 2, 4 * NT * D])
        CW = sb("CW", [P, E, NT])
        CWT = sb("CWT", [E, TP])
        stats = sb("stats", [P, NT, 6])
        mv = sb("mv", [P, NT, 2])
        var_e = sb("var_e", [P, NT])
        rstd = sb("rstd", [P, NT])
        inv_deg = sb("inv_deg", [P, NT])
        inv_deg_k = sb("inv_deg_k", [P, 6, NT])
        s1, s2 = sb("s1", [128, 16]), sb("s2", [128, 16])
        o1, o2 = sb("o1", [128, 16]), sb("o2", [128, 16])
        v12 = sb("v12", [128, 2, 16])
        sm = [sb(f"sm{i}", [P, 40]) for i in range(8)]
        kcol = sb("kcol", [128, 8])

        def scratch(i, shape):
            n = int(np.prod(shape[1:]))
            lo = (i % 4) * NT * D
            v = big[0:shape[0], i // 4, lo:lo + n]
            if len(shape) == 3:
                return v.rearrange("p (a b) -> p a b", b=shape[2])
            return v

        psF = ctx.enter_context(nc.psum_tensor("psF", [128, 2, 2, 512], F32))
        psT = ctx.enter_context(nc.psum_tensor("psT", [128, 2, 512], F32))
        psX = ctx.enter_context(nc.psum_tensor("psX", [128, 2, 512], F32))

        def spread(ps, slot):
            return ps[:, slot].rearrange("p a n -> p (a n)")[:, 0:NT * 128].rearrange("p (j n) -> p j n", n=128)

        f_full, f_free = sem("f_full"), sem("f_free")
        t_full, t_free = sem("t_full"), sem("t_free")
        x_full, x_free = sem("x_full"), sem("x_free")
        ld_x, ld_idx, ld_rows, ld_cols = sem("ld_x"), sem("ld_idx"), sem("ld_rows"), sem("ld_cols")
        ld_small = [sem(f"ld_small{i}") for i in range(4)]
        ld_ffn = [sem("ld_ffn_a"), sem("ld_ffn_b")]
        ffn_used = sem("ffn_used")
        stored = sem("stored")
        consts = sem("consts")
        v_step, a_step, g_step = sem("v_step"), sem("a_step"), sem("g_step")
        idx_f = sem("idx_f")
        bounds_ready = sem("bounds_ready")
        hot_ready, hot_used = sem("hot_ready"), sem("hot_used")
        var_ready, rstd_ready = sem("var_ready"), sem("rstd_ready")
        xn_ready = sem("xn_ready")
        x_ready = sem("x_ready")
        xb_ready = sem("xb_ready")
        cw_ready = sem("cw_ready")
        l0_std, l0_std_r, l0_kv = sem("l0_std"), sem("l0_std_r"), sem("l0_kv")
        l0_w = sem("l0_w")
        logit_ready, exp_ready = sem("logit_ready"), sem("exp_ready")
        l1_pre, l1_u = sem("l1_pre"), sem("l1_u")
        l1_kmin, l1_kexp, l1_k, l1_q, l1_qT = (sem(n) for n in ("l1_kmin", "l1_kexp", "l1_k", "l1_q", "l1_qT"))
        l1_bd, l1_x1, l1_x1b = sem("l1_bd"), sem("l1_x1"), sem("l1_x1b")
        l1_term, l1_sum = sem("l1_term"), sem("l1_sum")
        bn_v, bn_r, bn_ready = sem("bn_v"), sem("bn_r"), sem("bn_ready")
        l2_ab, l2_kT, l2_kmax, l2_kexp, l2_g = (sem(n) for n in ("l2_ab", "l2_kT", "l2_kmax", "l2_kexp", "l2_g"))
        g_bias, g_exp, g_e, g_full, g_free = (sem(n) for n in ("g_bias", "g_exp", "g_e", "g_full", "g_free"))
        l3_qk, l3_sq, l3_qn, l3_qq, l3_nr = (sem(n) for n in ("l3_qk", "l3_sq", "l3_qn", "l3_qq", "l3_nr"))
        l3_kk, l3_kn2, l3_knr, l3_y1, l3_gnn, l3_q, l3_gw = (sem(n) for n in ("l3_kk", "l3_kn2", "l3_knr", "l3_y1", "l3_gnn", "l3_q", "l3_gw"))
        xe_ready, xe_used = sem("xe_ready"), sem("xe_used")

        hot_src = ACC[:].rearrange("p t d -> p (t d)").bitcast(BF16).rearrange("p (r n) -> p r n", r=R)
        y0, k0, v0 = scratch(0, [P, NT, D]), scratch(1, [P, NT, D]), scratch(2, [P, NT, D])
        sq0 = scratch(3, [P, NT, D])
        ag, agT = scratch(4, [P, NT, D]), scratch(5, [128, KC, TP])
        wc, kv0 = scratch(6, [128, KC, D]), scratch(4, [128, KC, 128])
        idx_float = scratch(7, [G, 2, R * P])
        u_pre, u = scratch(0, [P, NT, D]), scratch(1, [P, NT, D])
        k_neg, k1, v1m = scratch(2, [P, NT, D]), scratch(3, [P, NT, D]), scratch(4, [P, NT, D])
        q_neg, q_pos = scratch(5, [128, KC, TP]), scratch(6, [128, KC, TP])
        bd = scratch(7, [128, KC, 132])
        mix, x1m, x1T, hT1, x1b = (scratch(2, [P, NT, D]), scratch(3, [P, NT, D]), scratch(4, [128, KC, TP]),
                                   scratch(5, [128, KC, TP]), scratch(6, [P, NT, D]))
        term = [scratch(1, [P, NT, D]), scratch(0, [P, NT, D])]
        total, totalT = ACC, scratch(7, [128, KC, TP])
        a_row = big[0:P, 0, 0:H8 * TP].rearrange("p (h n) -> p h n", n=TP)
        no_edge = big[0:P, 1, 0:NT * N].rearrange("p (m n) -> p m n", n=N)
        he = sb("he", [P, NT, H8, HC + 1])
        zm = [w_ffn[0:P, i, 0:NT * N].rearrange("p (m n) -> p m n", n=N) for i in range(2)]
        e1 = [w_ffn[0:P, i, NT * N + 3:NT * N + 3 + N] for i in range(2)]
        e2 = [big[0:P, 1, (5 + i) * TP:(5 + i) * TP + N] for i in range(2)]
        pT = [XT[0:P, i, 0:N].rearrange("p (j n) -> p j n", n=P) for i in range(2)]
        q2T, k2T, kx2 = big[:, 1, 0:TP], big[:, 1, TP:2 * TP], big[:, 1, 2 * TP:3 * TP]
        k2m, v2m = big[0:P, 1, 3 * TP:3 * TP + 640], big[0:P, 1, 4 * TP + 12:4 * TP + 652]
        ctT, gw2 = big[:, 1, 5 * TP + 24:5 * TP + 152], big[:, 1, 5 * TP + 152:5 * TP + 408]
        hm = scratch(3, [P, NT, D])
        hsum = sb("hsum", [P, 2, NT, H8])
        asT = CWT
        mx = sb("mx", [P, NT])
        a_now = sb("a_now", [P, N])
        gm, gb1, gb2, z2 = (sb(n, [P, H8, NT]) for n in ("gm", "gb1", "gb2", "z2"))
        ad_h = hsum[:, 1].rearrange("p t h -> p h t")
        den = sb("den", [P, NT])
        qk = big[0:P, 0, 0:NT * 2 * D].rearrange("p (t n) -> p t n", n=2 * D)
        qk2 = big[0:P, 1, 0:NT * 2 * D].rearrange("p (t n) -> p t n", n=2 * D)
        gnn3 = XN[:, :, 0:D]
        y3, v3, vT3, kk3 = scratch(2, [P, NT, D]), scratch(3, [P, NT, D]), scratch(6, [128, KC, TP]), ACC
        qT3, kvT, gw3 = scratch(0, [128, KC, TP]), scratch(7, [128, KC, D]), scratch(7, [128, 2 * KC, D])[:, KC:2 * KC, :]
        hidden = [big[:, u_, 0:8 * TP].rearrange("p (k n) -> p k n", n=TP) for u_ in range(2)]
        xe = [a_mem[:, b * KC * TP:(b + 1) * KC * TP].rearrange("p (c n) -> p c n", n=TP) for b in range(2)]

        F_K2 = 2 * NT + E * 4 + 2 * KC + E * 2 * KC + 2

        block = ctx.enter_context(nc.Block())

        @block.sync
        def _(sp):
            sp.dma_start(X[:], x.rearrange("(t p) d -> p t d", p=P)).then_inc(ld_x, 16)
            sp.dma_start(idx[:, 1, :], dst.rearrange("(g k) -> g k", g=G)).then_inc(ld_idx, 16)
            sp.dma_start(idx[:, 0, :], src.rearrange("(g k) -> g k", g=G)).then_inc(ld_idx, 16)
            sp.dma_start(w_rows[:], rows.partition_broadcast(P)).then_inc(ld_rows, 16)
            edge = [0, SMALL["l1_win"][0], SMALL["l2_w"][0], SMALL["l3_w0"][0], SMALL["end"]]
            sp.dma_start(w_small[:, edge[0]:edge[1]], small[:, edge[0]:edge[1]]).then_inc(ld_small[0], 16)
            sp.dma_start(w_cols[:], cols).then_inc(ld_cols, 16)
            sp.dma_start(w_eb2[:], eb2).then_inc(ld_cols, 16)
            for n in range(1, 4):
                sp.dma_start(w_small[:, edge[n]:edge[n + 1]], small[:, edge[n]:edge[n + 1]]).then_inc(ld_small[n], 16)

            done = 0
            for weights, n in ((ffn0, FFN0), (ffn1, FFN1), (ffn3, FFN3)):
                if n == FFN3:
                    sp.wait_ge(x_ready, 6)
                with sp.Fori(0, E // 2) as i:
                    for b in range(2):
                        sp.wait_ge(ffn_used, i * 2 + (done + b + 1))
                        sp.dma_start(w_ffn[:, b, 0:n], weights[bass.ds(i * 2 + b, 1), :, :].rearrange("o p n -> (o p) n"))\
                          .then_inc(ld_ffn[b], 16)
                done += E
            sp.wait_ge(x_ready, 8)
            sp.dma_start(out.rearrange("(t p) d -> p t d", p=P), X[:]).then_inc(stored, 16)
            sp.wait_ge(stored, 16)

        @block.gpsimd
        def _(pool):
            steps = Count()

            def link(ins):
                ins.then_inc(g_step, 1)
                steps.n += 1
                pool.wait_ge(g_step, steps.n)

            for tensor, value in ((ident, 0.0), (pick, 0.0), (headmask, 0.0), (headcols, 0.0), (ones, 1.0),
                                  (minus_half, -0.5), (half, 0.5)):
                link(pool.memset(tensor[:], value))
            link(pool.memset(zeros, 0.0))
            link(pool.memset(XN[:, :, D:D + 1], 1.0))
            link(pool.memset(he[:, :, :, HC:HC + 1], 1.0))
            link(pool.memset(XT[:, :, N:TP], 0.0))
            link(pool.memset(asT[:, N:TP], 0.0))
            link(pool.iota(iota, pattern=[[1, 640]], base=0, channel_multiplier=0, allow_small_or_imprecise_dtypes=True))
            link(pool.iota(order[:], pattern=[[-1, E]], base=E, channel_multiplier=0, allow_small_or_imprecise_dtypes=True))
            link(pool.iota(tile_start[:], pattern=[[P, NT], [0, G]], base=0, channel_multiplier=0, allow_small_or_imprecise_dtypes=True))
            link(pool.iota(group_no[:, 0, :], pattern=[[-1, G]], base=G, channel_multiplier=0, allow_small_or_imprecise_dtypes=True))
            link(pool.iota(group_no[:, 1, :], pattern=[[1, G]], base=1, channel_multiplier=0, allow_small_or_imprecise_dtypes=True))
            link(pool.affine_select(out=ident[:], in_=ident[:], compare_op=ALU.not_equal, fill=1.0, base=0,
                                    pattern=[[-1, 128]], channel_multiplier=1))
            link(pool.affine_select(out=pick[:], in_=pick[:], compare_op=ALU.not_equal, fill=1.0, base=0,
                                    pattern=[[-1, H8], [0, 128]], channel_multiplier=1))
            for h in range(4):
                link(pool.memset(headmask[HC * h:HC * h + HC, HC * h:HC * h + HC], 1.0))
                ins = pool.memset(headcols[HC * h:HC * h + HC, h:h + 1], 1.0)
                link(ins) if h < 3 else ins.then_inc(consts, 1)

            ln = Count()

            def rsqrt():
                ln.n += 1
                pool.wait_ge(var_ready, ln.n)
                pool.tensor_tensor(rstd[:], var_e[:], minus_half[0:P, 0:NT], ALU.pow).then_inc(rstd_ready, 1)

            def residual(name):
                pool.tensor_tensor(XB[:], X[:], row(name), ALU.add).then_inc(xb_ready, 1)

            rsqrt()
            pool.wait_ge(ld_rows, 16)
            residual("l0_br")
            rsqrt()
            pool.wait_ge(bn_v, 1)
            pool.tensor_tensor(v12[:, 0, :], v12[:, 0, :], minus_half[:], ALU.pow)
            pool.tensor_tensor(v12[:, 1, :], v12[:, 1, :], minus_half[:], ALU.pow).then_inc(bn_r, 1)
            rsqrt()
            pool.wait_ge(x_ready, 2)
            residual("l1_bout")
            rsqrt()
            pool.wait_ge(l1_x1, 1)
            pool.tensor_tensor(x1b[:], x1m[:], row("l1_b2"), ALU.add).then_inc(l1_x1b, 1)
            rsqrt()
            pool.wait_ge(l1_u, 1)
            pool.tensor_copy(total[:], u[:]).then_inc(l1_sum, 2)
            with pool.Fori(0, 3) as i:
                for b in range(2):
                    pool.wait_ge(l1_term, i * 2 + (b + 1))
                    pool.wait_ge(l1_sum, i * 2 + (b + 2))
                    pool.tensor_tensor(total[:], total[:], term[1 - b][:], ALU.add).then_inc(l1_sum, 1)
            rsqrt()
            rsqrt()
            pool.wait_ge(x_ready, 4)
            residual("l2_bout")
            rsqrt()
            pool.wait_ge(x_ready, 5)
            residual("l2_ffnb")
            rsqrt()
            pool.wait_ge(x_ready, 6)
            residual("l3_bout")
            for s_in, s_out, a in ((l3_qq, l3_nr, sm[4][:, 0:NT]), (l3_kn2, l3_knr, kcol[:, 0:KC])):
                pool.wait_ge(s_in, 1)
                pool.tensor_tensor(a, a, half[0:a.shape[0], 0:a.shape[1]], ALU.pow).then_inc(s_out, 1)
            pool.wait_ge(l3_gnn, 1)
            pool.tensor_tensor(XB[:], XB[:], gnn3, ALU.add).then_inc(xb_ready, 1)
            rsqrt()
            rsqrt()

        @block.scalar
        def _(act):
            f = Count(2)
            a = Count()

            def link(ins):
                ins.then_inc(a_step, 1)
                a.n += 1
                act.wait_ge(a_step, a.at())

            def full(halves=TH):
                act.wait_ge(f_full, f.at(1))
                return psF[:, f.slot, :, 0:halves]

            def free(ins):
                ins.then_inc(f_free, 1)
                f.n += 1

            def halves(v):
                return v.rearrange("p (a n) -> p a n", a=2)

            act.wait_ge(consts, 1)
            for m in range(NT):
                full()
                act.activation(A[:, m, 0:512], psF[0:P, f.slot, 0, :], ACT.Copy)
                free(act.activation(A[:, m, 512:N], psF[0:P, f.slot, 1, 0:N - 512], ACT.Copy))

            for m in range(NT):
                full()
                free(act.activation(AT[:, :, m * P:m * P + P], spread(psF, f.slot)[0:P, :, 0:P], ACT.Copy))

            act.wait_ge(l0_std, 1)
            act.activation(sm[1][:], sm[1][:], ACT.Sqrt, scale=1.0 / (HC - 1)).then_inc(l0_std_r, 1)

            def soft(n):
                act.wait_ge(logit_ready, n)
                act.activation(sm[1][:], sm[1][:], ACT.Exp).then_inc(exp_ready, 1)

            soft(1)
            act.wait_ge(ld_cols, 32)
            with act.Fori(0, E // 2) as i:
                f.enter(i, 8)
                for b in range(2):
                    for k in range(4):
                        ps = full()
                        bias = col("l0_b1")[:, bass.ds((i * 2 + b) * 4 + k, 1)]
                        free(act.activation(halves(hidden[b][:, k, :]), ps, ACT.Gelu, bias=bias))
                f.leave(E // 2)
            act.wait_ge(l1_pre, 1)
            act.activation(u[:], u_pre[:], ACT.Silu).then_inc(l1_u, 1)
            for c in range(KC):
                ps = full()
                act.activation(halves(q_pos[:, c, :]), ps, ACT.Relu)
                free(act.activation(halves(q_neg[:, c, :]), ps, ACT.Relu, scale=-1.0))
            act.wait_ge(f_free, f.n)
            act.activation(q_neg[:], q_neg[:], ACT.Exp, scale=-1.0).then_inc(l1_q, 1)
            act.wait_ge(l1_kmin, NT)
            act.activation(k_neg[:], k_neg[:], ACT.Exp).then_inc(l1_kexp, 1)
            for c in range(KC):
                ps = full()
                free(act.activation(halves(hT1[:, c, :]), ps, ACT.Gelu, bias=col("l1_mb1")[:, c:c + 1]))
            soft(2)
            act.wait_ge(bn_ready, 1)
            with act.Fori(0, E // 2) as i:
                f.enter(i, 8)
                for layer, s, o in ((0, s1, o1), (1, s2, o2)):
                    for b in range(2):
                        for c in range(KC):
                            ps = full()
                            at = bass.ds((i * 2 + b) * KC + c, 1)
                            free(act.activation(halves(hidden[b][:, layer * KC + c, :]), ps, ACT.Relu,
                                                bias=o[:, at], scale=s[:, at]))
                f.leave(E // 2)
            free(act.activation(halves(q2T), full(), ACT.Copy))
            free(act.activation(halves(k2T), full(), ACT.Copy))
            act.wait_ge(l2_kmax, 1)
            act.activation(kx2[:, 0:N], k2T[:, 0:N], ACT.Exp, bias=kcol[:, 0:1], accum_out=kcol[:, 1:2]).then_inc(l2_kexp, 1)
            for h in range(H8):
                ps = full()
                free(act.activation(halves(a_row[:, h, :]), ps[0:P], ACT.Copy))
            units = Count(2)
            with act.Fori(0, H8 // 2) as i:
                units.enter(i, 2 * NT)
                for b in range(2):
                    act.wait_ge(g_bias, i * 2 + (b + 1))
                    for m in range(NT):
                        s = units.slot
                        at = bass.ds(i * 2 + b, 1)
                        act.wait_ge(g_full, units.at(1))
                        act.activation(e1[s], zm[b][:, m, :], ACT.Exp, bias=gb1[:, at, m])
                        act.activation(e2[s], zm[b][:, m, :], ACT.Exp, bias=gb2[:, at, m], scale=0.2).then_inc(g_exp, 1)
                        units.n += 1
                units.leave(H8 // 2)
            act.wait_ge(l3_qk, 1)
            for t in range(NT):
                for w in range(2):
                    ins = act.activation(qk2[:, t, w * D:w * D + D], qk[:, t, w * D:w * D + D], ACT.Square,
                                         bias=sm[0][:, 2 * t + w:2 * t + w + 1],
                                         accum_out=sm[1][:, 2 * t + w:2 * t + w + 1])
            ins.then_inc(l3_sq, 1)
            for c in range(KC):
                ps = full()
                free(act.activation(halves(vT3[:, c, :]), ps, ACT.Identity, bias=col("l3_bv")[:, c:c + 1]))
            act.wait_ge(l3_qn, 1)
            for t in range(NT):
                ins = act.activation(qk[:, t, 0:D], qk2[:, t, 0:D], ACT.Square, accum_out=sm[4][:, t:t + 1])
            ins.then_inc(l3_qq, 1)
            act.activation(kk3[:], qk2[:, :, D:2 * D], ACT.Square).then_inc(l3_kk, 1)
            soft(3)
            with act.Fori(0, E // 2) as i:
                f.enter(i, 16)
                for b in range(2):
                    for k in range(8):
                        ps = full()
                        bias = col("l3_b1")[:, bass.ds((i * 2 + b) * 8 + k, 1)]
                        free(act.activation(halves(hidden[b][:, k, :]), ps, ACT.Gelu, bias=bias))
                f.leave(E // 2)

        @block.tensor
        def _(pe):
            f, t, xr = Count(2), Count(2), Count(2)

            def f_slot():
                if f.more is not None or f.n >= 2:
                    pe.wait_ge(f_free, f.at(-1))
                return psF[:, f.slot]

            def f_done(ins):
                ins.then_inc(f_full, 1)
                f.n += 1

            def t_slot():
                if t.more is not None or t.n >= 2:
                    pe.wait_ge(t_free, t.at(-1))
                return psT[:, t.slot]

            def t_done(ins):
                ins.then_inc(t_full, 1)
                t.n += 1

            def x_slot():
                if xr.n >= 2:
                    pe.wait_ge(x_free, xr.n - 1)
                return psX[:, xr.slot]

            def x_done(ins):
                ins.then_inc(x_full, 1)
                xr.n += 1

            def turn(a):
                for c in range(KC):
                    ps = x_slot()
                    for i in range(4):
                        ins = pe.transpose(ps[:, i * P:i * P + P], a[:, i, c * 128:c * 128 + 128], ident[0:P, 0:P])
                    x_done(ins)
                ps = x_slot()
                for c in range(KC):
                    ins = pe.transpose(ps[:, c * P:c * P + P], a[:, 4, c * 128:c * 128 + 128], ident[0:P, 0:P])
                x_done(ins)

            def turned():
                pe.wait_ge(x_free, xr.n)

            def rows_of(terms, n, at=0):
                for i in range(NT):
                    ps = t_slot()
                    pairs = terms(i)
                    for k, (lhsT, rhs) in enumerate(pairs):
                        ins = pe.matmul(ps[0:P, at:at + n], lhsT, rhs, start=k == 0, stop=k == len(pairs) - 1)
                    t_done(ins)

            def linear(actT, w, a=0, b=D, chunks=KC):
                return lambda i: [(actT[:, c, i * P:i * P + P], w[:, c, a:b]) for c in range(chunks)]

            def chunk_fm(ps, weight, actT, chunks):
                for c in range(chunks):
                    for h in range(2):
                        ins = pe.matmul(ps[:, h, 0:TH], weight(c), actT[:, c, h * TH:h * TH + TH],
                                        start=c == 0, stop=c == chunks - 1)
                return ins

            def router(n, w):
                ps = t_slot()
                for i in range(NT):
                    for c in range(KC):
                        ins = pe.matmul(ps[0:P, i * E:i * E + E], XT[:, c, i * P:i * P + P], w[:, c, :],
                                        start=c == 0, stop=c == KC - 1)
                t_done(ins)
                pe.wait_ge(cw_ready, n + 1)
                for tiles in ((0, 1, 2, 3), (4,)):
                    ps = x_slot()
                    for i in tiles:
                        ins = pe.transpose(ps[0:E, (i % 4) * P:(i % 4) * P + P], CW[:, :, i], ident[0:P, 0:P])
                    x_done(ins)
                turned()
                rows_of(lambda i: [(CWT[:, i * P:i * P + P], w_eb2[:, n, :])], D)

            pe.wait_ge(consts, 1)
            pe.wait_ge(idx_f, 1)
            ps = x_slot()
            for w in range(2):
                for r in range(R):
                    pe.transpose(ps[0:P, (w * R + r) * G:(w * R + r) * G + G], idx_float[:, w, r * P:r * P + P], ident[0:G, 0:G])
            for w in range(2):
                ins = pe.transpose(ps[0:1, (2 * R + w) * G:(2 * R + w) * G + G], ends[:, w:w + 1], ident[0:G, 0:G])
            x_done(ins)
            pe.wait_ge(xn_ready, 1)
            turn(XN)
            pe.wait_ge(bounds_ready, 1)
            count = [pe.value_load(bounds_i[0:1, 1, m:m + 1], min_val=1, max_val=G) for m in range(NT)]
            before = [pe.value_load(bounds_i[0:1, 2, m:m + 1], min_val=0, max_val=G * NT) for m in range(NT)]
            for m in range(NT):
                ps = f_slot()
                for part, lo, hi in ((0, 0, 512), (1, 512, N)):
                    ins = pe.matmul(ps[0:P, part, 0:hi - lo], zeros[:, 0:P], zeros[:, 0:hi - lo],
                                    start=True, stop=False, skip_group_check=True)
                if m == 0:
                    ins.then_inc(hot_used, 2)
                with pe.Fori(0, count[m]) as j:
                    for r in range(R):
                        if r % 2 == 0:
                            pe.wait_ge(hot_ready, (before[m] + j) * 2 + (r // 2 + 1))
                        pe.matmul(ps[0:P, 0, :], hot_dst[:, r, 0:P], hot_src[:, r, 0:512],
                                  start=False, stop=False, skip_group_check=True)
                        ins = pe.matmul(ps[0:P, 1, 0:N - 512], hot_dst[:, r, 0:P], hot_src[:, r, 512:N],
                                        start=False, stop=False, skip_group_check=True)
                        if r % 2:
                            ins.then_inc(hot_used, 1)
                for part, lo, hi in ((0, 0, 512), (1, 512, N)):
                    ins = pe.matmul(ps[0:P, part, 0:hi - lo], zeros[:, 0:P], zeros[:, 0:hi - lo],
                                    start=False, stop=True, skip_group_check=True)
                f_done(ins)
            for m in range(NT):
                pe.wait_ge(f_free, m + 1)
                f_slot()
                ps = spread(psF, f.slot)
                for j in range(NT):
                    ins = pe.transpose(ps[0:P, j, 0:P], A[:, m, j * P:j * P + P], ident[0:P, 0:P])
                f_done(ins)
            pe.wait_ge(f_free, f.n)
            rows_of(lambda m: [(AT[:, j, m * P:m * P + P], XN[:, j, :]) for j in range(NT)], D + 1)
            pe.wait_ge(t_free, t.n)
            turn(ag)
            pe.wait_ge(l0_kv, 1)
            ps = t_slot()
            for c in range(KC):
                for i in range(NT):
                    ins = pe.matmul(ps[:, c * 128:c * 128 + 128], k0[:, i, c * 128:c * 128 + 128],
                                    v0[:, i, c * 128:c * 128 + 128], start=i == 0, stop=i == NT - 1)
            t_done(ins)
            turned()
            pe.wait_ge(ld_small[0], 16)
            pe.wait_ge(l0_w, 1)
            rows_of(lambda i: linear(agT, W("l0_wl"))(i) + linear(XT, wc)(i), D)

            def experts_two_layers(weights_n, hid, chunks, act_in, wait=None):
                with pe.Fori(0, E // 2) as i:
                    f.enter(i, 2 * chunks)
                    t.enter(i, 2 * NT)
                    for b in range(2):
                        w1 = w_ffn[:, b, 0:KC * hid].rearrange("p (c n) -> p c n", c=KC)
                        w2 = w_ffn[:, b, KC * hid:KC * hid + chunks * D].rearrange("p (k n) -> p k n", n=D)
                        pe.wait_ge(ld_ffn[b], i * 16 + (weights_n + 16))
                        if wait is not None:
                            pe.wait_ge(wait, i * 2 + (b + 1))
                        for k in range(chunks):
                            ins = chunk_fm(f_slot(), lambda c: w1[:, c, k * 128:k * 128 + 128], act_in(b), KC)
                            f_done(ins)
                        for m in range(NT):
                            ps = t_slot()
                            for k in range(chunks):
                                if m == 0:
                                    pe.wait_ge(f_free, f.at(k + 1 - chunks))
                                ins = pe.matmul(ps[0:P, 0:D], hidden[b][:, k, m * P:m * P + P], w2[:, k, :],
                                                start=k == 0, stop=k == chunks - 1)
                            t_done(ins)
                        pe.wait_ge(t_full, t.at())
                        pe.nop().then_inc(ffn_used, 1)
                    f.leave(E // 2)
                    t.leave(E // 2)

            pe.nop().then_inc(ffn_used, 2)
            pe.wait_ge(xn_ready, 2)
            turn(XN)
            turned()
            pe.wait_ge(ld_cols, 32)
            router(0, W("l0_gate"))
            experts_two_layers(0, 512, 4, lambda b: XT)
            pe.wait_ge(ld_small[1], 16)
            pe.wait_ge(xn_ready, 3)
            turn(XN)
            turned()
            rows_of(linear(XT, W("l1_win")), D)
            for c in range(KC):
                f_done(chunk_fm(f_slot(), lambda k: W("l1_qkv")[:, k, c * 128:c * 128 + 128], XT, KC))
            rows_of(linear(XT, W("l1_qkv"), D, 3 * D), 2 * D)
            pe.wait_ge(l1_k, 1)
            ps = t_slot()
            for c in range(KC):
                for rhs, at, n in ((v1m, c * 128, 128), (None, D + c, 1)):
                    for i in range(NT):
                        ins = pe.matmul(ps[:, at:at + n], k1[:, i, c * 128:c * 128 + 128],
                                        ones[0:P, 0:1] if rhs is None else rhs[:, i, c * 128:c * 128 + 128],
                                        start=i == 0, stop=i == NT - 1)
            t_done(ins)
            pe.wait_ge(l1_qT, 1)
            pe.wait_ge(l1_bd, 1)
            for i in range(NT):
                ps = t_slot()
                for c in range(KC):
                    ins = pe.matmul(ps[0:P, c * 132:c * 132 + 132], q_pos[:, c, i * P:i * P + P], bd[:, c, :],
                                    start=True, stop=True)
                t_done(ins)
            pe.wait_ge(l1_x1, 1)
            turn(x1m)
            turned()
            for c in range(KC):
                f_done(chunk_fm(f_slot(), lambda k: W("l1_w1")[:, k, c * 128:c * 128 + 128], x1T, KC))
            pe.wait_ge(f_free, f.n)
            rows_of(linear(hT1, W("l1_w2")), D)
            pe.wait_ge(l1_u, 1)
            with pe.Fori(0, 3) as i:
                t.enter(i, 2 * NT)
                for b in range(2):
                    pe.wait_ge(t_free, t.at())
                    rows_of(lambda m: [(AT[:, j, m * P:m * P + P], term[b][:, j, :]) for j in range(NT)], D)
                t.leave(3)
            pe.wait_ge(l1_sum, 8)
            turn(total)
            turned()
            rows_of(linear(totalT, W("l1_wout")), D)
            pe.wait_ge(xn_ready, 4)
            turn(XN)
            turned()
            router(1, W("l1_wr"))
            with pe.Fori(0, E // 2) as i:
                f.enter(i, 8)
                t.enter(i, 2 * NT)
                w = [w_ffn[:, b, 0:FFN1].rearrange("p (l c n) -> p l c n", l=3, c=KC) for b in range(2)]
                for layer in range(2):
                    for b in range(2):
                        if layer == 0:
                            pe.wait_ge(ld_ffn[b], i * 16 + (E // 2 * 16 + 16))
                        else:
                            pe.wait_ge(f_free, f.at(-2))
                        src_fm = XT if layer == 0 else hidden[b][:, 0:KC, :]
                        for c in range(KC):
                            f_done(chunk_fm(f_slot(), lambda k: w[b][:, layer, k, c * 128:c * 128 + 128], src_fm, KC))
                for b in range(2):
                    pe.wait_ge(f_free, f.at(-2 + 2 * b))
                    rows_of(linear(hidden[b][:, KC:2 * KC, :], w[b][:, 2]), D)
                    pe.wait_ge(t_full, t.at())
                    pe.nop().then_inc(ffn_used, 1)
                f.leave(E // 2)
                t.leave(E // 2)
            pe.wait_ge(ld_small[2], 16)
            pe.wait_ge(xn_ready, 5)
            turn(XN)
            turned()
            rows_of(linear(XT, W("l2_w")), D)
            for w in range(2):
                f_done(chunk_fm(f_slot(), lambda k: W("l2_qkv")[:, k, w * 128:w * 128 + 128], XT, KC))
            for tiles in ((0, 1, 2, 3), (4,)):
                ps = t_slot()
                for i in tiles:
                    for c in range(KC):
                        ins = pe.matmul(ps[0:P, (i % 4) * 128:(i % 4) * 128 + 128], XT[:, c, i * P:i * P + P],
                                        W("l2_qkv")[:, c, 256:384], start=c == 0, stop=c == KC - 1)
                t_done(ins)
            pe.wait_ge(l2_ab, 1)
            for tiles in ((0, 1, 2, 3), (4,)):
                ps = x_slot()
                for i in tiles:
                    ins = pe.transpose(ps[0:H8, (i % 4) * P:(i % 4) * P + P], hsum[:, 0, i, :], ident[0:P, 0:P])
                x_done(ins)
            turned()
            for h in range(H8):
                ps = f_slot()
                for half_ in range(2):
                    ins = pe.matmul(ps[0:P, half_, 0:TH], pick[:, h, 0:P], asT[:, half_ * TH:half_ * TH + TH],
                                    start=True, stop=True)
                f_done(ins)
            pe.wait_ge(l2_kexp, 1)
            for tiles in ((0, 1, 2, 3), (4,)):
                ps = x_slot()
                for i in tiles:
                    ins = pe.transpose(ps[0:P, (i % 4) * 128:(i % 4) * 128 + 128], kx2[:, i * P:i * P + P], ident[:])
                x_done(ins)
            turned()
            ps = t_slot()
            for i in range(NT):
                ins = pe.matmul(ps[:, 0:128], v2m[:, i * 128:i * 128 + 128], k2m[:, i * 128:i * 128 + 128],
                                start=i == 0, stop=i == NT - 1)
            t_done(ins)
            pe.wait_ge(t_free, t.n)
            ps = t_slot()
            t_done(pe.matmul(ps[:, 0:D], ctT, W("l2_wout", 1)[:, 0, :], start=True, stop=True))
            pe.wait_ge(t_free, t.n)
            rows_of(lambda i: [(q2T[:, i * P:i * P + P], gw2)], D)
            pe.wait_ge(f_free, f.n)
            pe.nop().then_inc(g_full, 2)
            units = Count(2)

            def attend(b, m, ps):
                pe.wait_ge(g_free, units.at())
                s = (units.n - 1) % 2
                for j in range(NT):
                    ins = pe.matmul(ps[0:P, m * (HC + 1):(m + 1) * (HC + 1)], pT[s][:, j, :],
                                    he[:, j, bass.ds(gi * 2 + b, 1), :], start=j == 0, stop=j == NT - 1)
                return ins

            with pe.Fori(0, H8 // 2) as gi:
                units.enter(gi, 2 * NT)
                t.enter(gi, 2)
                ps_t = None
                for n in range(2 * NT):
                    b, m = n // NT, n % NT
                    s = units.slot
                    if m == 0:
                        if b:
                            t_done(attend(b - 1, NT - 1, ps_t))
                        ps_t = t_slot()
                    pe.wait_ge(g_e, units.at(1))
                    for j in range(NT):
                        ins = pe.transpose(spread(psF, s)[0:P, j, 0:P], e1[s][:, j * P:j * P + P], ident[0:P, 0:P])
                    ins.then_inc(g_full, 1)
                    if m:
                        attend(b, m - 1, ps_t)
                    units.n += 1
                t_done(attend(1, NT - 1, ps_t))
                units.leave(H8 // 2)
                t.leave(H8 // 2)
            pe.wait_ge(xn_ready, 6)
            turn(XN)
            turned()
            rows_of(linear(XT, W("l2_ffn")), D)
            pe.wait_ge(ld_small[3], 16)
            pe.wait_ge(xn_ready, 7)
            turn(XN)
            turned()
            rows_of(linear(XT, W("l3_qkv"), 0, 2 * D), 2 * D)
            rows_of(linear(XT, W("l3_w1")), D)
            rows_of(linear(XT, W("l3_qkv"), 2 * D, 3 * D), D)
            for c in range(KC):
                f_done(chunk_fm(f_slot(), lambda k: W("l3_qkv")[:, k, 2 * D + c * 128:2 * D + c * 128 + 128], XT, KC))
            pe.wait_ge(l3_y1, 1)
            rows_of(lambda m: [(A[:, j, m * P:m * P + P], y3[:, j, :]) for j in range(NT)] + linear(XT, W("l3_w0"))(m), D)
            pe.wait_ge(l3_kk, 1)
            ps = t_slot()
            for c in range(KC):
                for i in range(NT):
                    ins = pe.matmul(ps[:, c:c + 1], kk3[:, i, c * 128:c * 128 + 128], ones[0:P, 0:1],
                                    start=i == 0, stop=i == NT - 1)
            t_done(ins)
            ps = t_slot()
            for c in range(KC):
                for i in range(NT):
                    ins = pe.matmul(ps[:, c * D:c * D + D], v3[:, i, c * 128:c * 128 + 128], qk2[:, i, D:2 * D],
                                    start=i == 0, stop=i == NT - 1)
            t_done(ins)
            pe.wait_ge(t_free, t.n)
            ps = t_slot()
            for c in range(KC):
                for k in range(KC):
                    ins = pe.matmul(ps[:, c * D:c * D + D], kvT[:, k, c * 128:c * 128 + 128], W("l3_wout")[:, k, :],
                                    start=k == 0, stop=k == KC - 1)
            t_done(ins)
            pe.wait_ge(l3_q, 1)
            turn(qk2[:, :, 0:D])
            turned()
            pe.wait_ge(l3_gw, 1)
            pe.wait_ge(f_free, f.n)
            rows_of(lambda i: linear(vT3, W("l3_wout"))(i) + linear(qT3, gw3)(i), D)
            pe.wait_ge(xn_ready, 8)
            turn(XN)
            turned()
            router(2, W("l3_wr"))
            pe.wait_ge(xn_ready, 9)
            turn(XN)
            turned()
            experts_two_layers(2 * (E // 2) * 16, 1024, 8, lambda b: xe[b], xe_ready)

        @block.vector
        def _(dve):
            t, xr, v, tf = Count(2), Count(2), Count(), Count()

            def V(ins):
                ins.then_inc(v_step, 1)
                v.n += 1
                return ins

            def settle():
                dve.wait_ge(v_step, v.at())

            def link(ins):
                V(ins)
                settle()

            def announce(what):
                settle()
                if t.n:
                    dve.wait_ge(t_free, t.n)
                dve.nop().then_inc(what, 1)

            def t_full_slot():
                dve.wait_ge(t_full, t.at(1))
                return psT[:, t.slot]

            def t_emptied(ins):
                ins.then_inc(t_free, 1)
                t.n += 1

            def t_settle():
                dve.wait_ge(t_free, t.n)

            def x_full_slot():
                dve.wait_ge(x_full, xr.n + 1)
                return psX[:, xr.slot]

            def x_emptied(ins):
                ins.then_inc(x_free, 1)
                xr.n += 1

            def turned_to(dst_fm):
                for c in range(KC):
                    ps = x_full_slot()
                    x_emptied(dve.tensor_copy(dst_fm[:, c, 0:4 * P], ps[:, 0:4 * P]))
                ps = x_full_slot()
                x_emptied(dve.tensor_copy(dst_fm[:, :, 4 * P:N], ps[:, 0:KC * P].rearrange("p (c n) -> p c n", c=KC)))

            norms = Count()

            def layer_norm(a, b, what=xn_ready):
                for i in range(NT):
                    V(dve.bn_stats(stats[:, i, :], a[:, i, 0:D]))
                settle()
                for i in range(NT):
                    V(dve.bn_aggr(mv[:, i, :], stats[:, i, :]))
                settle()
                dve.tensor_scalar(var_e[:], mv[:, :, 1], LN_EPS, None, ALU.add).then_inc(var_ready, 1)
                norms.n += 1
                dve.wait_ge(rstd_ready, norms.n)
                for i in range(NT):
                    ins = dve.tensor_scalar(b[:, i, 0:D], a[:, i, 0:D], mv[:, i, 0:1], rstd[:, i:i + 1],
                                            ALU.subtract, ALU.mult)
                    if what is None:
                        V(ins)
                    elif i == NT - 1:
                        ins.then_inc(what, 1)
                if what is None:
                    settle()

            def per_node(a):
                return a.unsqueeze(2).to_broadcast([P, NT, E])

            def router(n, bias, top2=False, shares=False):
                view = [s[:].rearrange("p (t e) -> p t e", e=E) for s in sm]
                ps = t_full_slot()
                t_emptied(dve.tensor_tensor(view[0], ps[0:P, 0:NT * E].rearrange("p (t e) -> p t e", e=E), row(bias), ALU.add))
                t_settle()
                link(dve.tensor_reduce(sm[2][:, 0:NT], view[0], AX.X, ALU.max))
                dve.tensor_tensor(view[1], view[0], per_node(sm[2][:, 0:NT]), ALU.subtract).then_inc(logit_ready, 1)
                dve.wait_ge(exp_ready, n)
                link(dve.tensor_reduce(sm[2][:, 0:NT], view[1], AX.X, ALU.add))
                link(dve.reciprocal(sm[2][:, 0:NT], sm[2][:, 0:NT]))
                link(dve.tensor_tensor(view[0], view[1], per_node(sm[2][:, 0:NT]), ALU.mult))
                if top2:
                    order3 = order[:].unsqueeze(1).to_broadcast([P, NT, E])
                    rest = view[0]
                    for first in (True, False):
                        pick_ = view[3 if first else 4]
                        link(dve.tensor_reduce(sm[2][:, 0:NT], rest, AX.X, ALU.max))
                        link(dve.tensor_tensor(view[5], rest, per_node(sm[2][:, 0:NT]), ALU.is_equal))
                        link(dve.tensor_tensor(view[5], view[5], order3, ALU.mult))
                        link(dve.tensor_reduce(sm[2][:, 0:NT], view[5], AX.X, ALU.max))
                        link(dve.tensor_tensor(pick_, view[5], per_node(sm[2][:, 0:NT]), ALU.is_equal))
                        if first:
                            rest = view[6]
                            link(dve.scalar_tensor_tensor(out=sm[6][:], in0=sm[3][:], scalar=-4.0, in1=sm[0][:],
                                                          op0=ALU.mult, op1=ALU.add))
                    link(dve.tensor_tensor(sm[3][:], sm[3][:], sm[4][:], ALU.add))
                    link(dve.tensor_tensor(sm[0][:], sm[0][:], sm[3][:], ALU.mult))
                    if shares:
                        link(dve.tensor_reduce(sm[2][:, 0:NT], view[0], AX.X, ALU.add))
                        link(dve.reciprocal(sm[2][:, 0:NT], sm[2][:, 0:NT]))
                        link(dve.tensor_tensor(view[0], view[0], per_node(sm[2][:, 0:NT]), ALU.mult))
                dve.tensor_copy(CW[:].rearrange("p e t -> p t e"), view[0]).then_inc(cw_ready, 1)
                for lo, n_ in ((0, 4 * P), (4 * P, P)):
                    ps = x_full_slot()
                    x_emptied(dve.tensor_copy(CWT[:, lo:lo + n_], ps[0:E, 0:n_]))
                for i in range(NT):
                    ps = t_full_slot()
                    t_emptied(dve.tensor_tensor(X[:, i, :], ps[0:P, 0:D], X[:, i, :], ALU.add))

            def add_experts(scale=None):
                with dve.Fori(0, E // 2) as i:
                    t.enter(i, 2 * NT)
                    for b in range(2):
                        if scale is not None:
                            scale(i, b)
                        for m in range(NT):
                            ps = t_full_slot()
                            dve.wait_ge(t_free, t.at(-NT + 1))
                            t_emptied(dve.scalar_tensor_tensor(out=X[:, m, :], in0=ps[0:P, 0:D],
                                                               scalar=CW[:, bass.ds(i * 2 + b, 1), m],
                                                               in1=X[:, m, :], op0=ALU.mult, op1=ALU.add))
                    t.leave(E // 2)

            def add_rows(a, b):
                for i in range(NT):
                    ps = t_full_slot()
                    t_emptied(dve.tensor_tensor(a[:, i, 0:D], ps[0:P, 0:D], b[:, i, :], ALU.add))

            dve.wait_ge(consts, 1)
            dve.wait_ge(ld_idx, 32)
            link(dve.tensor_copy(idx_float, idx[:]))
            link(dve.tensor_reduce(ends[:, 0:1], idx_float[:, 1, :], AX.X, ALU.min))
            dve.tensor_reduce(ends[:, 1:2], idx_float[:, 1, :], AX.X, ALU.max).then_inc(idx_f, 1)
            ps = x_full_slot()
            for w in range(2):
                V(dve.tensor_copy(idxT[:, w, 0:G, :].rearrange("p g r -> p r g"),
                                  ps[0:P, w * R * G:(w + 1) * R * G].rearrange("p (r g) -> p r g", g=G)))
            x_emptied(dve.tensor_copy(endsT[:].rearrange("p a g -> p (a g)"), ps[0:1, 2 * R * G:(2 * R + 2) * G]))
            dve.wait_ge(x_free, xr.n)
            high, low = (endsT[:, w, :].unsqueeze(1).to_broadcast([1, NT, G]) for w in (1, 0))
            held = span[:, :, 0, :]
            V(dve.tensor_tensor(held, high, tile_start[:], ALU.is_ge))
            link(dve.scalar_tensor_tensor(out=span[:, :, 1, :], in0=low, scalar=float(-P), in1=tile_start[:],
                                          op0=ALU.add, op1=ALU.is_lt))
            link(dve.tensor_tensor(held, held, span[:, :, 1, :], ALU.mult))
            link(dve.tensor_tensor(span[:, :, 1, :], held, group_no[:, 1, :].unsqueeze(1).to_broadcast([1, NT, G]), ALU.mult))
            link(dve.tensor_tensor(held, held, group_no[:, 0, :].unsqueeze(1).to_broadcast([1, NT, G]), ALU.mult))
            link(dve.tensor_reduce(bounds[:, 0, :], span[:, :, 0, :], AX.X, ALU.max))
            link(dve.tensor_scalar(bounds[:, 0, :], bounds[:, 0, :], -1.0, float(G), ALU.mult, ALU.add))
            link(dve.tensor_scalar(bounds[:, 0, :], bounds[:, 0, :], float(G - 1), None, ALU.min))
            link(dve.tensor_reduce(last[:], span[:, :, 1, :], AX.X, ALU.max))
            link(dve.tensor_tensor(bounds[:, 1, :], last[:], bounds[:, 0, :], ALU.subtract))
            link(dve.tensor_scalar(bounds[:, 1, :], bounds[:, 1, :], 1.0, None, ALU.max))
            link(dve.memset(bounds[:, 2, 0:1], 0.0))
            for m in range(1, NT):
                link(dve.tensor_tensor(bounds[:, 2, m:m + 1], bounds[:, 2, m - 1:m], bounds[:, 1, m - 1:m], ALU.add))
            dve.tensor_copy(bounds_i[:], bounds[:]).then_inc(bounds_ready, 1)

            dve.wait_ge(ld_x, 16)
            layer_norm(X, XN)
            turned_to(XT)
            dve.wait_ge(bounds_ready, 1)
            first = [dve.value_load(bounds_i[0:1, 0, m:m + 1], min_val=0, max_val=G - 1) for m in range(NT)]
            count = [dve.value_load(bounds_i[0:1, 1, m:m + 1], min_val=1, max_val=G) for m in range(NT)]
            before = [dve.value_load(bounds_i[0:1, 2, m:m + 1], min_val=0, max_val=G * NT) for m in range(NT)]
            for m in range(NT):
                with dve.Fori(0, count[m]) as j:
                    for r in range(R):
                        if r % 2 == 0:
                            dve.wait_ge(hot_used, (before[m] + j) * 2 + (r // 2 + 1))
                        dve.tensor_scalar(hot_src[:, r, :], iota[:], idxT[:, 0, bass.ds(first[m] + j, 1), r],
                                          None, ALU.is_equal)
                        ins = dve.tensor_scalar(hot_dst[:, r, 0:P], iota[:, m * P:m * P + P],
                                                idxT[:, 1, bass.ds(first[m] + j, 1), r], None, ALU.is_equal)
                        if r % 2:
                            ins.then_inc(hot_ready, 1)
            heads = [s[:].rearrange("p (t h) -> p t h", h=H8) for s in sm]

            def by_head(a):
                return a.rearrange("p t (h c) -> p t h c", c=HC)

            def per_head(a):
                return a.unsqueeze(3).to_broadcast([P, NT, H8, HC])

            dve.wait_ge(xn_ready, 1)
            link(dve.tensor_reduce(heads[0], by_head(XN[:, :, 0:D]), AX.X, ALU.add))
            link(dve.tensor_scalar(sm[0][:], sm[0][:], 1.0 / HC, None, ALU.mult))
            link(dve.tensor_tensor(by_head(y0[:]), by_head(XN[:, :, 0:D]), per_head(heads[0]), ALU.subtract))
            link(dve.tensor_tensor(sq0[:], y0[:], y0[:], ALU.mult))
            dve.tensor_reduce(heads[1], by_head(sq0[:]), AX.X, ALU.add).then_inc(l0_std, 1)
            dve.wait_ge(l0_std_r, 1)
            link(dve.tensor_scalar(sm[1][:], sm[1][:], 1e-5, None, ALU.add))
            link(dve.reciprocal(sm[1][:], sm[1][:]))
            link(dve.tensor_tensor(by_head(y0[:]), by_head(y0[:]), per_head(heads[1]), ALU.mult))
            dve.wait_ge(ld_rows, 16)
            V(dve.tensor_tensor(k0[:], y0[:], row("l0_kw"), ALU.mult))
            link(dve.tensor_tensor(v0[:], y0[:], row("l0_vw"), ALU.mult))
            link(dve.tensor_tensor(k0[:], k0[:], row("l0_kb"), ALU.add))
            dve.tensor_tensor(v0[:], v0[:], row("l0_vb"), ALU.add).then_inc(l0_kv, 1)
            for m in range(NT):
                ps = t_full_slot()
                link(dve.tensor_scalar(inv_deg[:, m:m + 1], ps[0:P, D:D + 1], 1.0, None, ALU.max))
                link(dve.reciprocal(inv_deg[:, m:m + 1], inv_deg[:, m:m + 1]))
                t_emptied(dve.tensor_scalar(ag[:, m, :], ps[0:P, 0:D], inv_deg[:, m:m + 1], None, ALU.mult))
            for k in range(6):
                V(dve.tensor_scalar(inv_deg_k[:, k, :], inv_deg[:], 1.0 / (k + 1), None, ALU.mult))
            turned_to(agT)
            ps = t_full_slot()
            dve.wait_ge(ld_small[0], 16)
            link(dve.tensor_copy(wc[:], W("l0_wr")))
            for c in range(KC):
                at = wc[:, c, c * 128:c * 128 + 128]
                link(dve.tensor_tensor(at, at, ident[:], ALU.add))
                ins = dve.scalar_tensor_tensor(out=kv0[:, c, :], in0=ps[:, c * 128:c * 128 + 128], scalar=1.0 / N,
                                               in1=headmask[:], op0=ALU.mult, op1=ALU.mult)
                V(ins) if c == 0 else t_emptied(ins)
            settle()
            t_settle()
            for c in range(KC):
                at = wc[:, c, c * 128:c * 128 + 128]
                ins = dve.tensor_tensor(at, at, kv0[:, c, :], ALU.add)
            ins.then_inc(l0_w, 1)
            dve.wait_ge(xb_ready, 1)
            add_rows(X, XB)
            announce(x_ready)
            layer_norm(X, XN)
            turned_to(XT)
            router(1, "l0_gb", top2=True)
            dve.wait_ge(ld_cols, 32)
            V(dve.tensor_scalar(v12[:, 0, :], col("v1"), 1e-3, None, ALU.add))
            V(dve.tensor_scalar(v12[:, 1, :], col("v2"), 1e-3, None, ALU.add))
            announce(bn_v)
            dve.wait_ge(bn_r, 1)
            for w, s, o in ((0, s1, o1), (1, s2, o2)):
                V(dve.tensor_tensor(s[:], v12[:, w, :], col(f"g{w + 1}"), ALU.mult))
                link(dve.tensor_tensor(o[:], col(f"b{w + 1}"), col(f"m{w + 1}"), ALU.subtract))
                link(dve.tensor_tensor(o[:], o[:], s[:], ALU.mult))
                link(dve.tensor_tensor(o[:], o[:], col(f"be{w + 1}"), ALU.add))
            announce(bn_ready)
            add_experts()
            announce(x_ready)
            layer_norm(X, XN)
            turned_to(XT)
            add_rows(u_pre, row("l1_bin"))
            announce(l1_pre)
            for i in range(NT):
                ps = t_full_slot()
                dve.tensor_scalar(k_neg[:, i, :], ps[0:P, 0:D], 0.0, None, ALU.min).then_inc(l1_kmin, 1)
                V(dve.tensor_scalar(k1[:, i, :], ps[0:P, 0:D], 0.0, None, ALU.max))
                t_emptied(dve.tensor_copy(v1m[:, i, :], ps[0:P, D:2 * D]))
            settle()
            dve.wait_ge(l1_kexp, 1)
            dve.tensor_tensor(k1[:], k1[:], k_neg[:], ALU.add).then_inc(l1_k, 1)
            dve.wait_ge(l1_q, 1)
            dve.tensor_tensor(q_pos[:], q_pos[:], q_neg[:], ALU.add).then_inc(l1_qT, 1)
            ps = t_full_slot()
            for c in range(KC):
                V(dve.tensor_scalar(bd[:, c, 128:132], headcols[:], ps[:, D + c:D + c + 1], None, ALU.mult))
                ins = dve.tensor_tensor(bd[:, c, 0:128], ps[:, c * 128:c * 128 + 128], headmask[:], ALU.mult)
                V(ins) if c == 0 else t_emptied(ins)
            announce(l1_bd)
            for i in range(NT):
                ps = t_full_slot()
                p3 = ps[0:P, 0:KC * 132].rearrange("p (c n) -> p c n", c=KC)
                z = sm[i][:, 0:8].rearrange("p (c h) -> p c h", c=KC)
                link(dve.tensor_scalar(z, p3[:, :, 128:132], 1e-6, None, ALU.add))
                link(dve.reciprocal(sm[i][:, 0:8], sm[i][:, 0:8]))
                for c in range(KC):
                    ins = dve.tensor_tensor(mix[:, i, c * 128:c * 128 + 128].rearrange("p (h e) -> p h e", e=HC),
                                            p3[:, c, 0:128].rearrange("p (h e) -> p h e", e=HC),
                                            z[:, c, :].unsqueeze(2).to_broadcast([P, 4, HC]), ALU.mult)
                    V(ins) if c == 0 else t_emptied(ins)
            t_settle()
            settle()
            link(dve.tensor_tensor(mix[:], mix[:], XN[:, :, 0:D], ALU.add))
            layer_norm(mix, x1m, None)
            link(dve.tensor_tensor(x1m[:], x1m[:], row("l1_g1"), ALU.mult))
            dve.tensor_tensor(x1m[:], x1m[:], row("l1_b1"), ALU.add).then_inc(l1_x1, 1)
            V(dve.memset(x1T[:, :, N:TP], 0.0))
            turned_to(x1T)
            dve.wait_ge(l1_x1b, 1)
            add_rows(mix, x1b)
            t_settle()
            layer_norm(mix, mix, None)
            link(dve.tensor_tensor(mix[:], mix[:], row("l1_g2"), ALU.mult))
            link(dve.tensor_tensor(mix[:], mix[:], row("l1_be2"), ALU.add))
            dve.wait_ge(xb_ready, 2)
            link(dve.tensor_tensor(XB[:], XB[:], mix[:], ALU.add))
            with dve.Fori(0, 3) as i:
                t.enter(i, 2 * NT)
                for b in range(2):
                    for m in range(NT):
                        ps = t_full_slot()
                        if m == 0:
                            dve.wait_ge(l1_sum, i * 2 + (b + 1))
                        ins = dve.tensor_scalar(term[1 - b][:, m, :], ps[0:P, 0:D],
                                                inv_deg_k[:, bass.ds(i * 2 + b, 1), m], None, ALU.mult)
                        t_emptied(ins)
                    dve.wait_ge(t_free, t.at())
                    dve.nop().then_inc(l1_term, 1)
                t.leave(3)
            turned_to(totalT)
            add_rows(X, XB)
            announce(x_ready)
            layer_norm(X, XN)
            turned_to(XT)
            router(2, "l1_br")
            add_experts()
            announce(x_ready)
            layer_norm(X, XN)
            turned_to(XT)
            for i in range(NT):
                ps = t_full_slot()
                t_emptied(dve.tensor_copy(he[:, i, :, 0:HC], ps[0:P, 0:D].rearrange("p (h c) -> p h c", c=HC)))
            t_settle()
            for w, name in ((0, "l2_as"), (1, "l2_ad")):
                a, b = ROWS[name]
                for i in range(NT):
                    V(dve.tensor_tensor(hm[:, i, :].rearrange("p (h c) -> p h c", c=HC), he[:, i, :, 0:HC],
                                        w_rows[:, a:b].rearrange("p (h c) -> p h c", c=HC), ALU.mult))
                settle()
                V(dve.tensor_reduce(hsum[:, w], by_head(hm[:]), AX.X, ALU.add))
                settle()
            announce(l2_ab)
            for tiles, lo in (((0, 1, 2, 3), 0), ((4,), 512)):
                ps = t_full_slot()
                t_emptied(dve.tensor_copy(v2m[:, lo:lo + len(tiles) * 128], ps[0:P, 0:len(tiles) * 128]))
            for lo, n_ in ((0, 4 * P), (4 * P, P)):
                ps = x_full_slot()
                x_emptied(dve.tensor_copy(asT[:, lo:lo + n_], ps[0:H8, 0:n_]))
            dve.wait_ge(f_free, F_K2)
            link(dve.tensor_reduce(kcol[:, 2:3], k2T[:, 0:N], AX.X, ALU.max))
            dve.tensor_scalar(kcol[:, 0:1], kcol[:, 2:3], -1.0, None, ALU.mult).then_inc(l2_kmax, 1)
            for tiles, lo in (((0, 1, 2, 3), 0), ((4,), 512)):
                ps = x_full_slot()
                x_emptied(dve.tensor_copy(k2m[:, lo:lo + len(tiles) * 128], ps[0:P, 0:len(tiles) * 128]))
            ps = t_full_slot()
            t_emptied(dve.tensor_tensor(ctT, ps[:, 0:128], headmask[:], ALU.mult))
            link(dve.reciprocal(kcol[:, 3:4], kcol[:, 1:2]))
            ps = t_full_slot()
            t_emptied(dve.tensor_scalar(gw2, ps[:, 0:D], kcol[:, 3:4], HC ** -0.5, ALU.mult, ALU.mult))
            dve.wait_ge(xb_ready, 3)
            add_rows(XB, XB)
            t_settle()
            for m in range(NT):
                V(dve.tensor_scalar(no_edge[:, m, :], A[:, m, :], 0.0, NO_EDGE, ALU.is_equal, ALU.mult))
            settle()
            dve.wait_ge(f_free, F_K2 + H8)
            units = Count(2)

            def head_row(h):
                V(dve.tensor_copy(a_now[:], a_row[:, h, 0:N].rearrange("p a n -> p (a n)")))

            def masked(b, m):
                V(dve.tensor_tensor_reduce(out=zm[b][:, m, :], in0=a_now[:], in1=no_edge[:, m, :],
                                           scale=1.0, scalar=-3e38, op0=ALU.add, op1=ALU.max,
                                           accum_out=mx[:, m:m + 1]))

            def biases(h):
                adh, zh, gh, b1h, b2h = (y[:, h, :].rearrange("p a n -> p (a n)") for y in (ad_h, z2, gm, gb1, gb2))
                settle()
                link(dve.tensor_tensor(zh, mx[:], adh, ALU.add))
                link(dve.scalar_tensor_tensor(out=gh, in0=zh, scalar=0.2, in1=zh, op0=ALU.mult, op1=ALU.max))
                link(dve.tensor_tensor(b1h, adh, gh, ALU.subtract))
                dve.scalar_tensor_tensor(out=b2h, in0=adh, scalar=0.2, in1=gh, op0=ALU.mult, op1=ALU.subtract)\
                   .then_inc(g_bias, 1)

            def to_sbuf(m, back):
                s = (units.n - back) % 2
                dve.wait_ge(g_full, units.at(3 - back))
                dve.tensor_tensor(pT[s][:], spread(psF, s)[0:P, :, 0:P], AT[:, :, m * P:m * P + P], ALU.mult)\
                   .then_inc(g_free, 1)

            def head(h, b, following):
                if following is not None:
                    head_row(following)
                for m in range(NT):
                    s = units.slot
                    settle()
                    dve.wait_ge(g_exp, units.at(1))
                    dve.tensor_tensor(e1[s], e1[s], e2[s], ALU.max).then_inc(g_e, 1)
                    if following is not None:
                        masked(1 - b, m)
                    if m:
                        to_sbuf(m - 1, 1)
                    units.n += 1
                if following is not None:
                    biases(following)
                to_sbuf(NT - 1, 1)
                ps = t_full_slot()
                p3 = ps[0:P, 0:NT * (HC + 1)].rearrange("p (m n) -> p m n", m=NT)
                link(dve.tensor_scalar(den[:], p3[:, :, HC], 1e-16, None, ALU.add))
                link(dve.reciprocal(den[:], den[:]))
                t_emptied(dve.tensor_tensor(ACC[:].rearrange("p t (h c) -> p t h c", c=HC)[:, :, h, :].rearrange("p t a c -> p t (a c)"),
                                            p3[:, :, 0:HC], den[:].unsqueeze(2).to_broadcast([P, NT, HC]), ALU.mult))

            head_row(bass.ds(0, 1))
            settle()
            for m in range(NT):
                masked(0, m)
            biases(bass.ds(0, 1))
            with dve.Fori(0, H8 // 2 - 1) as i:
                t.enter(i, 2)
                v.enter(i, 2 * (NT + 6))
                units.enter(i, 2 * NT)
                for b in range(2):
                    head(bass.ds(i * 2 + b, 1), b, bass.ds(i * 2 + b + 1, 1))
                units.leave(H8 // 2 - 1)
                v.leave(H8 // 2 - 1)
                t.leave(H8 // 2 - 1)
            head(bass.ds(H8 - 2, 1), 0, bass.ds(H8 - 1, 1))
            head(bass.ds(H8 - 1, 1), 1, None)
            t_settle()
            link(dve.tensor_tensor(ACC[:], ACC[:], row("l2_bias"), ALU.add))
            link(dve.tensor_scalar(ACC[:], ACC[:], 0.0, None, ALU.max))
            dve.tensor_tensor(X[:], XB[:], ACC[:], ALU.add).then_inc(x_ready, 1)
            dve.wait_ge(x_ready, 5)
            layer_norm(X, XN)
            turned_to(XT)
            dve.wait_ge(xb_ready, 4)
            add_rows(X, XB)
            announce(x_ready)
            layer_norm(X, XN)
            turned_to(XT)
            a, b = ROWS["l3_bqk"]
            for i in range(NT):
                ps = t_full_slot()
                t_emptied(dve.tensor_tensor(qk[:, i, :], ps[0:P, :], w_rows[:, a:b], ALU.add))
            t_settle()
            link(dve.tensor_reduce(sm[0][:, 0:2 * NT], qk[:].rearrange("p t (w n) -> p (t w) n", n=D), AX.X, ALU.add))
            dve.tensor_scalar(sm[0][:, 0:2 * NT], sm[0][:, 0:2 * NT], -1.0 / D, None, ALU.mult).then_inc(l3_qk, 1)
            for i in range(NT):
                ps = t_full_slot()
                t_emptied(dve.tensor_copy(y3[:, i, :], ps[0:P, 0:D]))
            announce(l3_y1)
            add_rows(v3, row("l3_bv"))
            dve.wait_ge(l3_sq, 1)
            link(dve.tensor_scalar(sm[1][:, 0:2 * NT], sm[1][:, 0:2 * NT], 1e-7, None, ALU.add))
            link(dve.reciprocal(sm[1][:, 0:2 * NT], sm[1][:, 0:2 * NT]))
            for i in range(NT):
                for w in range(2):
                    V(dve.tensor_scalar(qk2[:, i, w * D:w * D + D], qk2[:, i, w * D:w * D + D],
                                        sm[1][:, 2 * i + w:2 * i + w + 1], None, ALU.mult))
            announce(l3_qn)
            for i in range(NT):
                ps = t_full_slot()
                t_emptied(dve.tensor_scalar(gnn3[:, i, :], ps[0:P, 0:D], 0.0, None, ALU.max))
            announce(l3_gnn)
            dve.wait_ge(l3_nr, 1)
            link(dve.tensor_scalar(sm[4][:, 0:NT], sm[4][:, 0:NT], 1e-12, None, ALU.max))
            link(dve.reciprocal(sm[4][:, 0:NT], sm[4][:, 0:NT]))
            for i in range(NT):
                ins = dve.tensor_scalar(qk2[:, i, 0:D], qk2[:, i, 0:D], sm[4][:, i:i + 1], None, ALU.mult)
            ins.then_inc(l3_q, 1)
            ps = t_full_slot()
            t_emptied(dve.tensor_copy(kcol[:, 0:KC], ps[:, 0:KC]))
            announce(l3_kn2)
            ps = t_full_slot()
            t_emptied(dve.tensor_copy(kvT[:].rearrange("p c n -> p (c n)"), ps[:]))
            dve.wait_ge(l3_knr, 1)
            link(dve.tensor_scalar(kcol[:, 0:KC], kcol[:, 0:KC], 1e-12, None, ALU.max))
            link(dve.reciprocal(kcol[:, 0:KC], kcol[:, 0:KC]))
            ps = t_full_slot()
            V(dve.tensor_scalar(gw3[:, 0, :], ps[:, 0:D], kcol[:, 0:1], N ** -0.5, ALU.mult, ALU.mult))
            t_emptied(dve.tensor_scalar(gw3[:, 1, :], ps[:, D:2 * D], kcol[:, 1:2], N ** -0.5, ALU.mult, ALU.mult))
            announce(l3_gw)
            turned_to(qT3)
            dve.wait_ge(xb_ready, 6)
            add_rows(X, XB)
            announce(x_ready)
            layer_norm(X, XN)
            turned_to(XT)
            router(3, "l3_br", top2=True, shares=True)
            t_settle()
            layer_norm(XN, XN)
            turned_to(XT)
            dve.wait_ge(x_free, xr.n)

            def expert_input(i, b):
                dve.wait_ge(ffn_used, i * 2 + (2 * E + b + 1))
                for c in range(KC):
                    at = bass.ds((i * 2 + b) * KC + c, 1)
                    ins = dve.tensor_scalar(xe[b][:, c, 0:N], XT[:, c, 0:N], col("l3_g")[:, at], col("l3_b")[:, at],
                                            ALU.mult, ALU.add)
                ins.then_inc(xe_ready, 1)

            for b in range(2):
                link(dve.memset(xe[b][:, :, N:TP], 0.0))
            add_experts(expert_input)
            announce(x_ready)


_INPUTS = ["x", "src", "dst"]


def kernel(**inputs):
    import numpy as _np
    import concourse.bacc as _bacc
    from concourse import mybir as _mybir
    from concourse.bass_utils import run_bass_kernel_spmd as _run

    a = {k: _np.asarray(v) for k, v in inputs.items()}

    def chunks(w):
        return w.reshape(-1, 128, w.shape[-1]).transpose(1, 0, 2).reshape(128, -1)

    def packed(table, parts):
        assert list(parts) == [n for n in table if n != "end"]
        return _np.ascontiguousarray(_np.concatenate(list(parts.values()), axis=-1))

    def columns(v):
        return v.reshape(-1, 128).T

    small = packed(SMALL, {
        "l0_wl": chunks(a["L0_gnn_W_l"].T), "l0_wr": chunks(a["L0_gnn_W_r"].T), "l0_gate": chunks(a["L0_ffn_gate_w"]),
        "l1_win": chunks(a["L1_gnn_W_in"].T), "l1_qkv": chunks(a["L1_mix_Wqkv"].T), "l1_w1": chunks(a["L1_mix_W1"].T),
        "l1_w2": chunks(a["L1_mix_W2"].T), "l1_wout": chunks(a["L1_gnn_W_out"].T), "l1_wr": chunks(a["L1_ffn_Wr"]),
        "l2_w": chunks(a["L2_gnn_W"].reshape(D, D)), "l2_qkv": chunks(a["L2_mix_W_qkv"]),
        "l2_wout": chunks(a["L2_mix_W_out"]), "l2_ffn": chunks(a["L2_ffn_weight"].T),
        "l3_w0": chunks(a["L3_gnn_w0"]), "l3_w1": chunks(a["L3_gnn_w1"]), "l3_qkv": chunks(a["L3_mix_W_qkv"]),
        "l3_wout": chunks(a["L3_mix_W_out"]), "l3_wr": chunks(a["L3_ffn_Wr"])})
    bqkv = a["L3_mix_b_qkv"]
    rows = packed(ROWS, {
        "l0_br": a["L0_gnn_b_r"], "l0_kw": a["L0_mix_kln_weight"].reshape(-1), "l0_kb": a["L0_mix_kln_bias"].reshape(-1),
        "l0_vw": a["L0_mix_vln_weight"].reshape(-1), "l0_vb": a["L0_mix_vln_bias"].reshape(-1),
        "l0_gb": a["L0_ffn_gate_b"], "l1_bin": a["L1_gnn_b_in"], "l1_bout": a["L1_gnn_b_out"],
        "l1_g1": a["L1_mix_ln1_g"], "l1_b1": a["L1_mix_ln1_b"], "l1_b2": a["L1_mix_b2"], "l1_g2": a["L1_mix_ln2_g"],
        "l1_be2": a["L1_mix_ln2_b"], "l1_br": a["L1_ffn_br"], "l2_as": a["L2_gnn_att_src"].reshape(-1),
        "l2_ad": a["L2_gnn_att_dst"].reshape(-1), "l2_bias": a["L2_gnn_bias"], "l2_bout": a["L2_mix_b_out"],
        "l2_ffnb": a["L2_ffn_bias"], "l3_bqk": bqkv[:2 * D], "l3_bv": bqkv[2 * D:], "l3_bout": a["L3_mix_b_out"],
        "l3_br": a["L3_ffn_br"]})
    cols = packed(COLS, {
        "l0_b1": columns(a["L0_ffn_b1"]), "l1_mb1": columns(a["L1_mix_b1"]),
        "b1": columns(a["L1_ffn_b1"]), "g1": columns(a["L1_ffn_g1"]), "be1": columns(a["L1_ffn_be1"]),
        "m1": columns(a["L1_ffn_m1"]), "v1": columns(a["L1_ffn_v1"]),
        "b2": columns(a["L1_ffn_b2"]), "g2": columns(a["L1_ffn_g2"]), "be2": columns(a["L1_ffn_be2"]),
        "m2": columns(a["L1_ffn_m2"]), "v2": columns(a["L1_ffn_v2"]), "l3_bv": columns(bqkv[2 * D:]),
        "l3_g": columns(a["L3_ffn_ln_g"]), "l3_b": columns(a["L3_ffn_ln_b"]), "l3_b1": columns(a["L3_ffn_b1"])})
    eb2 = _np.ascontiguousarray(_np.stack([a["L0_ffn_b2"], a["L1_ffn_bo"], a["L3_ffn_b2"]], axis=1))

    def experts(*layers):
        return _np.ascontiguousarray(_np.stack([_np.concatenate([chunks(w[e]) for w in layers], axis=1) for e in range(E)]))

    arrays = {"x": a["x"], "src": a["src"], "dst": a["dst"], "small": small, "rows": rows, "cols": cols, "eb2": eb2,
              "ffn0": experts(a["L0_ffn_W1"], a["L0_ffn_W2"]),
              "ffn1": experts(a["L1_ffn_W1"], a["L1_ffn_W2"], a["L1_ffn_Wo"]),
              "ffn3": experts(a["L3_ffn_W1"], a["L3_ffn_W2"])}
    arrays = {f"in_{k}": _np.ascontiguousarray(v) for k, v in arrays.items()}
    nc = _bacc.Bacc("TRN2", target_bir_lowering=False, num_devices=1)
    args = [nc.dram_tensor(k, v.shape, _mybir.dt.from_np(v.dtype), kind="ExternalInput").ap() for k, v in arrays.items()]
    args.append(nc.dram_tensor("out_x", (N, D), F32, kind="ExternalOutput").ap())
    gps_network(nc, *args)
    r = _run(nc, [arrays], core_ids=[0])
    return r.results[0]["out_x"]
```

```python
from contextlib import ExitStack

import numpy as np

import concourse.bass as bass
from concourse import mybir

F32 = mybir.dt.float32
BF16 = mybir.dt.bfloat16
F16 = mybir.dt.float16
F32R = mybir.dt.float32r
I32 = mybir.dt.int32
ALU = mybir.AluOpType
ACT = mybir.ActivationFunctionType
AX = mybir.AxisListType

N = 625
D = 256
P = 125
NT = N // P
KC = D // 128
TP = 628
TH = TP // 2
E = 8
NE = 20000
G, R = 40, 4
H8, HC = 8, 32
S = 128
ITEMS = (2 * N + E * (S - 1)) // S
PAIRS = (ITEMS + 1) // 2
LN_EPS = 1e-5
NO_EDGE = -1e30

SMALL = {}
ROWS = {}
COLS = {}


def _place(table, parts):
    at = 0
    for name, n in parts:
        table[name] = (at, at + n)
        at += n
    table["end"] = at


SMALL_L0 = [("l0_wl", KC * D), ("l0_wr", KC * D), ("l0_gate", KC * E)]
SMALL_L1 = [("l1_win", KC * D), ("l1_qkv", KC * 3 * D), ("l1_w1", KC * D), ("l1_w2", KC * D),
            ("l1_wout", KC * D), ("l1_wr", KC * E)]
SMALL_L2 = [("l2_w", KC * D), ("l2_qkv", KC * 384), ("l2_wout", D), ("l2_ffn", KC * D)]
SMALL_L3 = [("l3_w0", KC * D), ("l3_w1", KC * D), ("l3_qkv", KC * 3 * D), ("l3_wout", KC * D), ("l3_wr", KC * E)]
_place(SMALL, SMALL_L0 + SMALL_L1 + SMALL_L2 + SMALL_L3)
_place(ROWS, [("l0_br", D), ("l0_kw", D), ("l0_kb", D), ("l0_vw", D), ("l0_vb", D), ("l0_gb", E),
              ("l1_bin", D), ("l1_bout", D), ("l1_g1", D), ("l1_b1", D), ("l1_b2", D), ("l1_g2", D),
              ("l1_be2", D), ("l1_br", E), ("l2_as", D), ("l2_ad", D), ("l2_bias", D), ("l2_bout", D),
              ("l2_ffnb", D), ("l3_bqk", 2 * D), ("l3_bv", D), ("l3_bout", D), ("l3_br", E)])
_place(COLS, [("l0_b1", E * 4), ("l1_mb1", KC), ("b1", 16), ("g1", 16), ("be1", 16), ("m1", 16), ("v1", 16),
              ("b2", 16), ("g2", 16), ("be2", 16), ("m2", 16), ("v2", 16), ("l3_bv", KC),
              ("l3_g", 16), ("l3_b", 16), ("l3_b1", E * 8)])
FFN0, FFN1, FFN3 = KC * 512 + 4 * D, 6 * D, KC * 1024 + 8 * D


class Count:

    def __init__(self, slots=1):
        self.n, self.more, self.slots = 0, None, slots

    def at(self, d=0):
        return self.n + d if self.more is None else self.more + (self.n + d)

    @property
    def slot(self):
        return self.n % self.slots

    def enter(self, i, per):
        assert per % self.slots == 0
        self.first, self.per, self.more = self.n, per, i * per

    def leave(self, times):
        assert self.n - self.first == self.per, (self.n - self.first, self.per)
        self.n, self.more = self.first + times * self.per, None


def gps_network(nc, x, src, dst, small, rows, cols, eb2, ffn0, ffn1, ffn3, out):
    with ExitStack() as ctx:
        def sb(name, shape, dt=F32):
            return ctx.enter_context(nc.sbuf_tensor(name, shape, dt))

        def sem(name):
            return ctx.enter_context(nc.semaphore(name))

        def next_at():
            return -(-nc.sbuf_base // 32) * 32

        w_small = sb("w_small", [128, SMALL["end"]])
        w_rows = sb("w_rows", [P, ROWS["end"]])
        w_cols = sb("w_cols", [128, COLS["end"]])
        w_eb2 = sb("w_eb2", [E, 3, D])
        w_ffn = sb("w_ffn", [128, 2, FFN3])

        def W(name, k=KC):
            a, b = SMALL[name]
            return w_small[:, a:b].rearrange("p (c n) -> p c n", c=k)

        def row(name, tiles=NT):
            a, b = ROWS[name]
            return w_rows[:, a:b].unsqueeze(1).to_broadcast([P, tiles, b - a])

        def col(name):
            a, b = COLS[name]
            return w_cols[:, a:b]

        ident = sb("ident", [128, 128])
        headmask = sb("headmask", [128, 128])
        headcols = sb("headcols", [128, 4])
        pick = sb("pick", [E, H8, 128])
        ones = sb("ones", [128, 2])
        order = sb("order", [P, E])
        minus_half, half = sb("minus_half", [128, 16]), sb("half", [128, 16])
        group_no = sb("group_no", [1, 2, G])
        tile_start = sb("tile_start", [1, NT, G])

        earlier = sb("earlier", [P, S])
        all_ones = sb("all_ones", [P, S])
        ident_r = sb("ident_r", [P, S], F32R)
        slot_no = sb("slot_no", [P, S], F16)
        upto = sb("upto", [128, E, E])
        tile_end = sb("tile_end", [128, NT])
        item_no = sb("item_no", [128, 2 * PAIRS + 1])
        pair_no = sb("pair_no", [128, PAIRS])

        ends = sb("ends", [G, 2])
        endsT = sb("endsT", [1, 2, G])
        last = sb("last", [1, NT])
        bounds = sb("bounds", [1, 3, NT])
        bounds_i = sb("bounds_i", [1, 3, NT], I32)
        a_mem = sb("a_mem", [128, NT * N])
        A = a_mem[0:P, :].rearrange("p (m n) -> p m n", n=N)
        at_mem = sb("at_mem", [128, NT * N])
        AT = at_mem[0:P, :].rearrange("p (m n) -> p m n", n=N)
        idx = at_mem[0:G, 0:1000].bitcast(I32).rearrange("g (w k) -> g w k", w=2)
        idxT = at_mem[0:P, 1000:1640].rearrange("p (w g r) -> p w g r", w=2, r=R)
        span = at_mem[0:1, 1640:2040].rearrange("p (m w g) -> p m w g", m=NT, w=2)
        hot_dst = at_mem[0:P, 2040:2296].bitcast(BF16).rearrange("p (r n) -> p r n", r=R)
        iota = at_mem[0:P, 2296:2616].bitcast(F16)
        zeros = at_mem[0:1, 2616:2872].bitcast(BF16)

        def tm(name, n=D):
            return sb(name, [P, NT, n])

        def fm(name):
            return sb(name, [128, KC, TP])

        X, XN = tm("X"), tm("XN", D + 1)
        xb_at, XB = next_at(), tm("XB")
        acc_at, ACC = next_at(), tm("ACC")
        XT = fm("XT")
        big_at = next_at()
        big = sb("big", [128, 2, 4 * NT * D])
        CW = sb("CW", [P, E, NT])
        CWT = sb("CWT", [E, TP])
        stats = sb("stats", [P, NT, 6])
        mv = sb("mv", [P, NT, 2])
        var_e = sb("var_e", [P, NT])
        rstd = sb("rstd", [P, NT])
        inv_deg = sb("inv_deg", [P, NT])
        inv_deg_k = sb("inv_deg_k", [P, 6, NT])
        s1, s2 = sb("s1", [128, 16]), sb("s2", [128, 16])
        o1, o2 = sb("o1", [128, 16]), sb("o2", [128, 16])
        v12 = sb("v12", [128, 2, 16])
        sm = [sb(f"sm{i}", [P, 40]) for i in range(8)]
        kcol = sb("kcol", [128, 8])

        def scratch(i, shape):
            n = int(np.prod(shape[1:]))
            lo = (i % 4) * NT * D
            v = big[0:shape[0], i // 4, lo:lo + n]
            if len(shape) == 3:
                return v.rearrange("p (a b) -> p a b", b=shape[2])
            return v

        psF = ctx.enter_context(nc.psum_tensor("psF", [128, 2, 2, 512], F32))
        psT = ctx.enter_context(nc.psum_tensor("psT", [128, 2, 512], F32))
        psX = ctx.enter_context(nc.psum_tensor("psX", [128, 2, 512], F32))

        def spread(ps, slot):
            return ps[:, slot].rearrange("p a n -> p (a n)")[:, 0:NT * 128].rearrange("p (j n) -> p j n", n=128)

        f_full, f_free = sem("f_full"), sem("f_free")
        t_full, t_free = sem("t_full"), sem("t_free")
        x_full, x_free = sem("x_full"), sem("x_free")
        ld_x, ld_idx, ld_rows, ld_cols = sem("ld_x"), sem("ld_idx"), sem("ld_rows"), sem("ld_cols")
        ld_small = [sem(f"ld_small{i}") for i in range(4)]
        ld_ffn = [sem("ld_ffn_a"), sem("ld_ffn_b")]
        ffn_used = sem("ffn_used")
        stored = sem("stored")
        consts = sem("consts")
        v_step, a_step, g_step = sem("v_step"), sem("a_step"), sem("g_step")
        idx_f = sem("idx_f")
        bounds_ready = sem("bounds_ready")
        hot_ready, hot_used = sem("hot_ready"), sem("hot_used")
        var_ready, rstd_ready = sem("var_ready"), sem("rstd_ready")
        xn_ready = sem("xn_ready")
        x_ready = sem("x_ready")
        xb_ready = sem("xb_ready")
        cw_ready = sem("cw_ready")
        l0_std, l0_std_r, l0_kv = sem("l0_std"), sem("l0_std_r"), sem("l0_kv")
        l0_w = sem("l0_w")
        logit_ready, exp_ready = sem("logit_ready"), sem("exp_ready")
        l1_pre, l1_u = sem("l1_pre"), sem("l1_u")
        l1_kmin, l1_kexp, l1_k, l1_q, l1_qT = (sem(n) for n in ("l1_kmin", "l1_kexp", "l1_k", "l1_q", "l1_qT"))
        l1_bd, l1_x1, l1_x1b = sem("l1_bd"), sem("l1_x1"), sem("l1_x1b")
        l1_term, l1_sum = sem("l1_term"), sem("l1_sum")
        bn_v, bn_r, bn_ready = sem("bn_v"), sem("bn_r"), sem("bn_ready")
        l2_ab, l2_kT, l2_kmax, l2_kexp, l2_g = (sem(n) for n in ("l2_ab", "l2_kT", "l2_kmax", "l2_kexp", "l2_g"))
        g_bias, g_exp, g_e, g_full, g_free = (sem(n) for n in ("g_bias", "g_exp", "g_e", "g_full", "g_free"))
        l3_qk, l3_sq, l3_qn, l3_qq, l3_nr = (sem(n) for n in ("l3_qk", "l3_sq", "l3_qn", "l3_qq", "l3_nr"))
        l3_kk, l3_kn2, l3_knr, l3_y1, l3_gnn, l3_q, l3_gw = (sem(n) for n in ("l3_kk", "l3_kn2", "l3_knr", "l3_y1", "l3_gnn", "l3_q", "l3_gw"))

        class ItemSems:

            def __init__(self, level):
                def s(name):
                    return sem(f"{name}{level}")
                self.plan = s("plan")
                self.split = s("split")
                self.weights = [s("weights_a"), s("weights_b")]
                self.hot = s("hot")
                self.x_full, self.x_ready = s("ix_full"), s("ix_ready")
                self.h_full, self.h_ready = s("ih_full"), s("ih_ready")
                self.hot_full, self.hot_out = s("hot_full"), s("hot_out")
                self.y_full, self.y_ready = s("iy_full"), s("iy_ready")
                self.o_full, self.o_free = s("io_full"), s("io_free")
                self.step = s("item_step")

        items = [ItemSems(0), ItemSems(3)]

        hot_src = ACC[:].rearrange("p t d -> p (t d)").bitcast(BF16).rearrange("p (r n) -> p r n", r=R)
        y0, k0, v0 = scratch(0, [P, NT, D]), scratch(1, [P, NT, D]), scratch(2, [P, NT, D])
        sq0 = scratch(3, [P, NT, D])
        ag, agT = scratch(4, [P, NT, D]), scratch(5, [128, KC, TP])
        wc, kv0 = scratch(6, [128, KC, D]), scratch(4, [128, KC, 128])
        idx_float = scratch(7, [G, 2, R * P])
        u_pre, u = scratch(0, [P, NT, D]), scratch(1, [P, NT, D])
        k_neg, k1, v1m = scratch(2, [P, NT, D]), scratch(3, [P, NT, D]), scratch(4, [P, NT, D])
        q_neg, q_pos = scratch(5, [128, KC, TP]), scratch(6, [128, KC, TP])
        bd = scratch(7, [128, KC, 132])
        mix, x1m, x1T, hT1, x1b = (scratch(2, [P, NT, D]), scratch(3, [P, NT, D]), scratch(4, [128, KC, TP]),
                                   scratch(5, [128, KC, TP]), scratch(6, [P, NT, D]))
        term = [scratch(1, [P, NT, D]), scratch(0, [P, NT, D])]
        total, totalT = ACC, scratch(7, [128, KC, TP])
        a_row = big[0:P, 0, 0:H8 * TP].rearrange("p (h n) -> p h n", n=TP)
        no_edge = big[0:P, 1, 0:NT * N].rearrange("p (m n) -> p m n", n=N)
        he = sb("he", [P, NT, H8, HC + 1])
        zm = [w_ffn[0:P, i, 0:NT * N].rearrange("p (m n) -> p m n", n=N) for i in range(2)]
        e1 = [w_ffn[0:P, i, NT * N + 3:NT * N + 3 + N] for i in range(2)]
        e2 = [big[0:P, 1, (5 + i) * TP:(5 + i) * TP + N] for i in range(2)]
        pT = [XT[0:P, i, 0:N].rearrange("p (j n) -> p j n", n=P) for i in range(2)]
        q2T, k2T, kx2 = big[:, 1, 0:TP], big[:, 1, TP:2 * TP], big[:, 1, 2 * TP:3 * TP]
        k2m, v2m = big[0:P, 1, 3 * TP:3 * TP + 640], big[0:P, 1, 4 * TP + 12:4 * TP + 652]
        ctT, gw2 = big[:, 1, 5 * TP + 24:5 * TP + 152], big[:, 1, 5 * TP + 152:5 * TP + 408]
        hm = scratch(3, [P, NT, D])
        hsum = sb("hsum", [P, 2, NT, H8])
        asT = CWT
        mx = sb("mx", [P, NT])
        a_now = sb("a_now", [P, N])
        gm, gb1, gb2, z2 = (sb(n, [P, H8, NT]) for n in ("gm", "gb1", "gb2", "z2"))
        ad_h = hsum[:, 1].rearrange("p t h -> p h t")
        den = sb("den", [P, NT])
        qk = big[0:P, 0, 0:NT * 2 * D].rearrange("p (t n) -> p t n", n=2 * D)
        qk2 = big[0:P, 1, 0:NT * 2 * D].rearrange("p (t n) -> p t n", n=2 * D)
        gnn3 = XN[:, :, 0:D]
        y3, v3, vT3, kk3 = scratch(2, [P, NT, D]), scratch(3, [P, NT, D]), scratch(6, [128, KC, TP]), ACC
        qT3, kvT, gw3 = scratch(0, [128, KC, TP]), scratch(7, [128, KC, D]), scratch(7, [128, 2 * KC, D])[:, KC:2 * KC, :]
        pool_at = [0]

        def at(name, shape, offset):
            return nc.alloc_sbuf_tensor_at(name, shape, F32R, offset=offset)[:]

        def piece(parts, shape, name=None):
            n = -(-int(np.prod(shape)) // 8) * 8
            lo, pool_at[0] = pool_at[0], pool_at[0] + n
            if name:
                return at(name, [parts] + shape, big_at + 4 * lo)
            v = big[:].rearrange("p a n -> p (a n)")[0:parts, lo:lo + int(np.prod(shape))]
            if len(shape) == 2:
                return v.rearrange("p (a b) -> p a b", b=shape[1])
            return v

        hot_in = [piece(P, [NT, S], f"hot_in{b}") for b in range(2)]
        hot_out = piece(S, [TP], "hot_out")
        x_item = piece(128, [KC, S])
        h_item = piece(128, [8, S])
        y_item = piece(S, [2, D], "y_item")
        chosen = piece(P, [NT + 1, E])
        choice_sum = piece(P, [NT + 1, E])
        rank_p1 = piece(P, [NT, E])
        rank = piece(P, [E, NT])
        rank_item = [piece(P, [NT]) for _ in range(2)]
        n_chosen, n_tiles, e_end, e_start = (piece(128, [E]) for _ in range(4))
        by_tile = piece(128, [E, NT])
        by_expert = piece(128, [E, E])
        by_item, by_item2 = (piece(128, [2 * PAIRS + 1, E]) for _ in range(2))
        item_e, item_start, item_off = (piece(128, [2 * PAIRS + 1]) for _ in range(3))
        by_pair, n_pairs = piece(128, [PAIRS]), piece(128, [1])
        plan = piece(1, [2 * PAIRS + 2]).bitcast(I32)
        assert pool_at[0] <= 8 * NT * D
        xn_high, xn_low = at("xn_high", [P, NT, D], xb_at), at("xn_low", [P, NT, D], acc_at)

        hidden = [big[:, u_, 0:8 * TP].rearrange("p (k n) -> p k n", n=TP) for u_ in range(2)]

        F_K2 = 2 * NT + 2 * KC + E * 2 * KC + 2

        block = ctx.enter_context(nc.Block())

        @block.sync
        def _(sp):
            sp.dma_start(X[:], x.rearrange("(t p) d -> p t d", p=P)).then_inc(ld_x, 16)
            sp.dma_start(idx[:, 1, :], dst.rearrange("(g k) -> g k", g=G)).then_inc(ld_idx, 16)
            sp.dma_start(idx[:, 0, :], src.rearrange("(g k) -> g k", g=G)).then_inc(ld_idx, 16)
            sp.dma_start(w_rows[:], rows.partition_broadcast(P)).then_inc(ld_rows, 16)
            edge = [0, SMALL["l1_win"][0], SMALL["l2_w"][0], SMALL["l3_w0"][0], SMALL["end"]]
            sp.dma_start(w_small[:, edge[0]:edge[1]], small[:, edge[0]:edge[1]]).then_inc(ld_small[0], 16)
            sp.dma_start(w_cols[:], cols).then_inc(ld_cols, 16)
            sp.dma_start(w_eb2[:], eb2).then_inc(ld_cols, 16)
            for n in range(1, 4):
                sp.dma_start(w_small[:, edge[n]:edge[n + 1]], small[:, edge[n]:edge[n + 1]]).then_inc(ld_small[n], 16)

            def item_weights(q, weights, n):
                sp.wait_ge(q.plan, 1)
                pairs = sp.value_load(plan[0:1, 2 * PAIRS + 1:2 * PAIRS + 2], min_val=1, max_val=PAIRS)
                with sp.Fori(0, pairs) as i:
                    for b in range(2):
                        e = sp.value_load(plan[0:1, bass.ds(i * 2 + b, 1)], min_val=0, max_val=E - 1)
                        sp.wait_ge(q.y_full, i * 2 + (b + 1))
                        sp.dma_start(w_ffn[:, b, 0:n], weights[bass.ds(e, 1), :, :].rearrange("o p n -> (o p) n"))\
                          .then_inc(q.weights[b], 16)

            item_weights(items[0], ffn0, FFN0)
            with sp.Fori(0, E // 2) as i:
                for b in range(2):
                    sp.wait_ge(ffn_used, i * 2 + (b + 1))
                    sp.dma_start(w_ffn[:, b, 0:FFN1], ffn1[bass.ds(i * 2 + b, 1), :, :].rearrange("o p n -> (o p) n"))\
                      .then_inc(ld_ffn[b], 16)
            item_weights(items[1], ffn3, FFN3)
            sp.wait_ge(x_ready, 8)
            sp.dma_start(out.rearrange("(t p) d -> p t d", p=P), X[:]).then_inc(stored, 16)
            sp.wait_ge(stored, 16)

        @block.gpsimd
        def _(pool):
            steps = Count()

            def link(ins):
                ins.then_inc(g_step, 1)
                steps.n += 1
                pool.wait_ge(g_step, steps.n)

            for tensor, value in ((ident, 0.0), (pick, 0.0), (headmask, 0.0), (headcols, 0.0), (ones, 1.0),
                                  (minus_half, -0.5), (half, 0.5)):
                link(pool.memset(tensor[:], value))
            link(pool.memset(zeros, 0.0))
            link(pool.memset(XN[:, :, D:D + 1], 1.0))
            link(pool.memset(he[:, :, :, HC:HC + 1], 1.0))
            link(pool.memset(XT[:, :, N:TP], 0.0))
            link(pool.memset(asT[:, N:TP], 0.0))
            link(pool.iota(iota, pattern=[[1, 640]], base=0, channel_multiplier=0, allow_small_or_imprecise_dtypes=True))
            link(pool.iota(order[:], pattern=[[-1, E]], base=E, channel_multiplier=0, allow_small_or_imprecise_dtypes=True))
            link(pool.iota(tile_start[:], pattern=[[P, NT], [0, G]], base=0, channel_multiplier=0, allow_small_or_imprecise_dtypes=True))
            link(pool.iota(group_no[:, 0, :], pattern=[[-1, G]], base=G, channel_multiplier=0, allow_small_or_imprecise_dtypes=True))
            link(pool.iota(group_no[:, 1, :], pattern=[[1, G]], base=1, channel_multiplier=0, allow_small_or_imprecise_dtypes=True))
            link(pool.affine_select(out=ident[:], in_=ident[:], compare_op=ALU.not_equal, fill=1.0, base=0,
                                    pattern=[[-1, 128]], channel_multiplier=1))
            link(pool.affine_select(out=pick[:], in_=pick[:], compare_op=ALU.not_equal, fill=1.0, base=0,
                                    pattern=[[-1, H8], [0, 128]], channel_multiplier=1))
            link(pool.memset(all_ones[:], 1.0))
            link(pool.memset(earlier[:], 1.0))
            link(pool.memset(upto[:], 1.0))
            link(pool.affine_select(out=earlier[:], in_=earlier[:], compare_op=ALU.is_ge, fill=0.0, base=-1,
                                    pattern=[[1, S]], channel_multiplier=-1))
            link(pool.affine_select(out=upto[:], in_=upto[:], compare_op=ALU.is_ge, fill=0.0, base=0,
                                    pattern=[[1, E], [-1, E]], channel_multiplier=0))
            link(pool.tensor_copy(ident_r[:], ident[0:P, 0:S]))
            for tensor, step in ((slot_no, 1), (tile_end, S), (item_no, 1), (pair_no, 2)):
                link(pool.iota(tensor[:], pattern=[[step, tensor.shape[1]]], base=0, channel_multiplier=0,
                               allow_small_or_imprecise_dtypes=True))
            for h in range(4):
                link(pool.memset(headmask[HC * h:HC * h + HC, HC * h:HC * h + HC], 1.0))
                ins = pool.memset(headcols[HC * h:HC * h + HC, h:h + 1], 1.0)
                link(ins) if h < 3 else ins.then_inc(consts, 1)

            ln = Count()

            def rsqrt():
                ln.n += 1
                pool.wait_ge(var_ready, ln.n)
                pool.tensor_tensor(rstd[:], var_e[:], minus_half[0:P, 0:NT], ALU.pow).then_inc(rstd_ready, 1)

            def residual(name):
                pool.tensor_tensor(XB[:], X[:], row(name), ALU.add).then_inc(xb_ready, 1)

            rsqrt()
            pool.wait_ge(ld_rows, 16)
            residual("l0_br")
            rsqrt()
            rsqrt()
            pool.wait_ge(x_ready, 2)
            residual("l1_bout")
            pool.wait_ge(bn_v, 1)
            pool.tensor_tensor(v12[:, 0, :], v12[:, 0, :], minus_half[:], ALU.pow)
            pool.tensor_tensor(v12[:, 1, :], v12[:, 1, :], minus_half[:], ALU.pow).then_inc(bn_r, 1)
            rsqrt()
            pool.wait_ge(l1_x1, 1)
            pool.tensor_tensor(x1b[:], x1m[:], row("l1_b2"), ALU.add).then_inc(l1_x1b, 1)
            rsqrt()
            pool.wait_ge(l1_u, 1)
            pool.tensor_copy(total[:], u[:]).then_inc(l1_sum, 2)
            with pool.Fori(0, 3) as i:
                for b in range(2):
                    pool.wait_ge(l1_term, i * 2 + (b + 1))
                    pool.wait_ge(l1_sum, i * 2 + (b + 2))
                    pool.tensor_tensor(total[:], total[:], term[1 - b][:], ALU.add).then_inc(l1_sum, 1)
            rsqrt()
            rsqrt()
            pool.wait_ge(x_ready, 4)
            residual("l2_bout")
            rsqrt()
            pool.wait_ge(x_ready, 5)
            residual("l2_ffnb")
            rsqrt()
            pool.wait_ge(x_ready, 6)
            residual("l3_bout")
            for s_in, s_out, a in ((l3_qq, l3_nr, sm[4][:, 0:NT]), (l3_kn2, l3_knr, kcol[:, 0:KC])):
                pool.wait_ge(s_in, 1)
                pool.tensor_tensor(a, a, half[0:a.shape[0], 0:a.shape[1]], ALU.pow).then_inc(s_out, 1)
            pool.wait_ge(l3_gnn, 1)
            pool.tensor_tensor(XB[:], XB[:], gnn3, ALU.add).then_inc(xb_ready, 1)
            rsqrt()
            rsqrt()

        @block.scalar
        def _(act):
            f = Count(2)
            a = Count()

            def link(ins):
                ins.then_inc(a_step, 1)
                a.n += 1
                act.wait_ge(a_step, a.at())

            def full(halves=TH):
                act.wait_ge(f_full, f.at(1))
                return psF[:, f.slot, :, 0:halves]

            def free(ins):
                ins.then_inc(f_free, 1)
                f.n += 1

            def halves(v):
                return v.rearrange("p (a n) -> p a n", a=2)

            act.wait_ge(consts, 1)
            for m in range(NT):
                full()
                act.activation(A[:, m, 0:512], psF[0:P, f.slot, 0, :], ACT.Copy)
                free(act.activation(A[:, m, 512:N], psF[0:P, f.slot, 1, 0:N - 512], ACT.Copy))

            for m in range(NT):
                full()
                free(act.activation(AT[:, :, m * P:m * P + P], spread(psF, f.slot)[0:P, :, 0:P], ACT.Copy))

            act.wait_ge(l0_std, 1)
            act.activation(sm[1][:], sm[1][:], ACT.Sqrt, scale=1.0 / (HC - 1)).then_inc(l0_std_r, 1)

            def soft(n):
                act.wait_ge(logit_ready, n)
                act.activation(sm[1][:], sm[1][:], ACT.Exp).then_inc(exp_ready, 1)

            def item_layers(q, chunks, b1, affine=False):
                act.wait_ge(q.plan, 1)
                pairs = act.value_load(plan[0:1, 2 * PAIRS + 1:2 * PAIRS + 2], min_val=1, max_val=PAIRS)
                act.nop().then_inc(q.h_ready, 2)

                def expert(at):
                    return act.value_load(plan[0:1, at], min_val=0, max_val=E - 1)

                def x_to_sbuf(e):
                    for c in range(KC):
                        ps = psX[:, 0, c * S:c * S + S]
                        if affine:
                            ins = act.activation(x_item[:, c, :], ps, ACT.Identity, bias=col("l3_b")[:, bass.ds(e * KC + c, 1)],
                                                 scale=col("l3_g")[:, bass.ds(e * KC + c, 1)])
                        else:
                            ins = act.activation(x_item[:, c, :], ps, ACT.Copy)
                    ins.then_inc(q.x_ready, 1)

                e_next = expert(slice(0, 1))
                act.wait_ge(q.x_full, 1)
                x_to_sbuf(e_next)
                with act.Fori(0, pairs) as i:
                    for b in range(2):
                        e = expert(bass.ds(i * 2 + b, 1))
                        for k in range(chunks):
                            unit = b * (chunks // 4) + k // 4
                            if k % 4 == 0:
                                act.wait_ge(q.h_full, i * (chunks // 2) + (unit + 1))
                            ins = act.activation(h_item[:, k, :], psF[:, 0, unit % 2, (k % 4) * S:(k % 4) * S + S],
                                                 ACT.Gelu, bias=col(b1)[:, bass.ds(e * chunks + k, 1)])
                            if k % 4 == 3:
                                ins.then_inc(q.h_ready, 1)
                        act.wait_ge(q.hot_full, i * 2 + (b + 2))
                        act.activation(hot_out[:, 0:NT * P].rearrange("p (j n) -> p j n", n=P),
                                       spread(psF, 1)[:, :, 0:P], ACT.Copy).then_inc(q.hot_out, 1)
                        e_next = expert(bass.ds(i * 2 + (b + 1), 1))
                        act.wait_ge(q.x_full, i * 2 + (b + 2))
                        x_to_sbuf(e_next)

            soft(1)
            act.wait_ge(ld_cols, 32)
            item_layers(items[0], 4, "l0_b1")
            act.wait_ge(l1_pre, 1)
            act.activation(u[:], u_pre[:], ACT.Silu).then_inc(l1_u, 1)
            for c in range(KC):
                ps = full()
                act.activation(halves(q_pos[:, c, :]), ps, ACT.Relu)
                free(act.activation(halves(q_neg[:, c, :]), ps, ACT.Relu, scale=-1.0))
            act.wait_ge(f_free, f.n)
            act.activation(q_neg[:], q_neg[:], ACT.Exp, scale=-1.0).then_inc(l1_q, 1)
            act.wait_ge(l1_kmin, NT)
            act.activation(k_neg[:], k_neg[:], ACT.Exp).then_inc(l1_kexp, 1)
            for c in range(KC):
                ps = full()
                free(act.activation(halves(hT1[:, c, :]), ps, ACT.Gelu, bias=col("l1_mb1")[:, c:c + 1]))
            soft(2)
            act.wait_ge(bn_ready, 1)
            with act.Fori(0, E // 2) as i:
                f.enter(i, 8)
                for layer, s, o in ((0, s1, o1), (1, s2, o2)):
                    for b in range(2):
                        for c in range(KC):
                            ps = full()
                            at = bass.ds((i * 2 + b) * KC + c, 1)
                            free(act.activation(halves(hidden[b][:, layer * KC + c, :]), ps, ACT.Relu,
                                                bias=o[:, at], scale=s[:, at]))
                f.leave(E // 2)
            free(act.activation(halves(q2T), full(), ACT.Copy))
            free(act.activation(halves(k2T), full(), ACT.Copy))
            act.wait_ge(l2_kmax, 1)
            act.activation(kx2[:, 0:N], k2T[:, 0:N], ACT.Exp, bias=kcol[:, 0:1], accum_out=kcol[:, 1:2]).then_inc(l2_kexp, 1)
            for h in range(H8):
                ps = full()
                free(act.activation(halves(a_row[:, h, :]), ps[0:P], ACT.Copy))
            units = Count(2)
            with act.Fori(0, H8 // 2) as i:
                units.enter(i, 2 * NT)
                for b in range(2):
                    act.wait_ge(g_bias, i * 2 + (b + 1))
                    for m in range(NT):
                        s = units.slot
                        at = bass.ds(i * 2 + b, 1)
                        act.wait_ge(g_full, units.at(1))
                        act.activation(e1[s], zm[b][:, m, :], ACT.Exp, bias=gb1[:, at, m])
                        act.activation(e2[s], zm[b][:, m, :], ACT.Exp, bias=gb2[:, at, m], scale=0.2).then_inc(g_exp, 1)
                        units.n += 1
                units.leave(H8 // 2)
            act.wait_ge(l3_qk, 1)
            for t in range(NT):
                for w in range(2):
                    ins = act.activation(qk2[:, t, w * D:w * D + D], qk[:, t, w * D:w * D + D], ACT.Square,
                                         bias=sm[0][:, 2 * t + w:2 * t + w + 1],
                                         accum_out=sm[1][:, 2 * t + w:2 * t + w + 1])
            ins.then_inc(l3_sq, 1)
            for c in range(KC):
                ps = full()
                free(act.activation(halves(vT3[:, c, :]), ps, ACT.Identity, bias=col("l3_bv")[:, c:c + 1]))
            act.wait_ge(l3_qn, 1)
            for t in range(NT):
                ins = act.activation(qk[:, t, 0:D], qk2[:, t, 0:D], ACT.Square, accum_out=sm[4][:, t:t + 1])
            ins.then_inc(l3_qq, 1)
            act.activation(kk3[:], qk2[:, :, D:2 * D], ACT.Square).then_inc(l3_kk, 1)
            soft(3)
            item_layers(items[1], 8, "l3_b1", affine=True)

        @block.tensor
        def _(pe):
            f, t, xr = Count(2), Count(2), Count(2)

            def f_slot():
                if f.more is not None or f.n >= 2:
                    pe.wait_ge(f_free, f.at(-1))
                return psF[:, f.slot]

            def f_done(ins):
                ins.then_inc(f_full, 1)
                f.n += 1

            def t_slot():
                if t.more is not None or t.n >= 2:
                    pe.wait_ge(t_free, t.at(-1))
                return psT[:, t.slot]

            def t_done(ins):
                ins.then_inc(t_full, 1)
                t.n += 1

            def x_slot():
                if xr.n >= 2:
                    pe.wait_ge(x_free, xr.n - 1)
                return psX[:, xr.slot]

            def x_done(ins):
                ins.then_inc(x_full, 1)
                xr.n += 1

            def turn(a):
                for c in range(KC):
                    ps = x_slot()
                    for i in range(4):
                        ins = pe.transpose(ps[:, i * P:i * P + P], a[:, i, c * 128:c * 128 + 128], ident[0:P, 0:P])
                    x_done(ins)
                ps = x_slot()
                for c in range(KC):
                    ins = pe.transpose(ps[:, c * P:c * P + P], a[:, 4, c * 128:c * 128 + 128], ident[0:P, 0:P])
                x_done(ins)

            def turned():
                pe.wait_ge(x_free, xr.n)

            def rows_of(terms, n, at=0):
                for i in range(NT):
                    ps = t_slot()
                    pairs = terms(i)
                    for k, (lhsT, rhs) in enumerate(pairs):
                        ins = pe.matmul(ps[0:P, at:at + n], lhsT, rhs, start=k == 0, stop=k == len(pairs) - 1)
                    t_done(ins)

            def linear(actT, w, a=0, b=D, chunks=KC):
                return lambda i: [(actT[:, c, i * P:i * P + P], w[:, c, a:b]) for c in range(chunks)]

            def chunk_fm(ps, weight, actT, chunks):
                for c in range(chunks):
                    for h in range(2):
                        ins = pe.matmul(ps[:, h, 0:TH], weight(c), actT[:, c, h * TH:h * TH + TH],
                                        start=c == 0, stop=c == chunks - 1)
                return ins

            def router(n, w, plan_items=False):
                ps = t_slot()
                for i in range(NT):
                    for c in range(KC):
                        ins = pe.matmul(ps[0:P, i * E:i * E + E], XT[:, c, i * P:i * P + P], w[:, c, :],
                                        start=c == 0, stop=c == KC - 1)
                t_done(ins)
                pe.wait_ge(cw_ready, n + 1)
                if plan_items:
                    ps = x_slot()
                    pe.matmul(ps[:, 0:(NT + 1) * E], all_ones[:], choice_sum.rearrange("p t e -> p (t e)"), start=True, stop=False)
                    x_done(pe.matmul(ps[:, 0:(NT + 1) * E], earlier[:], chosen.rearrange("p t e -> p (t e)"), start=False, stop=True))
                for tiles in ((0, 1, 2, 3), (4,)):
                    ps = x_slot()
                    for i in tiles:
                        ins = pe.transpose(ps[0:E, (i % 4) * P:(i % 4) * P + P], CW[:, :, i], ident[0:P, 0:P])
                    x_done(ins)
                turned()
                rows_of(lambda i: [(CWT[:, i * P:i * P + P], w_eb2[:, n, :])], D)

            pe.wait_ge(consts, 1)
            pe.wait_ge(idx_f, 1)
            ps = x_slot()
            for w in range(2):
                for r in range(R):
                    pe.transpose(ps[0:P, (w * R + r) * G:(w * R + r) * G + G], idx_float[:, w, r * P:r * P + P], ident[0:G, 0:G])
            for w in range(2):
                ins = pe.transpose(ps[0:1, (2 * R + w) * G:(2 * R + w) * G + G], ends[:, w:w + 1], ident[0:G, 0:G])
            x_done(ins)
            pe.wait_ge(xn_ready, 1)
            turn(XN)
            pe.wait_ge(bounds_ready, 1)
            count = [pe.value_load(bounds_i[0:1, 1, m:m + 1], min_val=1, max_val=G) for m in range(NT)]
            before = [pe.value_load(bounds_i[0:1, 2, m:m + 1], min_val=0, max_val=G * NT) for m in range(NT)]
            for m in range(NT):
                ps = f_slot()
                for part, lo, hi in ((0, 0, 512), (1, 512, N)):
                    ins = pe.matmul(ps[0:P, part, 0:hi - lo], zeros[:, 0:P], zeros[:, 0:hi - lo],
                                    start=True, stop=False, skip_group_check=True)
                if m == 0:
                    ins.then_inc(hot_used, 2)
                with pe.Fori(0, count[m]) as j:
                    for r in range(R):
                        if r % 2 == 0:
                            pe.wait_ge(hot_ready, (before[m] + j) * 2 + (r // 2 + 1))
                        pe.matmul(ps[0:P, 0, :], hot_dst[:, r, 0:P], hot_src[:, r, 0:512],
                                  start=False, stop=False, skip_group_check=True)
                        ins = pe.matmul(ps[0:P, 1, 0:N - 512], hot_dst[:, r, 0:P], hot_src[:, r, 512:N],
                                        start=False, stop=False, skip_group_check=True)
                        if r % 2:
                            ins.then_inc(hot_used, 1)
                for part, lo, hi in ((0, 0, 512), (1, 512, N)):
                    ins = pe.matmul(ps[0:P, part, 0:hi - lo], zeros[:, 0:P], zeros[:, 0:hi - lo],
                                    start=False, stop=True, skip_group_check=True)
                f_done(ins)
            for m in range(NT):
                pe.wait_ge(f_free, m + 1)
                f_slot()
                ps = spread(psF, f.slot)
                for j in range(NT):
                    ins = pe.transpose(ps[0:P, j, 0:P], A[:, m, j * P:j * P + P], ident[0:P, 0:P])
                f_done(ins)
            pe.wait_ge(f_free, f.n)
            rows_of(lambda m: [(AT[:, j, m * P:m * P + P], XN[:, j, :]) for j in range(NT)], D + 1)
            pe.wait_ge(t_free, t.n)
            turn(ag)
            pe.wait_ge(l0_kv, 1)
            ps = t_slot()
            for c in range(KC):
                for i in range(NT):
                    ins = pe.matmul(ps[:, c * 128:c * 128 + 128], k0[:, i, c * 128:c * 128 + 128],
                                    v0[:, i, c * 128:c * 128 + 128], start=i == 0, stop=i == NT - 1)
            t_done(ins)
            turned()
            pe.wait_ge(ld_small[0], 16)
            pe.wait_ge(l0_w, 1)
            rows_of(lambda i: linear(agT, W("l0_wl"))(i) + linear(XT, wc)(i), D)

            def item_products(q, hid, chunks):
                pe.wait_ge(f_free, f.n)
                pe.wait_ge(t_free, t.n)
                pe.wait_ge(x_free, xr.n)
                pe.wait_ge(q.plan, 1)
                pairs = pe.value_load(plan[0:1, 2 * PAIRS + 1:2 * PAIRS + 2], min_val=1, max_val=PAIRS)
                pe.nop().then_inc(q.hot_full, 1)
                pe.nop().then_inc(q.y_full, 2)
                pe.wait_ge(q.split, 1)

                def gather(b):
                    for c in range(KC):
                        for part in (xn_high, xn_low):
                            for j in range(NT):
                                ins = pe.matmul(psX[:, 0, c * S:c * S + S], part[:, j, c * 128:c * 128 + 128], hot_in[b][:, j, :],
                                                start=part is xn_high and j == 0, stop=part is xn_low and j == NT - 1)
                    ins.then_inc(q.x_full, 1)

                pe.wait_ge(q.hot, 1)
                gather(0)
                with pe.Fori(0, pairs) as i:
                    for b in range(2):
                        w1 = w_ffn[:, b, 0:KC * hid].rearrange("p (c n) -> p c n", c=KC)
                        w2 = w_ffn[:, b, KC * hid:KC * hid + chunks * D].rearrange("p (k n) -> p k n", n=D)
                        units = chunks // 4
                        pe.wait_ge(q.weights[b], i * 16 + 16)
                        pe.wait_ge(q.x_ready, i * 2 + (b + 1))
                        for k in range(chunks):
                            unit = b * units + k // 4
                            if k % 4 == 0:
                                pe.wait_ge(q.h_ready, i * (2 * units) + (unit + 1))
                            for c in range(KC):
                                ins = pe.matmul(psF[:, 0, unit % 2, (k % 4) * S:(k % 4) * S + S], w1[:, c, k * 128:k * 128 + 128],
                                                x_item[:, c, :], start=c == 0, stop=c == KC - 1)
                            if k % 4 == 3:
                                ins.then_inc(q.h_full, 1)
                        for j in range(NT):
                            ins = pe.matmul(spread(psF, 1)[:, j, :], hot_in[b][:, j, :], ident_r[:], start=True, stop=True)
                        ins.then_inc(q.hot_full, 1)
                        for k in range(chunks):
                            if k % 4 == 0:
                                pe.wait_ge(q.h_ready, i * (2 * units) + (b * units + k // 4 + 3))
                            ins = pe.matmul(psX[:, 1, 0:D], h_item[:, k, :], w2[:, k, :], start=k == 0, stop=k == chunks - 1)
                        ins.then_inc(q.y_full, 1)
                        pe.wait_ge(q.hot, i * 2 + (b + 2))
                        gather(1 - b)
                        pe.wait_ge(q.hot_out, i * 2 + (b + 1))
                        pe.wait_ge(q.y_ready, i * 2 + (b + 1))
                        for j in range(NT):
                            unit = b * NT + j
                            pe.wait_ge(q.o_free, i * (2 * NT) + (unit + NT - 1))
                            for part in range(2):
                                ins = pe.matmul(psT[0:P, unit % 2, 0:D], hot_out[:, j * P:j * P + P], y_item[:, part, :],
                                                start=part == 0, stop=part == 1)
                            ins.then_inc(q.o_full, 1)
                pe.wait_ge(q.x_ready, pairs * 2 + 1)

            pe.wait_ge(xn_ready, 2)
            turn(XN)
            turned()
            pe.wait_ge(ld_cols, 32)
            router(0, W("l0_gate"), plan_items=True)
            item_products(items[0], 512, 4)
            pe.wait_ge(ld_small[1], 16)
            pe.wait_ge(xn_ready, 3)
            pe.nop().then_inc(ffn_used, 2)
            turn(XN)
            turned()
            rows_of(linear(XT, W("l1_win")), D)
            for c in range(KC):
                f_done(chunk_fm(f_slot(), lambda k: W("l1_qkv")[:, k, c * 128:c * 128 + 128], XT, KC))
            rows_of(linear(XT, W("l1_qkv"), D, 3 * D), 2 * D)
            pe.wait_ge(l1_k, 1)
            ps = t_slot()
            for c in range(KC):
                for rhs, at, n in ((v1m, c * 128, 128), (None, D + c, 1)):
                    for i in range(NT):
                        ins = pe.matmul(ps[:, at:at + n], k1[:, i, c * 128:c * 128 + 128],
                                        ones[0:P, 0:1] if rhs is None else rhs[:, i, c * 128:c * 128 + 128],
                                        start=i == 0, stop=i == NT - 1)
            t_done(ins)
            pe.wait_ge(l1_qT, 1)
            pe.wait_ge(l1_bd, 1)
            for i in range(NT):
                ps = t_slot()
                for c in range(KC):
                    ins = pe.matmul(ps[0:P, c * 132:c * 132 + 132], q_pos[:, c, i * P:i * P + P], bd[:, c, :],
                                    start=True, stop=True)
                t_done(ins)
            pe.wait_ge(l1_x1, 1)
            turn(x1m)
            turned()
            for c in range(KC):
                f_done(chunk_fm(f_slot(), lambda k: W("l1_w1")[:, k, c * 128:c * 128 + 128], x1T, KC))
            pe.wait_ge(f_free, f.n)
            rows_of(linear(hT1, W("l1_w2")), D)
            pe.wait_ge(l1_u, 1)
            with pe.Fori(0, 3) as i:
                t.enter(i, 2 * NT)
                for b in range(2):
                    pe.wait_ge(t_free, t.at())
                    rows_of(lambda m: [(AT[:, j, m * P:m * P + P], term[b][:, j, :]) for j in range(NT)], D)
                t.leave(3)
            pe.wait_ge(l1_sum, 8)
            turn(total)
            turned()
            rows_of(linear(totalT, W("l1_wout")), D)
            pe.wait_ge(xn_ready, 4)
            turn(XN)
            turned()
            router(1, W("l1_wr"))
            with pe.Fori(0, E // 2) as i:
                f.enter(i, 8)
                t.enter(i, 2 * NT)
                w = [w_ffn[:, b, 0:FFN1].rearrange("p (l c n) -> p l c n", l=3, c=KC) for b in range(2)]
                for layer in range(2):
                    for b in range(2):
                        if layer == 0:
                            pe.wait_ge(ld_ffn[b], i * 16 + 16)
                        else:
                            pe.wait_ge(f_free, f.at(-2))
                        src_fm = XT if layer == 0 else hidden[b][:, 0:KC, :]
                        for c in range(KC):
                            f_done(chunk_fm(f_slot(), lambda k: w[b][:, layer, k, c * 128:c * 128 + 128], src_fm, KC))
                for b in range(2):
                    pe.wait_ge(f_free, f.at(-2 + 2 * b))
                    rows_of(linear(hidden[b][:, KC:2 * KC, :], w[b][:, 2]), D)
                    pe.wait_ge(t_full, t.at())
                    pe.nop().then_inc(ffn_used, 1)
                f.leave(E // 2)
                t.leave(E // 2)
            pe.wait_ge(ld_small[2], 16)
            pe.wait_ge(xn_ready, 5)
            turn(XN)
            turned()
            rows_of(linear(XT, W("l2_w")), D)
            for w in range(2):
                f_done(chunk_fm(f_slot(), lambda k: W("l2_qkv")[:, k, w * 128:w * 128 + 128], XT, KC))
            for tiles in ((0, 1, 2, 3), (4,)):
                ps = t_slot()
                for i in tiles:
                    for c in range(KC):
                        ins = pe.matmul(ps[0:P, (i % 4) * 128:(i % 4) * 128 + 128], XT[:, c, i * P:i * P + P],
                                        W("l2_qkv")[:, c, 256:384], start=c == 0, stop=c == KC - 1)
                t_done(ins)
            pe.wait_ge(l2_ab, 1)
            for tiles in ((0, 1, 2, 3), (4,)):
                ps = x_slot()
                for i in tiles:
                    ins = pe.transpose(ps[0:H8, (i % 4) * P:(i % 4) * P + P], hsum[:, 0, i, :], ident[0:P, 0:P])
                x_done(ins)
            turned()
            for h in range(H8):
                ps = f_slot()
                for half_ in range(2):
                    ins = pe.matmul(ps[0:P, half_, 0:TH], pick[:, h, 0:P], asT[:, half_ * TH:half_ * TH + TH],
                                    start=True, stop=True)
                f_done(ins)
            pe.wait_ge(l2_kexp, 1)
            for tiles in ((0, 1, 2, 3), (4,)):
                ps = x_slot()
                for i in tiles:
                    ins = pe.transpose(ps[0:P, (i % 4) * 128:(i % 4) * 128 + 128], kx2[:, i * P:i * P + P], ident[:])
                x_done(ins)
            turned()
            ps = t_slot()
            for i in range(NT):
                ins = pe.matmul(ps[:, 0:128], v2m[:, i * 128:i * 128 + 128], k2m[:, i * 128:i * 128 + 128],
                                start=i == 0, stop=i == NT - 1)
            t_done(ins)
            pe.wait_ge(t_free, t.n)
            ps = t_slot()
            t_done(pe.matmul(ps[:, 0:D], ctT, W("l2_wout", 1)[:, 0, :], start=True, stop=True))
            pe.wait_ge(t_free, t.n)
            rows_of(lambda i: [(q2T[:, i * P:i * P + P], gw2)], D)
            pe.wait_ge(f_free, f.n)
            pe.nop().then_inc(g_full, 2)
            units = Count(2)

            def attend(b, m, ps):
                pe.wait_ge(g_free, units.at())
                s = (units.n - 1) % 2
                for j in range(NT):
                    ins = pe.matmul(ps[0:P, m * (HC + 1):(m + 1) * (HC + 1)], pT[s][:, j, :],
                                    he[:, j, bass.ds(gi * 2 + b, 1), :], start=j == 0, stop=j == NT - 1)
                return ins

            with pe.Fori(0, H8 // 2) as gi:
                units.enter(gi, 2 * NT)
                t.enter(gi, 2)
                ps_t = None
                for n in range(2 * NT):
                    b, m = n // NT, n % NT
                    s = units.slot
                    if m == 0:
                        if b:
                            t_done(attend(b - 1, NT - 1, ps_t))
                        ps_t = t_slot()
                    pe.wait_ge(g_e, units.at(1))
                    for j in range(NT):
                        ins = pe.transpose(spread(psF, s)[0:P, j, 0:P], e1[s][:, j * P:j * P + P], ident[0:P, 0:P])
                    ins.then_inc(g_full, 1)
                    if m:
                        attend(b, m - 1, ps_t)
                    units.n += 1
                t_done(attend(1, NT - 1, ps_t))
                units.leave(H8 // 2)
                t.leave(H8 // 2)
            pe.wait_ge(xn_ready, 6)
            turn(XN)
            turned()
            rows_of(linear(XT, W("l2_ffn")), D)
            pe.wait_ge(ld_small[3], 16)
            pe.wait_ge(xn_ready, 7)
            turn(XN)
            turned()
            rows_of(linear(XT, W("l3_qkv"), 0, 2 * D), 2 * D)
            rows_of(linear(XT, W("l3_w1")), D)
            rows_of(linear(XT, W("l3_qkv"), 2 * D, 3 * D), D)
            for c in range(KC):
                f_done(chunk_fm(f_slot(), lambda k: W("l3_qkv")[:, k, 2 * D + c * 128:2 * D + c * 128 + 128], XT, KC))
            pe.wait_ge(l3_y1, 1)
            rows_of(lambda m: [(A[:, j, m * P:m * P + P], y3[:, j, :]) for j in range(NT)] + linear(XT, W("l3_w0"))(m), D)
            pe.wait_ge(l3_kk, 1)
            ps = t_slot()
            for c in range(KC):
                for i in range(NT):
                    ins = pe.matmul(ps[:, c:c + 1], kk3[:, i, c * 128:c * 128 + 128], ones[0:P, 0:1],
                                    start=i == 0, stop=i == NT - 1)
            t_done(ins)
            ps = t_slot()
            for c in range(KC):
                for i in range(NT):
                    ins = pe.matmul(ps[:, c * D:c * D + D], v3[:, i, c * 128:c * 128 + 128], qk2[:, i, D:2 * D],
                                    start=i == 0, stop=i == NT - 1)
            t_done(ins)
            pe.wait_ge(t_free, t.n)
            ps = t_slot()
            for c in range(KC):
                for k in range(KC):
                    ins = pe.matmul(ps[:, c * D:c * D + D], kvT[:, k, c * 128:c * 128 + 128], W("l3_wout")[:, k, :],
                                    start=k == 0, stop=k == KC - 1)
            t_done(ins)
            pe.wait_ge(l3_q, 1)
            turn(qk2[:, :, 0:D])
            turned()
            pe.wait_ge(l3_gw, 1)
            pe.wait_ge(f_free, f.n)
            rows_of(lambda i: linear(vT3, W("l3_wout"))(i) + linear(qT3, gw3)(i), D)
            pe.wait_ge(xn_ready, 8)
            turn(XN)
            turned()
            router(2, W("l3_wr"), plan_items=True)
            item_products(items[1], 1024, 8)

        @block.vector
        def _(dve):
            t, xr, v, tf = Count(2), Count(2), Count(), Count()

            def V(ins):
                ins.then_inc(v_step, 1)
                v.n += 1
                return ins

            def settle():
                dve.wait_ge(v_step, v.at())

            def link(ins):
                V(ins)
                settle()

            def announce(what):
                settle()
                if t.n:
                    dve.wait_ge(t_free, t.n)
                dve.nop().then_inc(what, 1)

            def t_full_slot():
                dve.wait_ge(t_full, t.at(1))
                return psT[:, t.slot]

            def t_emptied(ins):
                ins.then_inc(t_free, 1)
                t.n += 1

            def t_settle():
                dve.wait_ge(t_free, t.n)

            def x_full_slot():
                dve.wait_ge(x_full, xr.n + 1)
                return psX[:, xr.slot]

            def x_emptied(ins):
                ins.then_inc(x_free, 1)
                xr.n += 1

            def turned_to(dst_fm):
                for c in range(KC):
                    ps = x_full_slot()
                    x_emptied(dve.tensor_copy(dst_fm[:, c, 0:4 * P], ps[:, 0:4 * P]))
                ps = x_full_slot()
                x_emptied(dve.tensor_copy(dst_fm[:, :, 4 * P:N], ps[:, 0:KC * P].rearrange("p (c n) -> p c n", c=KC)))

            norms = Count()

            def layer_norm(a, b, what=xn_ready):
                for i in range(NT):
                    V(dve.bn_stats(stats[:, i, :], a[:, i, 0:D]))
                settle()
                for i in range(NT):
                    V(dve.bn_aggr(mv[:, i, :], stats[:, i, :]))
                settle()
                dve.tensor_scalar(var_e[:], mv[:, :, 1], LN_EPS, None, ALU.add).then_inc(var_ready, 1)
                norms.n += 1
                dve.wait_ge(rstd_ready, norms.n)
                for i in range(NT):
                    ins = dve.tensor_scalar(b[:, i, 0:D], a[:, i, 0:D], mv[:, i, 0:1], rstd[:, i:i + 1],
                                            ALU.subtract, ALU.mult)
                    if what is None:
                        V(ins)
                    elif i == NT - 1:
                        ins.then_inc(what, 1)
                if what is None:
                    settle()

            def per_node(a):
                return a.unsqueeze(2).to_broadcast([P, NT, E])

            def router(n, bias, top2=False, shares=False):
                view = [s[:].rearrange("p (t e) -> p t e", e=E) for s in sm]
                ps = t_full_slot()
                t_emptied(dve.tensor_tensor(view[0], ps[0:P, 0:NT * E].rearrange("p (t e) -> p t e", e=E), row(bias), ALU.add))
                t_settle()
                link(dve.tensor_reduce(sm[2][:, 0:NT], view[0], AX.X, ALU.max))
                dve.tensor_tensor(view[1], view[0], per_node(sm[2][:, 0:NT]), ALU.subtract).then_inc(logit_ready, 1)
                dve.wait_ge(exp_ready, n)
                link(dve.tensor_reduce(sm[2][:, 0:NT], view[1], AX.X, ALU.add))
                link(dve.reciprocal(sm[2][:, 0:NT], sm[2][:, 0:NT]))
                link(dve.tensor_tensor(view[0], view[1], per_node(sm[2][:, 0:NT]), ALU.mult))
                if top2:
                    order3 = order[:].unsqueeze(1).to_broadcast([P, NT, E])
                    rest = view[0]
                    for first in (True, False):
                        pick_ = view[3 if first else 4]
                        link(dve.tensor_reduce(sm[2][:, 0:NT], rest, AX.X, ALU.max))
                        link(dve.tensor_tensor(view[5], rest, per_node(sm[2][:, 0:NT]), ALU.is_equal))
                        link(dve.tensor_tensor(view[5], view[5], order3, ALU.mult))
                        link(dve.tensor_reduce(sm[2][:, 0:NT], view[5], AX.X, ALU.max))
                        link(dve.tensor_tensor(pick_, view[5], per_node(sm[2][:, 0:NT]), ALU.is_equal))
                        if first:
                            rest = view[6]
                            link(dve.scalar_tensor_tensor(out=sm[6][:], in0=sm[3][:], scalar=-4.0, in1=sm[0][:],
                                                          op0=ALU.mult, op1=ALU.add))
                    link(dve.tensor_tensor(sm[3][:], sm[3][:], sm[4][:], ALU.add))
                    link(dve.tensor_tensor(sm[0][:], sm[0][:], sm[3][:], ALU.mult))
                    if shares:
                        link(dve.tensor_reduce(sm[2][:, 0:NT], view[0], AX.X, ALU.add))
                        link(dve.reciprocal(sm[2][:, 0:NT], sm[2][:, 0:NT]))
                        link(dve.tensor_tensor(view[0], view[0], per_node(sm[2][:, 0:NT]), ALU.mult))
                    V(dve.tensor_copy(chosen[:, 0:NT, :], view[3]))
                    V(dve.memset(chosen[:, NT, :], 0.0))
                    V(dve.memset(choice_sum[:, 0, :], 0.0))
                    link(dve.tensor_copy(choice_sum[:, 1, :], view[3][:, 0, :]))
                    for m in range(1, NT):
                        link(dve.tensor_tensor(choice_sum[:, m + 1, :], choice_sum[:, m, :], view[3][:, m, :], ALU.add))
                dve.tensor_copy(CW[:].rearrange("p e t -> p t e"), view[0]).then_inc(cw_ready, 1)
                if top2:
                    ps = x_full_slot()
                    V(dve.tensor_copy(n_chosen, ps[:, NT * E:(NT + 1) * E]))
                    x_emptied(dve.scalar_tensor_tensor(out=rank_p1, in0=ps[0:P, 0:NT * E].rearrange("p (t e) -> p t e", e=E),
                                                       scalar=1.0, in1=view[3], op0=ALU.add, op1=ALU.mult))
                for lo, n_ in ((0, 4 * P), (4 * P, P)):
                    ps = x_full_slot()
                    x_emptied(dve.tensor_copy(CWT[:, lo:lo + n_], ps[0:E, 0:n_]))
                for i in range(NT):
                    ps = t_full_slot()
                    t_emptied(dve.tensor_tensor(X[:, i, :], ps[0:P, 0:D], X[:, i, :], ALU.add))

            def across(a, n):
                return a.unsqueeze(2).to_broadcast([128, a.shape[1], n])

            def along(a, n):
                return a.unsqueeze(1).to_broadcast([128, n, a.shape[1]])

            def plan_items(q):
                count = 2 * PAIRS + 1
                dve.wait_ge(x_free, xr.n)
                settle()
                V(dve.tensor_scalar(rank.rearrange("p e t -> p t e"), rank_p1, -1.0, None, ALU.add))
                link(dve.tensor_tensor(by_tile, across(n_chosen, NT), along(tile_end[:], E), ALU.is_gt))
                link(dve.tensor_reduce(n_tiles, by_tile, AX.X, ALU.add))
                link(dve.tensor_tensor(by_expert, along(n_tiles, E), upto[:], ALU.mult))
                link(dve.tensor_reduce(e_end, by_expert, AX.X, ALU.add))
                V(dve.tensor_tensor(e_start, e_end, n_tiles, ALU.subtract))
                V(dve.tensor_scalar(by_pair, pair_no[:], e_end[:, E - 1:E], None, ALU.is_lt))
                link(dve.tensor_tensor(by_item, along(e_end, count), across(item_no[:], E), ALU.is_le))
                V(dve.tensor_reduce(item_e, by_item, AX.X, ALU.add))
                V(dve.tensor_reduce(n_pairs, by_pair, AX.X, ALU.add))
                link(dve.tensor_tensor(by_item2, along(e_start, count), across(item_no[:], E), ALU.is_le))
                V(dve.tensor_scalar(plan[:, 0:count], item_e[0:1, :], float(E - 1), None, ALU.min))
                V(dve.tensor_copy(plan[:, count:count + 1], n_pairs[0:1, :]))
                link(dve.tensor_tensor(by_item2, by_item2, along(e_start, count), ALU.mult))
                link(dve.tensor_reduce(item_start, by_item2, AX.X, ALU.max))
                link(dve.tensor_tensor(item_off, item_no[:], item_start, ALU.subtract))
                link(dve.tensor_scalar(item_off, item_off, float(S), None, ALU.mult))
                announce(q.plan)

            def split_rows(q, n):
                dve.wait_ge(xn_ready, n)
                link(dve.tensor_copy(xn_high, XN[:, :, 0:D]))
                dve.tensor_tensor(xn_low, XN[:, :, 0:D], xn_high, ALU.subtract).then_inc(q.split, 1)

            def add_items(q):
                pairs = dve.value_load(plan[0:1, 2 * PAIRS + 1:2 * PAIRS + 2], min_val=1, max_val=PAIRS)
                own = Count()

                def own_step(ins):
                    ins.then_inc(q.step, 1)
                    own.n += 1
                    dve.wait_ge(q.step, own.at())

                def fill_slots(b, e, at):
                    own_step(dve.tensor_scalar(rank_item[b].unsqueeze(1), rank[:, bass.ds(e, 1), :], item_off[0:P, at],
                                               None, ALU.subtract))
                    for j in range(NT):
                        ins = dve.tensor_scalar(hot_in[b][:, j, :], slot_no[:], rank_item[b][:, j:j + 1], None, ALU.is_equal)
                    ins.then_inc(q.hot, 1)

                def expert(at):
                    return dve.value_load(plan[0:1, at], min_val=0, max_val=E - 1)

                dve.nop().then_inc(q.o_free, NT)
                fill_slots(0, expert(slice(0, 1)), slice(0, 1))
                with dve.Fori(0, pairs) as i:
                    own.enter(i, 2 * 2)
                    for b in range(2):
                        e = expert(bass.ds(i * 2 + b, 1))
                        after = bass.ds(i * 2 + (b + 1), 1)
                        e_next = expert(after)
                        dve.wait_ge(q.hot_full, i * 2 + (b + 1))
                        fill_slots(1 - b, e_next, after)
                        dve.wait_ge(q.y_full, i * 2 + (b + 3))
                        own_step(dve.tensor_copy(y_item[:, 0, :], psX[:, 1, 0:D]))
                        dve.tensor_tensor(y_item[:, 1, :], psX[:, 1, 0:D], y_item[:, 0, :], ALU.subtract).then_inc(q.y_ready, 1)
                        for j in range(NT):
                            unit = b * NT + j
                            dve.wait_ge(q.o_full, i * (2 * NT) + (unit + 1))
                            dve.wait_ge(q.o_free, i * (2 * NT) + (unit + 1))
                            dve.scalar_tensor_tensor(out=X[:, j, :], in0=psT[0:P, unit % 2, 0:D], scalar=CW[:, bass.ds(e, 1), j],
                                                     in1=X[:, j, :], op0=ALU.mult, op1=ALU.add).then_inc(q.o_free, 1)
                dve.wait_ge(q.o_free, pairs * (2 * NT) + NT)

            def add_experts():
                with dve.Fori(0, E // 2) as i:
                    t.enter(i, 2 * NT)
                    for b in range(2):
                        for m in range(NT):
                            ps = t_full_slot()
                            dve.wait_ge(t_free, t.at(-NT + 1))
                            t_emptied(dve.scalar_tensor_tensor(out=X[:, m, :], in0=ps[0:P, 0:D],
                                                               scalar=CW[:, bass.ds(i * 2 + b, 1), m],
                                                               in1=X[:, m, :], op0=ALU.mult, op1=ALU.add))
                    t.leave(E // 2)

            def add_rows(a, b):
                for i in range(NT):
                    ps = t_full_slot()
                    t_emptied(dve.tensor_tensor(a[:, i, 0:D], ps[0:P, 0:D], b[:, i, :], ALU.add))

            dve.wait_ge(consts, 1)
            dve.wait_ge(ld_idx, 32)
            link(dve.tensor_copy(idx_float, idx[:]))
            link(dve.tensor_reduce(ends[:, 0:1], idx_float[:, 1, :], AX.X, ALU.min))
            dve.tensor_reduce(ends[:, 1:2], idx_float[:, 1, :], AX.X, ALU.max).then_inc(idx_f, 1)
            ps = x_full_slot()
            for w in range(2):
                V(dve.tensor_copy(idxT[:, w, 0:G, :].rearrange("p g r -> p r g"),
                                  ps[0:P, w * R * G:(w + 1) * R * G].rearrange("p (r g) -> p r g", g=G)))
            x_emptied(dve.tensor_copy(endsT[:].rearrange("p a g -> p (a g)"), ps[0:1, 2 * R * G:(2 * R + 2) * G]))
            dve.wait_ge(x_free, xr.n)
            high, low = (endsT[:, w, :].unsqueeze(1).to_broadcast([1, NT, G]) for w in (1, 0))
            held = span[:, :, 0, :]
            V(dve.tensor_tensor(held, high, tile_start[:], ALU.is_ge))
            link(dve.scalar_tensor_tensor(out=span[:, :, 1, :], in0=low, scalar=float(-P), in1=tile_start[:],
                                          op0=ALU.add, op1=ALU.is_lt))
            link(dve.tensor_tensor(held, held, span[:, :, 1, :], ALU.mult))
            link(dve.tensor_tensor(span[:, :, 1, :], held, group_no[:, 1, :].unsqueeze(1).to_broadcast([1, NT, G]), ALU.mult))
            link(dve.tensor_tensor(held, held, group_no[:, 0, :].unsqueeze(1).to_broadcast([1, NT, G]), ALU.mult))
            link(dve.tensor_reduce(bounds[:, 0, :], span[:, :, 0, :], AX.X, ALU.max))
            link(dve.tensor_scalar(bounds[:, 0, :], bounds[:, 0, :], -1.0, float(G), ALU.mult, ALU.add))
            link(dve.tensor_scalar(bounds[:, 0, :], bounds[:, 0, :], float(G - 1), None, ALU.min))
            link(dve.tensor_reduce(last[:], span[:, :, 1, :], AX.X, ALU.max))
            link(dve.tensor_tensor(bounds[:, 1, :], last[:], bounds[:, 0, :], ALU.subtract))
            link(dve.tensor_scalar(bounds[:, 1, :], bounds[:, 1, :], 1.0, None, ALU.max))
            link(dve.memset(bounds[:, 2, 0:1], 0.0))
            for m in range(1, NT):
                link(dve.tensor_tensor(bounds[:, 2, m:m + 1], bounds[:, 2, m - 1:m], bounds[:, 1, m - 1:m], ALU.add))
            dve.tensor_copy(bounds_i[:], bounds[:]).then_inc(bounds_ready, 1)

            dve.wait_ge(ld_x, 16)
            layer_norm(X, XN)
            turned_to(XT)
            dve.wait_ge(bounds_ready, 1)
            first = [dve.value_load(bounds_i[0:1, 0, m:m + 1], min_val=0, max_val=G - 1) for m in range(NT)]
            count = [dve.value_load(bounds_i[0:1, 1, m:m + 1], min_val=1, max_val=G) for m in range(NT)]
            before = [dve.value_load(bounds_i[0:1, 2, m:m + 1], min_val=0, max_val=G * NT) for m in range(NT)]
            for m in range(NT):
                with dve.Fori(0, count[m]) as j:
                    for r in range(R):
                        if r % 2 == 0:
                            dve.wait_ge(hot_used, (before[m] + j) * 2 + (r // 2 + 1))
                        dve.tensor_scalar(hot_src[:, r, :], iota[:], idxT[:, 0, bass.ds(first[m] + j, 1), r],
                                          None, ALU.is_equal)
                        ins = dve.tensor_scalar(hot_dst[:, r, 0:P], iota[:, m * P:m * P + P],
                                                idxT[:, 1, bass.ds(first[m] + j, 1), r], None, ALU.is_equal)
                        if r % 2:
                            ins.then_inc(hot_ready, 1)
            heads = [s[:].rearrange("p (t h) -> p t h", h=H8) for s in sm]

            def by_head(a):
                return a.rearrange("p t (h c) -> p t h c", c=HC)

            def per_head(a):
                return a.unsqueeze(3).to_broadcast([P, NT, H8, HC])

            dve.wait_ge(xn_ready, 1)
            link(dve.tensor_reduce(heads[0], by_head(XN[:, :, 0:D]), AX.X, ALU.add))
            link(dve.tensor_scalar(sm[0][:], sm[0][:], 1.0 / HC, None, ALU.mult))
            link(dve.tensor_tensor(by_head(y0[:]), by_head(XN[:, :, 0:D]), per_head(heads[0]), ALU.subtract))
            link(dve.tensor_tensor(sq0[:], y0[:], y0[:], ALU.mult))
            dve.tensor_reduce(heads[1], by_head(sq0[:]), AX.X, ALU.add).then_inc(l0_std, 1)
            dve.wait_ge(l0_std_r, 1)
            link(dve.tensor_scalar(sm[1][:], sm[1][:], 1e-5, None, ALU.add))
            link(dve.reciprocal(sm[1][:], sm[1][:]))
            link(dve.tensor_tensor(by_head(y0[:]), by_head(y0[:]), per_head(heads[1]), ALU.mult))
            dve.wait_ge(ld_rows, 16)
            V(dve.tensor_tensor(k0[:], y0[:], row("l0_kw"), ALU.mult))
            link(dve.tensor_tensor(v0[:], y0[:], row("l0_vw"), ALU.mult))
            link(dve.tensor_tensor(k0[:], k0[:], row("l0_kb"), ALU.add))
            dve.tensor_tensor(v0[:], v0[:], row("l0_vb"), ALU.add).then_inc(l0_kv, 1)
            for m in range(NT):
                ps = t_full_slot()
                link(dve.tensor_scalar(inv_deg[:, m:m + 1], ps[0:P, D:D + 1], 1.0, None, ALU.max))
                link(dve.reciprocal(inv_deg[:, m:m + 1], inv_deg[:, m:m + 1]))
                t_emptied(dve.tensor_scalar(ag[:, m, :], ps[0:P, 0:D], inv_deg[:, m:m + 1], None, ALU.mult))
            for k in range(6):
                V(dve.tensor_scalar(inv_deg_k[:, k, :], inv_deg[:], 1.0 / (k + 1), None, ALU.mult))
            turned_to(agT)
            ps = t_full_slot()
            dve.wait_ge(ld_small[0], 16)
            link(dve.tensor_copy(wc[:], W("l0_wr")))
            for c in range(KC):
                at = wc[:, c, c * 128:c * 128 + 128]
                link(dve.tensor_tensor(at, at, ident[:], ALU.add))
                ins = dve.scalar_tensor_tensor(out=kv0[:, c, :], in0=ps[:, c * 128:c * 128 + 128], scalar=1.0 / N,
                                               in1=headmask[:], op0=ALU.mult, op1=ALU.mult)
                V(ins) if c == 0 else t_emptied(ins)
            settle()
            t_settle()
            for c in range(KC):
                at = wc[:, c, c * 128:c * 128 + 128]
                ins = dve.tensor_tensor(at, at, kv0[:, c, :], ALU.add)
            ins.then_inc(l0_w, 1)
            dve.wait_ge(xb_ready, 1)
            add_rows(X, XB)
            announce(x_ready)
            layer_norm(X, XN)
            turned_to(XT)
            router(1, "l0_gb", top2=True)
            plan_items(items[0])
            split_rows(items[0], 2)
            add_items(items[0])
            announce(x_ready)
            layer_norm(X, XN)
            turned_to(XT)
            dve.wait_ge(ld_cols, 32)
            V(dve.tensor_scalar(v12[:, 0, :], col("v1"), 1e-3, None, ALU.add))
            V(dve.tensor_scalar(v12[:, 1, :], col("v2"), 1e-3, None, ALU.add))
            announce(bn_v)
            add_rows(u_pre, row("l1_bin"))
            announce(l1_pre)
            for i in range(NT):
                ps = t_full_slot()
                dve.tensor_scalar(k_neg[:, i, :], ps[0:P, 0:D], 0.0, None, ALU.min).then_inc(l1_kmin, 1)
                V(dve.tensor_scalar(k1[:, i, :], ps[0:P, 0:D], 0.0, None, ALU.max))
                t_emptied(dve.tensor_copy(v1m[:, i, :], ps[0:P, D:2 * D]))
            settle()
            dve.wait_ge(l1_kexp, 1)
            dve.tensor_tensor(k1[:], k1[:], k_neg[:], ALU.add).then_inc(l1_k, 1)
            dve.wait_ge(l1_q, 1)
            dve.tensor_tensor(q_pos[:], q_pos[:], q_neg[:], ALU.add).then_inc(l1_qT, 1)
            ps = t_full_slot()
            for c in range(KC):
                V(dve.tensor_scalar(bd[:, c, 128:132], headcols[:], ps[:, D + c:D + c + 1], None, ALU.mult))
                ins = dve.tensor_tensor(bd[:, c, 0:128], ps[:, c * 128:c * 128 + 128], headmask[:], ALU.mult)
                V(ins) if c == 0 else t_emptied(ins)
            announce(l1_bd)
            for i in range(NT):
                ps = t_full_slot()
                p3 = ps[0:P, 0:KC * 132].rearrange("p (c n) -> p c n", c=KC)
                z = sm[i][:, 0:8].rearrange("p (c h) -> p c h", c=KC)
                link(dve.tensor_scalar(z, p3[:, :, 128:132], 1e-6, None, ALU.add))
                link(dve.reciprocal(sm[i][:, 0:8], sm[i][:, 0:8]))
                for c in range(KC):
                    ins = dve.tensor_tensor(mix[:, i, c * 128:c * 128 + 128].rearrange("p (h e) -> p h e", e=HC),
                                            p3[:, c, 0:128].rearrange("p (h e) -> p h e", e=HC),
                                            z[:, c, :].unsqueeze(2).to_broadcast([P, 4, HC]), ALU.mult)
                    V(ins) if c == 0 else t_emptied(ins)
            t_settle()
            settle()
            link(dve.tensor_tensor(mix[:], mix[:], XN[:, :, 0:D], ALU.add))
            layer_norm(mix, x1m, None)
            link(dve.tensor_tensor(x1m[:], x1m[:], row("l1_g1"), ALU.mult))
            dve.tensor_tensor(x1m[:], x1m[:], row("l1_b1"), ALU.add).then_inc(l1_x1, 1)
            V(dve.memset(x1T[:, :, N:TP], 0.0))
            turned_to(x1T)
            dve.wait_ge(bn_r, 1)
            for w, s, o in ((0, s1, o1), (1, s2, o2)):
                V(dve.tensor_tensor(s[:], v12[:, w, :], col(f"g{w + 1}"), ALU.mult))
                link(dve.tensor_tensor(o[:], col(f"b{w + 1}"), col(f"m{w + 1}"), ALU.subtract))
                link(dve.tensor_tensor(o[:], o[:], s[:], ALU.mult))
                link(dve.tensor_tensor(o[:], o[:], col(f"be{w + 1}"), ALU.add))
            announce(bn_ready)
            dve.wait_ge(l1_x1b, 1)
            add_rows(mix, x1b)
            t_settle()
            layer_norm(mix, mix, None)
            link(dve.tensor_tensor(mix[:], mix[:], row("l1_g2"), ALU.mult))
            link(dve.tensor_tensor(mix[:], mix[:], row("l1_be2"), ALU.add))
            dve.wait_ge(xb_ready, 2)
            link(dve.tensor_tensor(XB[:], XB[:], mix[:], ALU.add))
            with dve.Fori(0, 3) as i:
                t.enter(i, 2 * NT)
                for b in range(2):
                    for m in range(NT):
                        ps = t_full_slot()
                        if m == 0:
                            dve.wait_ge(l1_sum, i * 2 + (b + 1))
                        ins = dve.tensor_scalar(term[1 - b][:, m, :], ps[0:P, 0:D],
                                                inv_deg_k[:, bass.ds(i * 2 + b, 1), m], None, ALU.mult)
                        t_emptied(ins)
                    dve.wait_ge(t_free, t.at())
                    dve.nop().then_inc(l1_term, 1)
                t.leave(3)
            turned_to(totalT)
            add_rows(X, XB)
            announce(x_ready)
            layer_norm(X, XN)
            turned_to(XT)
            router(2, "l1_br")
            add_experts()
            announce(x_ready)
            layer_norm(X, XN)
            turned_to(XT)
            for i in range(NT):
                ps = t_full_slot()
                t_emptied(dve.tensor_copy(he[:, i, :, 0:HC], ps[0:P, 0:D].rearrange("p (h c) -> p h c", c=HC)))
            t_settle()
            for w, name in ((0, "l2_as"), (1, "l2_ad")):
                a, b = ROWS[name]
                for i in range(NT):
                    V(dve.tensor_tensor(hm[:, i, :].rearrange("p (h c) -> p h c", c=HC), he[:, i, :, 0:HC],
                                        w_rows[:, a:b].rearrange("p (h c) -> p h c", c=HC), ALU.mult))
                settle()
                V(dve.tensor_reduce(hsum[:, w], by_head(hm[:]), AX.X, ALU.add))
                settle()
            announce(l2_ab)
            for tiles, lo in (((0, 1, 2, 3), 0), ((4,), 512)):
                ps = t_full_slot()
                t_emptied(dve.tensor_copy(v2m[:, lo:lo + len(tiles) * 128], ps[0:P, 0:len(tiles) * 128]))
            for lo, n_ in ((0, 4 * P), (4 * P, P)):
                ps = x_full_slot()
                x_emptied(dve.tensor_copy(asT[:, lo:lo + n_], ps[0:H8, 0:n_]))
            dve.wait_ge(f_free, F_K2)
            link(dve.tensor_reduce(kcol[:, 2:3], k2T[:, 0:N], AX.X, ALU.max))
            dve.tensor_scalar(kcol[:, 0:1], kcol[:, 2:3], -1.0, None, ALU.mult).then_inc(l2_kmax, 1)
            for tiles, lo in (((0, 1, 2, 3), 0), ((4,), 512)):
                ps = x_full_slot()
                x_emptied(dve.tensor_copy(k2m[:, lo:lo + len(tiles) * 128], ps[0:P, 0:len(tiles) * 128]))
            ps = t_full_slot()
            t_emptied(dve.tensor_tensor(ctT, ps[:, 0:128], headmask[:], ALU.mult))
            link(dve.reciprocal(kcol[:, 3:4], kcol[:, 1:2]))
            ps = t_full_slot()
            t_emptied(dve.tensor_scalar(gw2, ps[:, 0:D], kcol[:, 3:4], HC ** -0.5, ALU.mult, ALU.mult))
            dve.wait_ge(xb_ready, 3)
            add_rows(XB, XB)
            t_settle()
            for m in range(NT):
                V(dve.tensor_scalar(no_edge[:, m, :], A[:, m, :], 0.0, NO_EDGE, ALU.is_equal, ALU.mult))
            settle()
            dve.wait_ge(f_free, F_K2 + H8)
            units = Count(2)

            def head_row(h):
                V(dve.tensor_copy(a_now[:], a_row[:, h, 0:N].rearrange("p a n -> p (a n)")))

            def masked(b, m):
                V(dve.tensor_tensor_reduce(out=zm[b][:, m, :], in0=a_now[:], in1=no_edge[:, m, :],
                                           scale=1.0, scalar=-3e38, op0=ALU.add, op1=ALU.max,
                                           accum_out=mx[:, m:m + 1]))

            def biases(h):
                adh, zh, gh, b1h, b2h = (y[:, h, :].rearrange("p a n -> p (a n)") for y in (ad_h, z2, gm, gb1, gb2))
                settle()
                link(dve.tensor_tensor(zh, mx[:], adh, ALU.add))
                link(dve.scalar_tensor_tensor(out=gh, in0=zh, scalar=0.2, in1=zh, op0=ALU.mult, op1=ALU.max))
                link(dve.tensor_tensor(b1h, adh, gh, ALU.subtract))
                dve.scalar_tensor_tensor(out=b2h, in0=adh, scalar=0.2, in1=gh, op0=ALU.mult, op1=ALU.subtract)\
                   .then_inc(g_bias, 1)

            def to_sbuf(m, back):
                s = (units.n - back) % 2
                dve.wait_ge(g_full, units.at(3 - back))
                dve.tensor_tensor(pT[s][:], spread(psF, s)[0:P, :, 0:P], AT[:, :, m * P:m * P + P], ALU.mult)\
                   .then_inc(g_free, 1)

            def head(h, b, following):
                if following is not None:
                    head_row(following)
                for m in range(NT):
                    s = units.slot
                    settle()
                    dve.wait_ge(g_exp, units.at(1))
                    dve.tensor_tensor(e1[s], e1[s], e2[s], ALU.max).then_inc(g_e, 1)
                    if following is not None:
                        masked(1 - b, m)
                    if m:
                        to_sbuf(m - 1, 1)
                    units.n += 1
                if following is not None:
                    biases(following)
                to_sbuf(NT - 1, 1)
                ps = t_full_slot()
                p3 = ps[0:P, 0:NT * (HC + 1)].rearrange("p (m n) -> p m n", m=NT)
                link(dve.tensor_scalar(den[:], p3[:, :, HC], 1e-16, None, ALU.add))
                link(dve.reciprocal(den[:], den[:]))
                t_emptied(dve.tensor_tensor(ACC[:].rearrange("p t (h c) -> p t h c", c=HC)[:, :, h, :].rearrange("p t a c -> p t (a c)"),
                                            p3[:, :, 0:HC], den[:].unsqueeze(2).to_broadcast([P, NT, HC]), ALU.mult))

            head_row(bass.ds(0, 1))
            settle()
            for m in range(NT):
                masked(0, m)
            biases(bass.ds(0, 1))
            with dve.Fori(0, H8 // 2 - 1) as i:
                t.enter(i, 2)
                v.enter(i, 2 * (NT + 6))
                units.enter(i, 2 * NT)
                for b in range(2):
                    head(bass.ds(i * 2 + b, 1), b, bass.ds(i * 2 + b + 1, 1))
                units.leave(H8 // 2 - 1)
                v.leave(H8 // 2 - 1)
                t.leave(H8 // 2 - 1)
            head(bass.ds(H8 - 2, 1), 0, bass.ds(H8 - 1, 1))
            head(bass.ds(H8 - 1, 1), 1, None)
            t_settle()
            link(dve.tensor_tensor(ACC[:], ACC[:], row("l2_bias"), ALU.add))
            link(dve.tensor_scalar(ACC[:], ACC[:], 0.0, None, ALU.max))
            dve.tensor_tensor(X[:], XB[:], ACC[:], ALU.add).then_inc(x_ready, 1)
            dve.wait_ge(x_ready, 5)
            layer_norm(X, XN)
            turned_to(XT)
            dve.wait_ge(xb_ready, 4)
            add_rows(X, XB)
            announce(x_ready)
            layer_norm(X, XN)
            turned_to(XT)
            a, b = ROWS["l3_bqk"]
            for i in range(NT):
                ps = t_full_slot()
                t_emptied(dve.tensor_tensor(qk[:, i, :], ps[0:P, :], w_rows[:, a:b], ALU.add))
            t_settle()
            link(dve.tensor_reduce(sm[0][:, 0:2 * NT], qk[:].rearrange("p t (w n) -> p (t w) n", n=D), AX.X, ALU.add))
            dve.tensor_scalar(sm[0][:, 0:2 * NT], sm[0][:, 0:2 * NT], -1.0 / D, None, ALU.mult).then_inc(l3_qk, 1)
            for i in range(NT):
                ps = t_full_slot()
                t_emptied(dve.tensor_copy(y3[:, i, :], ps[0:P, 0:D]))
            announce(l3_y1)
            add_rows(v3, row("l3_bv"))
            dve.wait_ge(l3_sq, 1)
            link(dve.tensor_scalar(sm[1][:, 0:2 * NT], sm[1][:, 0:2 * NT], 1e-7, None, ALU.add))
            link(dve.reciprocal(sm[1][:, 0:2 * NT], sm[1][:, 0:2 * NT]))
            for i in range(NT):
                for w in range(2):
                    V(dve.tensor_scalar(qk2[:, i, w * D:w * D + D], qk2[:, i, w * D:w * D + D],
                                        sm[1][:, 2 * i + w:2 * i + w + 1], None, ALU.mult))
            announce(l3_qn)
            for i in range(NT):
                ps = t_full_slot()
                t_emptied(dve.tensor_scalar(gnn3[:, i, :], ps[0:P, 0:D], 0.0, None, ALU.max))
            announce(l3_gnn)
            dve.wait_ge(l3_nr, 1)
            link(dve.tensor_scalar(sm[4][:, 0:NT], sm[4][:, 0:NT], 1e-12, None, ALU.max))
            link(dve.reciprocal(sm[4][:, 0:NT], sm[4][:, 0:NT]))
            for i in range(NT):
                ins = dve.tensor_scalar(qk2[:, i, 0:D], qk2[:, i, 0:D], sm[4][:, i:i + 1], None, ALU.mult)
            ins.then_inc(l3_q, 1)
            ps = t_full_slot()
            t_emptied(dve.tensor_copy(kcol[:, 0:KC], ps[:, 0:KC]))
            announce(l3_kn2)
            ps = t_full_slot()
            t_emptied(dve.tensor_copy(kvT[:].rearrange("p c n -> p (c n)"), ps[:]))
            dve.wait_ge(l3_knr, 1)
            link(dve.tensor_scalar(kcol[:, 0:KC], kcol[:, 0:KC], 1e-12, None, ALU.max))
            link(dve.reciprocal(kcol[:, 0:KC], kcol[:, 0:KC]))
            ps = t_full_slot()
            V(dve.tensor_scalar(gw3[:, 0, :], ps[:, 0:D], kcol[:, 0:1], N ** -0.5, ALU.mult, ALU.mult))
            t_emptied(dve.tensor_scalar(gw3[:, 1, :], ps[:, D:2 * D], kcol[:, 1:2], N ** -0.5, ALU.mult, ALU.mult))
            announce(l3_gw)
            turned_to(qT3)
            dve.wait_ge(xb_ready, 6)
            add_rows(X, XB)
            announce(x_ready)
            layer_norm(X, XN)
            turned_to(XT)
            router(3, "l3_br", top2=True, shares=True)
            plan_items(items[1])
            t_settle()
            layer_norm(XN, XN)
            split_rows(items[1], 9)
            add_items(items[1])
            announce(x_ready)


_INPUTS = ["x", "src", "dst"]


def kernel(**inputs):
    import numpy as _np
    import concourse.bacc as _bacc
    from concourse import mybir as _mybir
    from concourse.bass_utils import run_bass_kernel_spmd as _run

    a = {k: _np.asarray(v) for k, v in inputs.items()}

    def chunks(w):
        return w.reshape(-1, 128, w.shape[-1]).transpose(1, 0, 2).reshape(128, -1)

    def packed(table, parts):
        assert list(parts) == [n for n in table if n != "end"]
        return _np.ascontiguousarray(_np.concatenate(list(parts.values()), axis=-1))

    def columns(v):
        return v.reshape(-1, 128).T

    small = packed(SMALL, {
        "l0_wl": chunks(a["L0_gnn_W_l"].T), "l0_wr": chunks(a["L0_gnn_W_r"].T), "l0_gate": chunks(a["L0_ffn_gate_w"]),
        "l1_win": chunks(a["L1_gnn_W_in"].T), "l1_qkv": chunks(a["L1_mix_Wqkv"].T), "l1_w1": chunks(a["L1_mix_W1"].T),
        "l1_w2": chunks(a["L1_mix_W2"].T), "l1_wout": chunks(a["L1_gnn_W_out"].T), "l1_wr": chunks(a["L1_ffn_Wr"]),
        "l2_w": chunks(a["L2_gnn_W"].reshape(D, D)), "l2_qkv": chunks(a["L2_mix_W_qkv"]),
        "l2_wout": chunks(a["L2_mix_W_out"]), "l2_ffn": chunks(a["L2_ffn_weight"].T),
        "l3_w0": chunks(a["L3_gnn_w0"]), "l3_w1": chunks(a["L3_gnn_w1"]), "l3_qkv": chunks(a["L3_mix_W_qkv"]),
        "l3_wout": chunks(a["L3_mix_W_out"]), "l3_wr": chunks(a["L3_ffn_Wr"])})
    bqkv = a["L3_mix_b_qkv"]
    rows = packed(ROWS, {
        "l0_br": a["L0_gnn_b_r"], "l0_kw": a["L0_mix_kln_weight"].reshape(-1), "l0_kb": a["L0_mix_kln_bias"].reshape(-1),
        "l0_vw": a["L0_mix_vln_weight"].reshape(-1), "l0_vb": a["L0_mix_vln_bias"].reshape(-1),
        "l0_gb": a["L0_ffn_gate_b"], "l1_bin": a["L1_gnn_b_in"], "l1_bout": a["L1_gnn_b_out"],
        "l1_g1": a["L1_mix_ln1_g"], "l1_b1": a["L1_mix_ln1_b"], "l1_b2": a["L1_mix_b2"], "l1_g2": a["L1_mix_ln2_g"],
        "l1_be2": a["L1_mix_ln2_b"], "l1_br": a["L1_ffn_br"], "l2_as": a["L2_gnn_att_src"].reshape(-1),
        "l2_ad": a["L2_gnn_att_dst"].reshape(-1), "l2_bias": a["L2_gnn_bias"], "l2_bout": a["L2_mix_b_out"],
        "l2_ffnb": a["L2_ffn_bias"], "l3_bqk": bqkv[:2 * D], "l3_bv": bqkv[2 * D:], "l3_bout": a["L3_mix_b_out"],
        "l3_br": a["L3_ffn_br"]})
    cols = packed(COLS, {
        "l0_b1": columns(a["L0_ffn_b1"]), "l1_mb1": columns(a["L1_mix_b1"]),
        "b1": columns(a["L1_ffn_b1"]), "g1": columns(a["L1_ffn_g1"]), "be1": columns(a["L1_ffn_be1"]),
        "m1": columns(a["L1_ffn_m1"]), "v1": columns(a["L1_ffn_v1"]),
        "b2": columns(a["L1_ffn_b2"]), "g2": columns(a["L1_ffn_g2"]), "be2": columns(a["L1_ffn_be2"]),
        "m2": columns(a["L1_ffn_m2"]), "v2": columns(a["L1_ffn_v2"]), "l3_bv": columns(bqkv[2 * D:]),
        "l3_g": columns(a["L3_ffn_ln_g"]), "l3_b": columns(a["L3_ffn_ln_b"]), "l3_b1": columns(a["L3_ffn_b1"])})
    eb2 = _np.ascontiguousarray(_np.stack([a["L0_ffn_b2"], a["L1_ffn_bo"], a["L3_ffn_b2"]], axis=1))

    def experts(*layers):
        return _np.ascontiguousarray(_np.stack([_np.concatenate([chunks(w[e]) for w in layers], axis=1) for e in range(E)]))

    arrays = {"x": a["x"], "src": a["src"], "dst": a["dst"], "small": small, "rows": rows, "cols": cols, "eb2": eb2,
              "ffn0": experts(a["L0_ffn_W1"], a["L0_ffn_W2"]),
              "ffn1": experts(a["L1_ffn_W1"], a["L1_ffn_W2"], a["L1_ffn_Wo"]),
              "ffn3": experts(a["L3_ffn_W1"], a["L3_ffn_W2"])}
    arrays = {f"in_{k}": _np.ascontiguousarray(v) for k, v in arrays.items()}
    nc = _bacc.Bacc("TRN2", target_bir_lowering=False, num_devices=1)
    args = [nc.dram_tensor(k, v.shape, _mybir.dt.from_np(v.dtype), kind="ExternalInput").ap() for k, v in arrays.items()]
    args.append(nc.dram_tensor("out_x", (N, D), F32, kind="ExternalOutput").ap())
    gps_network(nc, *args)
    r = _run(nc, [arrays], core_ids=[0])
    return r.results[0]["out_x"]
```

```python
from contextlib import ExitStack

import numpy as np

import concourse.bass as bass
from concourse import mybir

F32 = mybir.dt.float32
BF16 = mybir.dt.bfloat16
F16 = mybir.dt.float16
F32R = mybir.dt.float32r
I32 = mybir.dt.int32
ALU = mybir.AluOpType
ACT = mybir.ActivationFunctionType
AX = mybir.AxisListType

N = 625
D = 256
P = 125
NT = N // P
KC = D // 128
TP = 628
TH = TP // 2
E = 8
NE = 20000
V_TILES, G_TILES = (3, 4), (0, 1, 2)
TILES = (3, 0, 4, 1, 2)
G, R = 40, 4
H8, HC = 8, 32
S = 128
ITEMS = (2 * N + E * (S - 1)) // S
PAIRS = (ITEMS + 1) // 2
LN_EPS = 1e-5
NO_EDGE = -1e30

SMALL = {}
ROWS = {}
COLS = {}


def _place(table, parts):
    at = 0
    for name, n in parts:
        table[name] = (at, at + n)
        at += n
    table["end"] = at


SMALL_L0 = [("l0_wl", KC * D), ("l0_wr", KC * D), ("l0_gate", KC * E)]
SMALL_L1 = [("l1_win", KC * D), ("l1_qkv", KC * 3 * D), ("l1_w1", KC * D), ("l1_w2", KC * D),
            ("l1_wout", KC * D), ("l1_wr", KC * E)]
SMALL_L2 = [("l2_w", KC * D), ("l2_qkv", KC * 384), ("l2_wout", D), ("l2_ffn", KC * D)]
SMALL_L3 = [("l3_w0", KC * D), ("l3_w1", KC * D), ("l3_qkv", KC * 3 * D), ("l3_wout", KC * D), ("l3_wr", KC * E)]
_place(SMALL, SMALL_L0 + SMALL_L1 + SMALL_L2 + SMALL_L3)
_place(ROWS, [("l0_br", D), ("l0_kw", D), ("l0_kb", D), ("l0_vw", D), ("l0_vb", D), ("l0_gb", E),
              ("l1_bin", D), ("l1_bout", D), ("l1_g1", D), ("l1_b1", D), ("l1_b2", D), ("l1_g2", D),
              ("l1_be2", D), ("l1_br", E), ("l2_as", D), ("l2_ad", D), ("l2_bias", D), ("l2_bout", D),
              ("l2_ffnb", D), ("l3_bqk", 2 * D), ("l3_bv", D), ("l3_bout", D), ("l3_br", E)])
_place(COLS, [("l0_b1", E * 4), ("l1_mb1", KC), ("b1", 16), ("g1", 16), ("be1", 16), ("m1", 16), ("v1", 16),
              ("b2", 16), ("g2", 16), ("be2", 16), ("m2", 16), ("v2", 16), ("l3_bv", KC),
              ("l3_g", 16), ("l3_b", 16), ("l3_b1", E * 8)])
FFN0, FFN1, FFN3 = KC * 512 + 4 * D, 6 * D, KC * 1024 + 8 * D


class Count:

    def __init__(self, slots=1):
        self.n, self.more, self.slots = 0, None, slots

    def at(self, d=0):
        return self.n + d if self.more is None else self.more + (self.n + d)

    @property
    def slot(self):
        return self.n % self.slots

    def enter(self, i, per):
        assert per % self.slots == 0
        self.first, self.per, self.more = self.n, per, i * per

    def leave(self, times):
        assert self.n - self.first == self.per, (self.n - self.first, self.per)
        self.n, self.more = self.first + times * self.per, None


def gps_network(nc, x, src, dst, small, rows, cols, eb2, ffn0, ffn1, ffn3, out):
    with ExitStack() as ctx:
        def sb(name, shape, dt=F32):
            return ctx.enter_context(nc.sbuf_tensor(name, shape, dt))

        def sem(name):
            return ctx.enter_context(nc.semaphore(name))

        def next_at():
            return -(-nc.sbuf_base // 32) * 32

        w_small = sb("w_small", [128, SMALL["end"]])
        w_rows = sb("w_rows", [P, ROWS["end"]])
        w_cols = sb("w_cols", [128, COLS["end"]])
        w_eb2 = sb("w_eb2", [E, 3, D])
        w_ffn = sb("w_ffn", [128, 2, FFN3])

        def W(name, k=KC):
            a, b = SMALL[name]
            return w_small[:, a:b].rearrange("p (c n) -> p c n", c=k)

        def row(name, tiles=NT):
            a, b = ROWS[name]
            return w_rows[:, a:b].unsqueeze(1).to_broadcast([P, tiles, b - a])

        def col(name):
            a, b = COLS[name]
            return w_cols[:, a:b]

        ident = sb("ident", [128, 128])
        headmask = sb("headmask", [128, 128])
        headcols = sb("headcols", [128, 4])
        pick = sb("pick", [E, H8, 128])
        ones = sb("ones", [128, 2])
        order = sb("order", [P, E])
        minus_half, half = sb("minus_half", [128, 16]), sb("half", [128, 16])
        group_no = sb("group_no", [1, 2, G])
        tile_start = sb("tile_start", [1, NT, G])

        earlier = sb("earlier", [P, S])
        all_ones = sb("all_ones", [P, S])
        ident_r = sb("ident_r", [P, S], F32R)
        warm = ident[:].bitcast(BF16)
        table = sb("table", [128, 1])
        slot_no = sb("slot_no", [P, S], F16)
        upto = sb("upto", [128, E, E])
        tile_end = sb("tile_end", [128, NT])
        item_no = sb("item_no", [128, 2 * PAIRS + 1])
        pair_no = sb("pair_no", [128, PAIRS])

        ends = sb("ends", [G, 2])
        endsT = sb("endsT", [1, 2, G])
        last = sb("last", [1, NT])
        bounds = sb("bounds", [1, 3, NT])
        bounds_i = sb("bounds_i", [1, 3, NT], I32)
        a_mem = sb("a_mem", [128, NT * N])
        A = a_mem[0:P, :].rearrange("p (m n) -> p m n", n=N)
        at_mem = sb("at_mem", [128, NT * N])
        AT = at_mem[0:P, :].rearrange("p (m n) -> p m n", n=N)
        idx = at_mem[0:G, 0:1000].bitcast(I32).rearrange("g (w k) -> g w k", w=2)
        idxT = at_mem[0:P, 1000:1640].rearrange("p (w g r) -> p w g r", w=2, r=R)
        span = at_mem[0:1, 1640:2040].rearrange("p (m w g) -> p m w g", m=NT, w=2)
        hot_dst = at_mem[0:P, 2040:2296].bitcast(BF16).rearrange("p (r n) -> p r n", r=R)
        iota = at_mem[0:P, 2296:2616].bitcast(F16)
        zeros = at_mem[0:1, 2616:2872].bitcast(BF16)

        def tm(name, n=D):
            return sb(name, [P, NT, n])

        def fm(name):
            return sb(name, [128, KC, TP])

        X, XB, XN, ACC = tm("X"), tm("XB"), tm("XN", D + 1), tm("ACC")
        XT = fm("XT")
        big_at = next_at()
        big = sb("big", [128, 2, 4 * NT * D])
        CW = sb("CW", [P, E, NT])
        CWT = sb("CWT", [E, TP])
        stats = sb("stats", [P, NT, 6])
        mv = sb("mv", [P, NT, 2])
        var_e = sb("var_e", [P, NT])
        rstd = sb("rstd", [P, NT])
        inv_deg = sb("inv_deg", [P, NT])
        inv_deg_k = sb("inv_deg_k", [P, 6, NT])
        s1, s2 = sb("s1", [128, 16]), sb("s2", [128, 16])
        o1, o2 = sb("o1", [128, 16]), sb("o2", [128, 16])
        v12 = sb("v12", [128, 2, 16])
        sm = [sb(f"sm{i}", [P, 40]) for i in range(8)]
        kcol = sb("kcol", [128, 8])

        def scratch(i, shape):
            n = int(np.prod(shape[1:]))
            lo = (i % 4) * NT * D
            v = big[0:shape[0], i // 4, lo:lo + n]
            if len(shape) == 3:
                return v.rearrange("p (a b) -> p a b", b=shape[2])
            return v

        psF = ctx.enter_context(nc.psum_tensor("psF", [128, 2, 2, 512], F32))
        psT = ctx.enter_context(nc.psum_tensor("psT", [128, 2, 512], F32))
        psX = ctx.enter_context(nc.psum_tensor("psX", [128, 2, 512], F32))

        def wide(ps):
            return ps.rearrange("p a n -> p (a n)")[:, 0:N]

        def tile_out(j):
            ps = psX[0:P, 1] if j == 4 else psT[0:P, j // 2]
            at = D if j == 4 else j % 2 * D
            return ps[:, at:at + D]

        def spread(ps, slot):
            return ps[:, slot].rearrange("p a n -> p (a n)")[:, 0:NT * 128].rearrange("p (j n) -> p j n", n=128)

        f_full, f_free = sem("f_full"), sem("f_free")
        t_full, t_free = sem("t_full"), sem("t_free")
        x_full, x_free = sem("x_full"), sem("x_free")
        ld_x, ld_idx, ld_rows, ld_cols = sem("ld_x"), sem("ld_idx"), sem("ld_rows"), sem("ld_cols")
        ld_small = [sem(f"ld_small{i}") for i in range(4)]
        ld_ffn = [sem("ld_ffn_a"), sem("ld_ffn_b")]
        ffn_used = sem("ffn_used")
        stored = sem("stored")
        consts = sem("consts")
        v_step, a_step, g_step = sem("v_step"), sem("a_step"), sem("g_step")
        idx_f = sem("idx_f")
        bounds_ready = sem("bounds_ready")
        hot_ready, hot_used = sem("hot_ready"), sem("hot_used")
        var_ready, rstd_ready = sem("var_ready"), sem("rstd_ready")
        xn_ready = sem("xn_ready")
        x_ready = sem("x_ready")
        xb_ready = sem("xb_ready")
        cw_ready = sem("cw_ready")
        l0_std, l0_std_r, l0_kv = sem("l0_std"), sem("l0_std_r"), sem("l0_kv")
        l0_w = sem("l0_w")
        logit_ready, exp_ready = sem("logit_ready"), sem("exp_ready")
        l1_pre, l1_u = sem("l1_pre"), sem("l1_u")
        l1_kmin, l1_kexp, l1_k, l1_q, l1_qT = (sem(n) for n in ("l1_kmin", "l1_kexp", "l1_k", "l1_q", "l1_qT"))
        l1_bd, l1_x1, l1_x1b = sem("l1_bd"), sem("l1_x1"), sem("l1_x1b")
        l1_term, l1_sum = sem("l1_term"), sem("l1_sum")
        bn_v, bn_r, bn_ready = sem("bn_v"), sem("bn_r"), sem("bn_ready")
        l2_ab, l2_kT, l2_kmax, l2_kexp, l2_g = (sem(n) for n in ("l2_ab", "l2_kT", "l2_kmax", "l2_kexp", "l2_g"))
        g_shift = sem("g_shift")
        g_diag, g_he = sem("g_diag"), sem("g_he")
        g_rows = sem("g_rows")
        g_relu, g_exp = sem("g_relu"), sem("g_exp")
        g_shift_row = sem("g_shift_row")
        g_sum, g_sum_v = sem("g_sum"), sem("g_sum_v")
        g_p = sem("g_p")
        g_agg, g_turn = sem("g_agg"), sem("g_turn")
        g_out, g_norm = sem("g_out"), sem("g_norm")
        l3_qk, l3_sq, l3_qn, l3_qq, l3_nr = (sem(n) for n in ("l3_qk", "l3_sq", "l3_qn", "l3_qq", "l3_nr"))
        l3_kk, l3_kn2, l3_knr, l3_y1, l3_gnn, l3_q, l3_gw = (sem(n) for n in ("l3_kk", "l3_kn2", "l3_knr", "l3_y1", "l3_gnn", "l3_q", "l3_gw"))

        class ItemSems:

            def __init__(self, level):
                def s(name):
                    return sem(f"{name}{level}")
                self.plan = s("plan")
                self.weights = [s("weights_a"), s("weights_b")]
                self.hot = s("hot")
                self.x_full, self.x_ready = s("ix_full"), s("ix_ready")
                self.h_full, self.h_ready = s("ih_full"), s("ih_ready")
                self.hot_full, self.hot_out = s("hot_full"), s("hot_out")
                self.y_full, self.y_ready = s("iy_full"), s("iy_ready")
                self.o_full, self.o_free = s("io_full"), s("io_free")
                self.step = s("item_step")

        items = [ItemSems(0), ItemSems(3)]

        hot_src = ACC[:].rearrange("p t d -> p (t d)").bitcast(BF16).rearrange("p (r n) -> p r n", r=R)
        y0, k0, v0 = scratch(0, [P, NT, D]), scratch(1, [P, NT, D]), scratch(2, [P, NT, D])
        sq0 = scratch(3, [P, NT, D])
        ag, agT = scratch(4, [P, NT, D]), scratch(5, [128, KC, TP])
        wc, kv0 = scratch(6, [128, KC, D]), scratch(4, [128, KC, 128])
        idx_float = scratch(7, [G, 2, R * P])
        u_pre, u = scratch(0, [P, NT, D]), scratch(1, [P, NT, D])
        k_neg, k1, v1m = scratch(2, [P, NT, D]), scratch(3, [P, NT, D]), scratch(4, [P, NT, D])
        q_neg, q_pos = scratch(5, [128, KC, TP]), scratch(6, [128, KC, TP])
        bd = scratch(7, [128, KC, 132])
        mix, x1m, x1T, hT1, x1b = (scratch(2, [P, NT, D]), scratch(3, [P, NT, D]), scratch(4, [128, KC, TP]),
                                   scratch(5, [128, KC, TP]), scratch(6, [P, NT, D]))
        term = [scratch(1, [P, NT, D]), scratch(0, [P, NT, D])]
        total, totalT = ACC, scratch(7, [128, KC, TP])
        a_row = big[0:P, 0, 0:H8 * TP].rearrange("p (h n) -> p h n", n=TP)
        no_edge = big[0:P, 1, 0:NT * N].rearrange("p (m n) -> p m n", n=N)
        he = sb("he", [P, NT, H8, HC + 1])
        score, e_score = (w_ffn[0:P, i, 0:NT * N].rearrange("p (j n) -> p j n", n=N) for i in range(2))
        masked_row = [w_ffn[0:P, 0, NT * N:NT * N + N], big[0:P, 1, 7 * TP:7 * TP + N]]
        out_rows = w_ffn[0:HC + 1, 1, NT * N:NT * N + N]
        diagonal = [XT[0:P, i, 0:N].rearrange("p (m n) -> p m n", n=P) for i in range(2)]
        he_now = big[0:P, 1, 5 * TP:5 * TP + NT * (HC + 1)].rearrange("p (t c) -> p t c", c=HC + 1)
        shift_row = big[0:P, 1, 6 * TP:6 * TP + N]
        q2T, k2T, kx2 = big[:, 1, 0:TP], big[:, 1, TP:2 * TP], big[:, 1, 2 * TP:3 * TP]
        k2m, v2m = big[0:P, 1, 3 * TP:3 * TP + 640], big[0:P, 1, 4 * TP + 12:4 * TP + 652]
        ctT, gw2 = big[:, 1, 5 * TP + 24:5 * TP + 152], big[:, 1, 5 * TP + 152:5 * TP + 408]
        hm = scratch(3, [P, NT, D])
        hsum = sb("hsum", [P, 2, NT, H8])
        asT = CWT
        mx = sb("mx", [P, NT])
        a_now = sb("a_now", [P, N])
        gm, ad_t, shift, z2 = (sb(n, [P, H8, NT]) for n in ("gm", "ad_t", "shift", "z2"))
        as2, as8 = sb("as2", [P, NT, H8]), sb("as8", [P, NT, H8])
        ad_h = hsum[:, 1].rearrange("p t h -> p h t")
        den = sb("den", [P, NT])
        qk = big[0:P, 0, 0:NT * 2 * D].rearrange("p (t n) -> p t n", n=2 * D)
        qk2 = big[0:P, 1, 0:NT * 2 * D].rearrange("p (t n) -> p t n", n=2 * D)
        gnn3 = XN[:, :, 0:D]
        y3, v3, vT3, kk3 = scratch(2, [P, NT, D]), scratch(3, [P, NT, D]), scratch(6, [128, KC, TP]), ACC
        qT3, kvT, gw3 = scratch(0, [128, KC, TP]), scratch(7, [128, KC, D]), scratch(7, [128, 2 * KC, D])[:, KC:2 * KC, :]
        pool_at = [0]

        def at(name, shape, offset):
            return nc.alloc_sbuf_tensor_at(name, shape, F32R, offset=offset)[:]

        def piece(parts, shape, name=None):
            n = -(-int(np.prod(shape)) // 8) * 8
            lo, pool_at[0] = pool_at[0], pool_at[0] + n
            if name:
                return at(name, [parts] + shape, big_at + 4 * lo)
            v = big[:].rearrange("p a n -> p (a n)")[0:parts, lo:lo + int(np.prod(shape))]
            if len(shape) == 2:
                return v.rearrange("p (a b) -> p a b", b=shape[1])
            return v

        hot_in = [piece(P, [NT, S], f"hot_in{b}") for b in range(2)]
        hot_out = piece(S, [TP], "hot_out")
        x_item = piece(128, [KC, S])
        h_item = piece(128, [8, S])
        y_item = piece(S, [2, D], "y_item")
        chosen = piece(P, [NT + 1, E])
        choice_sum = piece(P, [NT + 1, E])
        rank_p1 = piece(P, [NT, E])
        rank = piece(P, [E, NT])
        rank_item = [piece(P, [NT]) for _ in range(2)]
        n_chosen, n_tiles, e_end, e_start = (piece(128, [E]) for _ in range(4))
        by_tile = piece(128, [E, NT])
        by_expert = piece(128, [E, E])
        by_item, by_item2 = (piece(128, [2 * PAIRS + 1, E]) for _ in range(2))
        item_e, item_start, item_off = (piece(128, [2 * PAIRS + 1]) for _ in range(3))
        by_pair, n_pairs = piece(128, [PAIRS]), piece(128, [1])
        plan = piece(1, [2 * PAIRS + 2]).bitcast(I32)
        assert pool_at[0] <= 8 * NT * D

        hidden = [big[:, u_, 0:8 * TP].rearrange("p (k n) -> p k n", n=TP) for u_ in range(2)]

        F_K2 = 2 * NT + 2 * KC + E * 2 * KC + 2

        block = ctx.enter_context(nc.Block())

        @block.sync
        def _(sp):
            sp.dma_start(X[:], x.rearrange("(t p) d -> p t d", p=P)).then_inc(ld_x, 16)
            sp.dma_start(idx[:, 1, :], dst.rearrange("(g k) -> g k", g=G)).then_inc(ld_idx, 16)
            sp.dma_start(idx[:, 0, :], src.rearrange("(g k) -> g k", g=G)).then_inc(ld_idx, 16)
            sp.dma_start(w_rows[:], rows.partition_broadcast(P)).then_inc(ld_rows, 16)
            edge = [0, SMALL["l1_win"][0], SMALL["l2_w"][0], SMALL["l3_w0"][0], SMALL["end"]]
            sp.dma_start(w_small[:, edge[0]:edge[1]], small[:, edge[0]:edge[1]]).then_inc(ld_small[0], 16)
            sp.dma_start(w_cols[:], cols).then_inc(ld_cols, 16)
            sp.dma_start(w_eb2[:], eb2).then_inc(ld_cols, 16)
            for n in range(1, 4):
                sp.dma_start(w_small[:, edge[n]:edge[n + 1]], small[:, edge[n]:edge[n + 1]]).then_inc(ld_small[n], 16)

            def item_weights(q, weights, n):
                sp.wait_ge(q.plan, 1)
                pairs = sp.value_load(plan[0:1, 2 * PAIRS + 1:2 * PAIRS + 2], min_val=1, max_val=PAIRS)
                with sp.Fori(0, pairs) as i:
                    for b in range(2):
                        e = sp.value_load(plan[0:1, bass.ds(i * 2 + b, 1)], min_val=0, max_val=E - 1)
                        sp.wait_ge(q.y_full, i * 2 + (b + 1))
                        sp.dma_start(w_ffn[:, b, 0:n], weights[bass.ds(e, 1), :, :].rearrange("o p n -> (o p) n"))\
                          .then_inc(q.weights[b], 16)

            item_weights(items[0], ffn0, FFN0)
            with sp.Fori(0, E // 2) as i:
                for b in range(2):
                    sp.wait_ge(ffn_used, i * 2 + (b + 1))
                    sp.dma_start(w_ffn[:, b, 0:FFN1], ffn1[bass.ds(i * 2 + b, 1), :, :].rearrange("o p n -> (o p) n"))\
                      .then_inc(ld_ffn[b], 16)
            item_weights(items[1], ffn3, FFN3)
            sp.wait_ge(x_ready, 8)
            sp.dma_start(out.rearrange("(t p) d -> p t d", p=P), X[:]).then_inc(stored, 16)
            sp.wait_ge(stored, 16)

        @block.gpsimd
        def _(pool):
            steps = Count()

            def link(ins):
                ins.then_inc(g_step, 1)
                steps.n += 1
                pool.wait_ge(g_step, steps.n)

            link(pool.memset(ident[:], 0.0))
            link(pool.affine_select(out=ident[:], in_=ident[:], compare_op=ALU.not_equal, fill=1.0, base=0,
                                    pattern=[[-1, 128]], channel_multiplier=1))
            link(pool.memset(zeros, 0.0))
            link(pool.iota(iota, pattern=[[1, 640]], base=0, channel_multiplier=0, allow_small_or_imprecise_dtypes=True))
            link(pool.iota(tile_start[:], pattern=[[P, NT], [0, G]], base=0, channel_multiplier=0, allow_small_or_imprecise_dtypes=True))
            link(pool.iota(group_no[:, 0, :], pattern=[[-1, G]], base=G, channel_multiplier=0, allow_small_or_imprecise_dtypes=True))
            pool.iota(group_no[:, 1, :], pattern=[[1, G]], base=1, channel_multiplier=0, allow_small_or_imprecise_dtypes=True).then_inc(consts, 1)
            pool.wait_ge(consts, 1)
            for tensor, value in ((pick, 0.0), (headmask, 0.0), (headcols, 0.0), (ones, 1.0),
                                  (minus_half, -0.5), (half, 0.5)):
                link(pool.memset(tensor[:], value))
            link(pool.memset(XN[:, :, D:D + 1], 1.0))
            link(pool.memset(he[:, :, :, HC:HC + 1], 1.0))
            link(pool.memset(XT[:, :, N:TP], 0.0))
            link(pool.memset(asT[:, N:TP], 0.0))
            link(pool.iota(order[:], pattern=[[-1, E]], base=E, channel_multiplier=0, allow_small_or_imprecise_dtypes=True))
            link(pool.affine_select(out=pick[:], in_=pick[:], compare_op=ALU.not_equal, fill=1.0, base=0,
                                    pattern=[[-1, H8], [0, 128]], channel_multiplier=1))
            link(pool.memset(all_ones[:], 1.0))
            link(pool.memset(earlier[:], 1.0))
            link(pool.memset(upto[:], 1.0))
            link(pool.affine_select(out=earlier[:], in_=earlier[:], compare_op=ALU.is_ge, fill=0.0, base=-1,
                                    pattern=[[1, S]], channel_multiplier=-1))
            link(pool.affine_select(out=upto[:], in_=upto[:], compare_op=ALU.is_ge, fill=0.0, base=0,
                                    pattern=[[1, E], [-1, E]], channel_multiplier=0))
            link(pool.tensor_copy(ident_r[:], ident[0:P, 0:S]))
            for tensor, step in ((slot_no, 1), (tile_end, S), (item_no, 1), (pair_no, 2)):
                link(pool.iota(tensor[:], pattern=[[step, tensor.shape[1]]], base=0, channel_multiplier=0,
                               allow_small_or_imprecise_dtypes=True))
            for h in range(4):
                link(pool.memset(headmask[HC * h:HC * h + HC, HC * h:HC * h + HC], 1.0))
                ins = pool.memset(headcols[HC * h:HC * h + HC, h:h + 1], 1.0)
                link(ins) if h < 3 else ins.then_inc(consts, 1)

            ln = Count()

            def rsqrt():
                ln.n += 1
                pool.wait_ge(var_ready, ln.n)
                pool.tensor_tensor(rstd[:], var_e[:], minus_half[0:P, 0:NT], ALU.pow).then_inc(rstd_ready, 1)

            def residual(name):
                pool.tensor_tensor(XB[:], X[:], row(name), ALU.add).then_inc(xb_ready, 1)

            pool.wait_ge(consts, 2)
            rsqrt()
            pool.wait_ge(ld_rows, 16)
            residual("l0_br")
            rsqrt()
            rsqrt()
            pool.wait_ge(x_ready, 2)
            residual("l1_bout")
            pool.wait_ge(bn_v, 1)
            pool.tensor_tensor(v12[:, 0, :], v12[:, 0, :], minus_half[:], ALU.pow)
            pool.tensor_tensor(v12[:, 1, :], v12[:, 1, :], minus_half[:], ALU.pow).then_inc(bn_r, 1)
            rsqrt()
            pool.wait_ge(l1_x1, 1)
            pool.tensor_tensor(x1b[:], x1m[:], row("l1_b2"), ALU.add).then_inc(l1_x1b, 1)
            rsqrt()
            pool.wait_ge(l1_u, 1)
            pool.tensor_copy(total[:], u[:]).then_inc(l1_sum, 2)
            with pool.Fori(0, 3) as i:
                for b in range(2):
                    pool.wait_ge(l1_term, i * 2 + (b + 1))
                    pool.wait_ge(l1_sum, i * 2 + (b + 2))
                    pool.tensor_tensor(total[:], total[:], term[1 - b][:], ALU.add).then_inc(l1_sum, 1)
            rsqrt()
            rsqrt()
            pool.wait_ge(x_ready, 4)
            residual("l2_bout")

            def diagonals(h, at):
                pool.wait_ge(g_shift, at + 1)
                if not (isinstance(at, int) and at == 0):
                    pool.wait_ge(g_rows, at)
                for k, a in enumerate((ad_t, shift)):
                    ins = pool.tensor_tensor(diagonal[k], ident[0:P, 0:P].unsqueeze(1).to_broadcast([P, NT, P]),
                                             a[:, h, :].rearrange("p a m -> p (a m)").unsqueeze(2).to_broadcast([P, NT, P]),
                                             ALU.mult)
                ins.then_inc(g_diag, 1)

            def exponents(h, at):
                pool.wait_ge(g_agg, at * NT + NT)
                pool.tensor_copy(he_now, he[:, :, h, :].rearrange("p t a c -> p t (a c)")).then_inc(g_he, 1)
                pool.wait_ge(g_shift_row, at + 1)
                for j in G_TILES:
                    pool.wait_ge(g_relu, at * NT + (j + 1))
                    pool.tensor_tensor(score[:, j, :], score[:, j, :], shift_row, ALU.add).then_inc(g_sum, 1)

            diagonals(bass.ds(0, 1), 0)
            diagonals(bass.ds(1, 1), 1)
            with pool.Fori(0, H8 - 2) as i:
                exponents(bass.ds(i, 1), i)
                diagonals(bass.ds(i + 2, 1), i + 2)
            for h in (H8 - 2, H8 - 1):
                exponents(bass.ds(h, 1), h)
            rsqrt()
            pool.wait_ge(x_ready, 5)
            residual("l2_ffnb")
            rsqrt()
            pool.wait_ge(x_ready, 6)
            residual("l3_bout")
            for s_in, s_out, a in ((l3_qq, l3_nr, sm[4][:, 0:NT]), (l3_kn2, l3_knr, kcol[:, 0:KC])):
                pool.wait_ge(s_in, 1)
                pool.tensor_tensor(a, a, half[0:a.shape[0], 0:a.shape[1]], ALU.pow).then_inc(s_out, 1)
            pool.wait_ge(l3_gnn, 1)
            pool.tensor_tensor(XB[:], XB[:], gnn3, ALU.add).then_inc(xb_ready, 1)
            rsqrt()
            rsqrt()

        @block.scalar
        def _(act):
            f = Count(2)
            a = Count()

            def link(ins):
                ins.then_inc(a_step, 1)
                a.n += 1
                act.wait_ge(a_step, a.at())

            def full(halves=TH):
                act.wait_ge(f_full, f.at(1))
                return psF[:, f.slot, :, 0:halves]

            def free(ins):
                ins.then_inc(f_free, 1)
                f.n += 1

            def halves(v):
                return v.rearrange("p (a n) -> p a n", a=2)

            act.wait_ge(consts, 2)
            for m in range(NT):
                full()
                act.activation(A[:, m, 0:512], psF[0:P, f.slot, 0, :], ACT.Copy)
                free(act.activation(A[:, m, 512:N], psF[0:P, f.slot, 1, 0:N - 512], ACT.Copy))

            for m in range(NT):
                full()
                free(act.activation(AT[:, :, m * P:m * P + P], spread(psF, f.slot)[0:P, :, 0:P], ACT.Copy))

            act.wait_ge(l0_std, 1)
            act.activation(sm[1][:], sm[1][:], ACT.Sqrt, scale=1.0 / (HC - 1)).then_inc(l0_std_r, 1)

            def soft(n):
                act.wait_ge(logit_ready, n)
                act.activation(sm[1][:], sm[1][:], ACT.Exp).then_inc(exp_ready, 1)

            def item_layers(q, chunks, b1, affine=False):
                act.wait_ge(q.plan, 1)
                pairs = act.value_load(plan[0:1, 2 * PAIRS + 1:2 * PAIRS + 2], min_val=1, max_val=PAIRS)
                act.nop().then_inc(q.h_ready, 2)

                def expert(at):
                    return act.value_load(plan[0:1, at], min_val=0, max_val=E - 1)

                def x_to_sbuf(e):
                    for c in range(KC):
                        ps = psX[:, 0, c * S:c * S + S]
                        if affine:
                            ins = act.activation(x_item[:, c, :], ps, ACT.Identity, bias=col("l3_b")[:, bass.ds(e * KC + c, 1)],
                                                 scale=col("l3_g")[:, bass.ds(e * KC + c, 1)])
                        else:
                            ins = act.activation(x_item[:, c, :], ps, ACT.Copy)
                    ins.then_inc(q.x_ready, 1)

                e_next = expert(slice(0, 1))
                act.wait_ge(q.x_full, 1)
                x_to_sbuf(e_next)
                with act.Fori(0, pairs) as i:
                    act.activation(table[:], ones[:, 0:1], ACT.Gelu)
                    for b in range(2):
                        e = expert(bass.ds(i * 2 + b, 1))
                        for k in range(chunks):
                            unit, place = divmod(k, chunks // 2)
                            if place == 0:
                                act.wait_ge(q.h_full, i * 4 + (b * 2 + unit + 1))
                            ins = act.activation(h_item[:, k, :], psF[:, 0, unit, place * S:place * S + S],
                                                 ACT.Gelu, bias=col(b1)[:, bass.ds(e * chunks + k, 1)])
                            if place == chunks // 2 - 1:
                                ins.then_inc(q.h_ready, 1)
                        act.wait_ge(q.hot_full, i * 2 + (b + 2))
                        act.activation(hot_out[:, 0:NT * P].rearrange("p (j n) -> p j n", n=P),
                                       spread(psF, 1)[:, :, 0:P], ACT.Copy).then_inc(q.hot_out, 1)
                        e_next = expert(bass.ds(i * 2 + (b + 1), 1))
                        act.wait_ge(q.x_full, i * 2 + (b + 2))
                        x_to_sbuf(e_next)

            soft(1)
            act.wait_ge(ld_cols, 32)
            item_layers(items[0], 4, "l0_b1")
            act.wait_ge(l1_pre, 1)
            act.activation(u[:], u_pre[:], ACT.Silu).then_inc(l1_u, 1)
            for c in range(KC):
                ps = full()
                act.activation(halves(q_pos[:, c, :]), ps, ACT.Relu)
                free(act.activation(halves(q_neg[:, c, :]), ps, ACT.Relu, scale=-1.0))
            act.wait_ge(f_free, f.n)
            act.activation(q_neg[:], q_neg[:], ACT.Exp, scale=-1.0).then_inc(l1_q, 1)
            act.wait_ge(l1_kmin, NT)
            act.activation(k_neg[:], k_neg[:], ACT.Exp).then_inc(l1_kexp, 1)
            for c in range(KC):
                ps = full()
                free(act.activation(halves(hT1[:, c, :]), ps, ACT.Gelu, bias=col("l1_mb1")[:, c:c + 1]))
            soft(2)
            act.wait_ge(bn_ready, 1)
            with act.Fori(0, E // 2) as i:
                f.enter(i, 8)
                for layer, s, o in ((0, s1, o1), (1, s2, o2)):
                    for b in range(2):
                        for c in range(KC):
                            ps = full()
                            at = bass.ds((i * 2 + b) * KC + c, 1)
                            free(act.activation(halves(hidden[b][:, layer * KC + c, :]), ps, ACT.Relu,
                                                bias=o[:, at], scale=s[:, at]))
                f.leave(E // 2)
            free(act.activation(halves(q2T), full(), ACT.Copy))
            free(act.activation(halves(k2T), full(), ACT.Copy))
            act.wait_ge(l2_kmax, 1)
            act.activation(kx2[:, 0:N], k2T[:, 0:N], ACT.Exp, bias=kcol[:, 0:1], accum_out=kcol[:, 1:2]).then_inc(l2_kexp, 1)
            for h in range(H8):
                ps = full()
                free(act.activation(halves(a_row[:, h, :]), ps[0:P], ACT.Copy))
            act.nop().then_inc(g_exp, NT)
            with act.Fori(0, H8) as i:
                h = bass.ds(i, 1)
                act.wait_ge(g_rows, i + 1)
                act.activation(shift_row, wide(psF[0:P, 1]), ACT.Copy).then_inc(g_shift_row, 1)
                for j in range(NT):
                    act.wait_ge(g_exp, i * NT + (TILES.index(j) + 1))
                    act.activation(score[:, j, :], wide(psF[0:P, 0]), ACT.Relu, bias=as8[:, j, h], scale=0.8)\
                       .then_inc(g_relu, 1)
                for n, j in enumerate(TILES):
                    if j in G_TILES:
                        act.wait_ge(g_sum, i * len(G_TILES) + (G_TILES.index(j) + 1))
                    else:
                        act.wait_ge(g_sum_v, i * len(V_TILES) + (V_TILES.index(j) + 1))
                    act.wait_ge(g_agg, i * NT + (n + 1))
                    act.activation(e_score[:, j, :], score[:, j, :], ACT.Exp, bias=as2[:, j, h]).then_inc(g_exp, 1)
            act.wait_ge(l3_qk, 1)
            for t in range(NT):
                for w in range(2):
                    ins = act.activation(qk2[:, t, w * D:w * D + D], qk[:, t, w * D:w * D + D], ACT.Square,
                                         bias=sm[0][:, 2 * t + w:2 * t + w + 1],
                                         accum_out=sm[1][:, 2 * t + w:2 * t + w + 1])
            ins.then_inc(l3_sq, 1)
            for c in range(KC):
                ps = full()
                free(act.activation(halves(vT3[:, c, :]), ps, ACT.Identity, bias=col("l3_bv")[:, c:c + 1]))
            act.wait_ge(l3_qn, 1)
            for t in range(NT):
                ins = act.activation(qk[:, t, 0:D], qk2[:, t, 0:D], ACT.Square, accum_out=sm[4][:, t:t + 1])
            ins.then_inc(l3_qq, 1)
            act.activation(kk3[:], qk2[:, :, D:2 * D], ACT.Square).then_inc(l3_kk, 1)
            soft(3)
            item_layers(items[1], 8, "l3_b1", affine=True)

        @block.tensor
        def _(pe):
            f, t, xr = Count(2), Count(2), Count(2)

            def f_slot():
                if f.more is not None or f.n >= 2:
                    pe.wait_ge(f_free, f.at(-1))
                return psF[:, f.slot]

            def f_done(ins):
                ins.then_inc(f_full, 1)
                f.n += 1

            def t_slot():
                if t.more is not None or t.n >= 2:
                    pe.wait_ge(t_free, t.at(-1))
                return psT[:, t.slot]

            def t_done(ins):
                ins.then_inc(t_full, 1)
                t.n += 1

            def x_slot():
                if xr.n >= 2:
                    pe.wait_ge(x_free, xr.n - 1)
                return psX[:, xr.slot]

            def x_done(ins):
                ins.then_inc(x_full, 1)
                xr.n += 1

            def keep_warm(n):
                ps = x_slot()
                for _ in range(n):
                    pe.matmul(ps[:, 0:2 * S], warm[:, 0:S], warm, start=True, stop=True)

            def turn_norm(k):
                keep_warm(36)
                turn(XN, k)

            def turn(a, norm=None):
                for c in range(KC):
                    ps = x_slot()
                    for i in range(4):
                        if norm and c == 0:
                            pe.wait_ge(xn_ready, NT * (norm - 1) + i + 1)
                        ins = pe.transpose(ps[:, i * P:i * P + P], a[:, i, c * 128:c * 128 + 128], ident[0:P, 0:P])
                    x_done(ins)
                ps = x_slot()
                if norm:
                    pe.wait_ge(xn_ready, NT * norm)
                for c in range(KC):
                    ins = pe.transpose(ps[:, c * P:c * P + P], a[:, 4, c * 128:c * 128 + 128], ident[0:P, 0:P])
                x_done(ins)

            def turned():
                pe.wait_ge(x_free, xr.n)

            def rows_of(terms, n, at=0):
                for i in range(NT):
                    ps = t_slot()
                    pairs = terms(i)
                    for k, (lhsT, rhs) in enumerate(pairs):
                        ins = pe.matmul(ps[0:P, at:at + n], lhsT, rhs, start=k == 0, stop=k == len(pairs) - 1)
                    t_done(ins)

            def linear(actT, w, a=0, b=D, chunks=KC):
                return lambda i: [(actT[:, c, i * P:i * P + P], w[:, c, a:b]) for c in range(chunks)]

            def chunk_fm(ps, weight, actT, chunks):
                for c in range(chunks):
                    for h in range(2):
                        ins = pe.matmul(ps[:, h, 0:TH], weight(c), actT[:, c, h * TH:h * TH + TH],
                                        start=c == 0, stop=c == chunks - 1)
                return ins

            def bias_rows(n):
                rows_of(lambda i: [(CWT[:, i * P:i * P + P], w_eb2[:, n, :])], D)

            def router(n, w, plan_items=False):
                ps = t_slot()
                for i in range(NT):
                    for c in range(KC):
                        ins = pe.matmul(ps[0:P, i * E:i * E + E], XT[:, c, i * P:i * P + P], w[:, c, :],
                                        start=c == 0, stop=c == KC - 1)
                t_done(ins)
                keep_warm(32 if plan_items else 12)
                pe.wait_ge(cw_ready, n + 1)
                if plan_items:
                    ps = x_slot()
                    pe.matmul(ps[:, 0:(NT + 1) * E], all_ones[:], choice_sum.rearrange("p t e -> p (t e)"), start=True, stop=False)
                    x_done(pe.matmul(ps[:, 0:(NT + 1) * E], earlier[:], chosen.rearrange("p t e -> p (t e)"), start=False, stop=True))
                for tiles in ((0, 1, 2, 3), (4,)):
                    ps = x_slot()
                    for i in tiles:
                        ins = pe.transpose(ps[0:E, (i % 4) * P:(i % 4) * P + P], CW[:, :, i], ident[0:P, 0:P])
                    x_done(ins)
                turned()
                if not plan_items:
                    bias_rows(n)

            pe.wait_ge(consts, 1)
            pe.wait_ge(idx_f, 1)
            ps = x_slot()
            for w in range(2):
                for r in range(R):
                    pe.transpose(ps[0:P, (w * R + r) * G:(w * R + r) * G + G], idx_float[:, w, r * P:r * P + P], ident[0:G, 0:G])
            for w in range(2):
                ins = pe.transpose(ps[0:1, (2 * R + w) * G:(2 * R + w) * G + G], ends[:, w:w + 1], ident[0:G, 0:G])
            x_done(ins)
            turn_norm(1)
            pe.wait_ge(bounds_ready, 1)
            count = [pe.value_load(bounds_i[0:1, 1, m:m + 1], min_val=1, max_val=G) for m in range(NT)]
            before = [pe.value_load(bounds_i[0:1, 2, m:m + 1], min_val=0, max_val=G * NT) for m in range(NT)]
            for m in range(NT):
                ps = f_slot()
                for part, lo, hi in ((0, 0, 512), (1, 512, N)):
                    ins = pe.matmul(ps[0:P, part, 0:hi - lo], zeros[:, 0:P], zeros[:, 0:hi - lo],
                                    start=True, stop=False, skip_group_check=True)
                if m == 0:
                    ins.then_inc(hot_used, 2)
                with pe.Fori(0, count[m]) as j:
                    for r in range(R):
                        if r % 2 == 0:
                            pe.wait_ge(hot_ready, (before[m] + j) * 2 + (r // 2 + 1))
                        pe.matmul(ps[0:P, 0, :], hot_dst[:, r, 0:P], hot_src[:, r, 0:512],
                                  start=False, stop=False, skip_group_check=True)
                        ins = pe.matmul(ps[0:P, 1, 0:N - 512], hot_dst[:, r, 0:P], hot_src[:, r, 512:N],
                                        start=False, stop=False, skip_group_check=True)
                        if r % 2:
                            ins.then_inc(hot_used, 1)
                for part, lo, hi in ((0, 0, 512), (1, 512, N)):
                    ins = pe.matmul(ps[0:P, part, 0:hi - lo], zeros[:, 0:P], zeros[:, 0:hi - lo],
                                    start=False, stop=True, skip_group_check=True)
                f_done(ins)
            for m in range(NT):
                pe.wait_ge(f_free, m + 1)
                f_slot()
                ps = spread(psF, f.slot)
                for j in range(NT):
                    ins = pe.transpose(ps[0:P, j, 0:P], A[:, m, j * P:j * P + P], ident[0:P, 0:P])
                f_done(ins)
            pe.wait_ge(f_free, f.n)
            pe.wait_ge(consts, 2)
            rows_of(lambda m: [(AT[:, j, m * P:m * P + P], XN[:, j, :]) for j in range(NT)], D + 1)
            pe.wait_ge(t_free, t.n)
            turn(ag)
            pe.wait_ge(l0_kv, 1)
            ps = t_slot()
            for c in range(KC):
                for i in range(NT):
                    ins = pe.matmul(ps[:, c * 128:c * 128 + 128], k0[:, i, c * 128:c * 128 + 128],
                                    v0[:, i, c * 128:c * 128 + 128], start=i == 0, stop=i == NT - 1)
            t_done(ins)
            turned()
            pe.wait_ge(ld_small[0], 16)
            pe.wait_ge(l0_w, 1)
            rows_of(lambda i: linear(agT, W("l0_wl"))(i) + linear(XT, wc)(i), D)

            def item_products(q, n, hid, chunks, rows_ready=None):
                pe.wait_ge(q.plan, 1)
                pairs = pe.value_load(plan[0:1, 2 * PAIRS + 1:2 * PAIRS + 2], min_val=1, max_val=PAIRS)
                pe.nop().then_inc(q.hot_full, 1)
                pe.nop().then_inc(q.y_full, 2)

                def gather(b):
                    for c in range(KC):
                        for j in range(NT):
                            ins = pe.matmul(psX[:, 0, c * S:c * S + S], XN[:, j, c * 128:c * 128 + 128],
                                            hot_in[b][:, j, :].bitcast(F32), start=j == 0, stop=j == NT - 1)
                    ins.then_inc(q.x_full, 1)

                keep_warm(32)
                pe.wait_ge(q.hot, 1)
                if rows_ready is not None:
                    pe.wait_ge(xn_ready, NT * rows_ready)
                gather(0)
                bias_rows(n)
                pe.wait_ge(f_free, f.n)
                pe.wait_ge(t_free, t.n)
                with pe.Fori(0, pairs) as i:
                    for b in range(2):
                        w1 = w_ffn[:, b, 0:KC * hid].rearrange("p (c n) -> p c n", c=KC)
                        w2 = w_ffn[:, b, KC * hid:KC * hid + chunks * D].rearrange("p (k n) -> p k n", n=D)
                        pe.wait_ge(q.weights[b], i * 16 + 16)
                        pe.wait_ge(q.x_ready, i * 2 + (b + 1))
                        for k in range(chunks):
                            unit, place = divmod(k, chunks // 2)
                            if place == 0:
                                pe.wait_ge(q.h_ready, i * 4 + (b * 2 + unit + 1))
                            for c in range(KC):
                                ins = pe.matmul(psF[:, 0, unit, place * S:place * S + S], w1[:, c, k * 128:k * 128 + 128],
                                                x_item[:, c, :], start=c == 0, stop=c == KC - 1)
                            if place == chunks // 2 - 1:
                                ins.then_inc(q.h_full, 1)
                        for j in range(NT):
                            ins = pe.matmul(spread(psF, 1)[:, j, :], hot_in[b][:, j, :], ident_r[:], start=True, stop=True)
                        ins.then_inc(q.hot_full, 1)
                        pe.wait_ge(q.o_free, i * 6 + (b * 3 + 3))
                        for k in range(chunks):
                            unit, place = divmod(k, chunks // 2)
                            if place == 0:
                                pe.wait_ge(q.h_ready, i * 4 + (b * 2 + unit + 3))
                            ins = pe.matmul(psX[:, 1, 0:D], h_item[:, k, :], w2[:, k, :], start=k == 0, stop=k == chunks - 1)
                        ins.then_inc(q.y_full, 1)
                        pe.wait_ge(q.hot, i * 2 + (b + 2))
                        gather(1 - b)
                        pe.wait_ge(q.hot_out, i * 2 + (b + 1))
                        pe.wait_ge(q.y_ready, i * 2 + (b + 1))
                        for j in range(NT):
                            for part in range(2):
                                ins = pe.matmul(tile_out(j), hot_out[:, j * P:j * P + P], y_item[:, part, :],
                                                start=part == 0, stop=part == 1)
                            if j in (1, 3, 4):
                                ins.then_inc(q.o_full, 1)
                pe.wait_ge(q.x_ready, pairs * 2 + 1)
                pe.wait_ge(q.o_free, pairs * 6 + 3)

            turn_norm(2)
            turned()
            pe.wait_ge(ld_cols, 32)
            router(0, W("l0_gate"), plan_items=True)
            item_products(items[0], 0, 512, 4)
            pe.wait_ge(ld_small[1], 16)
            pe.nop().then_inc(ffn_used, 2)
            turn_norm(3)
            turned()
            rows_of(linear(XT, W("l1_win")), D)
            for c in range(KC):
                f_done(chunk_fm(f_slot(), lambda k: W("l1_qkv")[:, k, c * 128:c * 128 + 128], XT, KC))
            rows_of(linear(XT, W("l1_qkv"), D, 3 * D), 2 * D)
            keep_warm(16)
            pe.wait_ge(l1_k, 1)
            ps = t_slot()
            for c in range(KC):
                for rhs, at, n in ((v1m, c * 128, 128), (None, D + c, 1)):
                    for i in range(NT):
                        ins = pe.matmul(ps[:, at:at + n], k1[:, i, c * 128:c * 128 + 128],
                                        ones[0:P, 0:1] if rhs is None else rhs[:, i, c * 128:c * 128 + 128],
                                        start=i == 0, stop=i == NT - 1)
            t_done(ins)
            pe.wait_ge(l1_qT, 1)
            pe.wait_ge(l1_bd, 1)
            for i in range(NT):
                ps = t_slot()
                for c in range(KC):
                    ins = pe.matmul(ps[0:P, c * 132:c * 132 + 132], q_pos[:, c, i * P:i * P + P], bd[:, c, :],
                                    start=True, stop=True)
                t_done(ins)
            keep_warm(72)
            pe.wait_ge(l1_x1, 1)
            turn(x1m)
            turned()
            for c in range(KC):
                f_done(chunk_fm(f_slot(), lambda k: W("l1_w1")[:, k, c * 128:c * 128 + 128], x1T, KC))
            pe.wait_ge(f_free, f.n)
            rows_of(linear(hT1, W("l1_w2")), D)
            keep_warm(12)
            pe.wait_ge(l1_u, 1)
            with pe.Fori(0, 3) as i:
                t.enter(i, 2 * NT)
                for b in range(2):
                    pe.wait_ge(t_free, t.at())
                    rows_of(lambda m: [(AT[:, j, m * P:m * P + P], term[b][:, j, :]) for j in range(NT)], D)
                t.leave(3)
            keep_warm(24)
            pe.wait_ge(l1_sum, 8)
            turn(total)
            turned()
            rows_of(linear(totalT, W("l1_wout")), D)
            turn_norm(4)
            turned()
            router(1, W("l1_wr"))
            with pe.Fori(0, E // 2) as i:
                f.enter(i, 8)
                t.enter(i, 2 * NT)
                w = [w_ffn[:, b, 0:FFN1].rearrange("p (l c n) -> p l c n", l=3, c=KC) for b in range(2)]
                for layer in range(2):
                    for b in range(2):
                        if layer == 0:
                            pe.wait_ge(ld_ffn[b], i * 16 + 16)
                        else:
                            pe.wait_ge(f_free, f.at(-2))
                        src_fm = XT if layer == 0 else hidden[b][:, 0:KC, :]
                        for c in range(KC):
                            f_done(chunk_fm(f_slot(), lambda k: w[b][:, layer, k, c * 128:c * 128 + 128], src_fm, KC))
                for b in range(2):
                    pe.wait_ge(f_free, f.at(-2 + 2 * b))
                    rows_of(linear(hidden[b][:, KC:2 * KC, :], w[b][:, 2]), D)
                    pe.wait_ge(t_full, t.at())
                    pe.nop().then_inc(ffn_used, 1)
                f.leave(E // 2)
                t.leave(E // 2)
            pe.wait_ge(ld_small[2], 16)
            turn_norm(5)
            turned()
            rows_of(linear(XT, W("l2_w")), D)
            for w in range(2):
                f_done(chunk_fm(f_slot(), lambda k: W("l2_qkv")[:, k, w * 128:w * 128 + 128], XT, KC))
            for tiles in ((0, 1, 2, 3), (4,)):
                ps = t_slot()
                for i in tiles:
                    for c in range(KC):
                        ins = pe.matmul(ps[0:P, (i % 4) * 128:(i % 4) * 128 + 128], XT[:, c, i * P:i * P + P],
                                        W("l2_qkv")[:, c, 256:384], start=c == 0, stop=c == KC - 1)
                t_done(ins)
            keep_warm(16)
            pe.wait_ge(l2_ab, 1)
            for tiles in ((0, 1, 2, 3), (4,)):
                ps = x_slot()
                for i in tiles:
                    ins = pe.transpose(ps[0:H8, (i % 4) * P:(i % 4) * P + P], hsum[:, 0, i, :], ident[0:P, 0:P])
                x_done(ins)
            turned()
            for h in range(H8):
                ps = f_slot()
                for half_ in range(2):
                    ins = pe.matmul(ps[0:P, half_, 0:TH], pick[:, h, 0:P], asT[:, half_ * TH:half_ * TH + TH],
                                    start=True, stop=True)
                f_done(ins)
            pe.wait_ge(l2_kexp, 1)
            for tiles in ((0, 1, 2, 3), (4,)):
                ps = x_slot()
                for i in tiles:
                    ins = pe.transpose(ps[0:P, (i % 4) * 128:(i % 4) * 128 + 128], kx2[:, i * P:i * P + P], ident[:])
                x_done(ins)
            turned()
            ps = t_slot()
            for i in range(NT):
                ins = pe.matmul(ps[:, 0:128], v2m[:, i * 128:i * 128 + 128], k2m[:, i * 128:i * 128 + 128],
                                start=i == 0, stop=i == NT - 1)
            t_done(ins)
            pe.wait_ge(t_free, t.n)
            ps = t_slot()
            t_done(pe.matmul(ps[:, 0:D], ctT, W("l2_wout", 1)[:, 0, :], start=True, stop=True))
            pe.wait_ge(t_free, t.n)
            rows_of(lambda i: [(q2T[:, i * P:i * P + P], gw2)], D)
            pe.wait_ge(f_free, f.n)
            pe.wait_ge(t_free, t.n)
            pe.wait_ge(x_free, xr.n)
            pe.nop().then_inc(g_agg, NT)

            def spare_products(n):
                for _ in range(n):
                    pe.matmul(psX[:, 1, 0:2 * S], warm[:, 0:S], warm, start=True, stop=True)

            def target_rows():
                for k in range(2):
                    for lo, hi in ((0, 512), (512, N)):
                        ins = pe.matmul(wide(psF[0:P, k])[:, lo:hi], all_ones[:, 0:P],
                                        diagonal[k].rearrange("p m n -> p (m n)")[:, lo:hi], start=True, stop=True)
                ins.then_inc(g_rows, 1)

            def attend(at, following):
                if following:
                    pe.wait_ge(g_diag, at + 2)
                    pe.wait_ge(g_relu, at * NT + NT)
                    target_rows()
                spare_products(4)
                pe.wait_ge(g_he, at + 1)
                for n, j in enumerate(TILES):
                    pe.wait_ge(g_p, at * NT + (n + 1))
                    for lo, hi in ((0, 512), (512, N)):
                        ins = pe.matmul(wide(psT[0:HC + 1])[:, lo:hi], he_now[:, j, :], e_score[:, j, lo:hi],
                                        start=n == 0, stop=n == NT - 1)
                    ins.then_inc(g_agg, 1)

                spare_products(6)
                pe.wait_ge(g_out, at + 1)
                pe.wait_ge(g_norm, at + 1)
                for m in range(NT):
                    ins = pe.matmul(psX[0:P, 0, m * (HC + 1):(m + 1) * (HC + 1)], out_rows[:, m * P:m * P + P],
                                    ident[0:HC + 1, 0:HC + 1], start=True, stop=True)
                ins.then_inc(g_turn, 1)

            spare_products(72)
            pe.wait_ge(g_diag, 1)
            target_rows()
            with pe.Fori(0, H8 - 1) as i:
                attend(i, True)
            attend(H8 - 1, False)
            pe.wait_ge(g_norm, H8 + 1)
            turn_norm(6)
            turned()
            rows_of(linear(XT, W("l2_ffn")), D)
            pe.wait_ge(ld_small[3], 16)
            turn_norm(7)
            turned()
            rows_of(linear(XT, W("l3_qkv"), 0, 2 * D), 2 * D)
            rows_of(linear(XT, W("l3_w1")), D)
            rows_of(linear(XT, W("l3_qkv"), 2 * D, 3 * D), D)
            for c in range(KC):
                f_done(chunk_fm(f_slot(), lambda k: W("l3_qkv")[:, k, 2 * D + c * 128:2 * D + c * 128 + 128], XT, KC))
            pe.wait_ge(l3_y1, 1)
            rows_of(lambda m: [(A[:, j, m * P:m * P + P], y3[:, j, :]) for j in range(NT)] + linear(XT, W("l3_w0"))(m), D)
            pe.wait_ge(l3_kk, 1)
            ps = t_slot()
            for c in range(KC):
                for i in range(NT):
                    ins = pe.matmul(ps[:, c:c + 1], kk3[:, i, c * 128:c * 128 + 128], ones[0:P, 0:1],
                                    start=i == 0, stop=i == NT - 1)
            t_done(ins)
            ps = t_slot()
            for c in range(KC):
                for i in range(NT):
                    ins = pe.matmul(ps[:, c * D:c * D + D], v3[:, i, c * 128:c * 128 + 128], qk2[:, i, D:2 * D],
                                    start=i == 0, stop=i == NT - 1)
            t_done(ins)
            pe.wait_ge(t_free, t.n)
            ps = t_slot()
            for c in range(KC):
                for k in range(KC):
                    ins = pe.matmul(ps[:, c * D:c * D + D], kvT[:, k, c * 128:c * 128 + 128], W("l3_wout")[:, k, :],
                                    start=k == 0, stop=k == KC - 1)
            t_done(ins)
            pe.wait_ge(l3_q, 1)
            turn(qk2[:, :, 0:D])
            turned()
            pe.wait_ge(l3_gw, 1)
            pe.wait_ge(f_free, f.n)
            rows_of(lambda i: linear(vT3, W("l3_wout"))(i) + linear(qT3, gw3)(i), D)
            turn_norm(8)
            turned()
            router(2, W("l3_wr"), plan_items=True)
            item_products(items[1], 2, 1024, 8, 9)

        @block.vector
        def _(dve):
            t, xr, v, tf = Count(2), Count(2), Count(), Count()

            def V(ins):
                ins.then_inc(v_step, 1)
                v.n += 1
                return ins

            def settle():
                dve.wait_ge(v_step, v.at())

            def link(ins):
                V(ins)
                settle()

            def announce(what):
                settle()
                if t.n:
                    dve.wait_ge(t_free, t.n)
                dve.nop().then_inc(what, 1)

            def t_full_slot():
                dve.wait_ge(t_full, t.at(1))
                return psT[:, t.slot]

            def t_emptied(ins):
                ins.then_inc(t_free, 1)
                t.n += 1

            def t_settle():
                dve.wait_ge(t_free, t.n)

            def x_full_slot():
                dve.wait_ge(x_full, xr.n + 1)
                return psX[:, xr.slot]

            def x_emptied(ins):
                ins.then_inc(x_free, 1)
                xr.n += 1

            def turned_to(dst_fm):
                for c in range(KC):
                    ps = x_full_slot()
                    x_emptied(dve.tensor_copy(dst_fm[:, c, 0:4 * P], ps[:, 0:4 * P]))
                ps = x_full_slot()
                x_emptied(dve.tensor_copy(dst_fm[:, :, 4 * P:N], ps[:, 0:KC * P].rearrange("p (c n) -> p c n", c=KC)))

            norms = Count()

            def layer_norm(a, b, what=xn_ready, begun=False):
                for i in () if begun else range(NT):
                    V(dve.bn_stats(stats[:, i, :], a[:, i, 0:D]))
                settle()
                for i in range(NT):
                    V(dve.bn_aggr(mv[:, i, :], stats[:, i, :]))
                settle()
                dve.tensor_scalar(var_e[:], mv[:, :, 1], LN_EPS, None, ALU.add).then_inc(var_ready, 1)
                norms.n += 1
                dve.wait_ge(rstd_ready, norms.n)
                for i in range(NT):
                    ins = dve.tensor_scalar(b[:, i, 0:D], a[:, i, 0:D], mv[:, i, 0:1], rstd[:, i:i + 1],
                                            ALU.subtract, ALU.mult)
                    if what is None:
                        V(ins)
                    else:
                        ins.then_inc(what, 1)
                if what is None:
                    settle()

            def per_node(a):
                return a.unsqueeze(2).to_broadcast([P, NT, E])

            def router(n, bias, top2=False, shares=False):
                view = [s[:].rearrange("p (t e) -> p t e", e=E) for s in sm]
                ps = t_full_slot()
                t_emptied(dve.tensor_tensor(view[0], ps[0:P, 0:NT * E].rearrange("p (t e) -> p t e", e=E), row(bias), ALU.add))
                t_settle()
                link(dve.tensor_reduce(sm[2][:, 0:NT], view[0], AX.X, ALU.max))
                dve.tensor_tensor(view[1], view[0], per_node(sm[2][:, 0:NT]), ALU.subtract).then_inc(logit_ready, 1)
                dve.wait_ge(exp_ready, n)
                link(dve.tensor_reduce(sm[2][:, 0:NT], view[1], AX.X, ALU.add))
                link(dve.reciprocal(sm[2][:, 0:NT], sm[2][:, 0:NT]))
                link(dve.tensor_tensor(view[0], view[1], per_node(sm[2][:, 0:NT]), ALU.mult))
                if top2:
                    order3 = order[:].unsqueeze(1).to_broadcast([P, NT, E])
                    rest = view[0]
                    for first in (True, False):
                        pick_ = view[3 if first else 4]
                        link(dve.tensor_reduce(sm[2][:, 0:NT], rest, AX.X, ALU.max))
                        link(dve.tensor_tensor(view[5], rest, per_node(sm[2][:, 0:NT]), ALU.is_equal))
                        link(dve.tensor_tensor(view[5], view[5], order3, ALU.mult))
                        link(dve.tensor_reduce(sm[2][:, 0:NT], view[5], AX.X, ALU.max))
                        link(dve.tensor_tensor(pick_, view[5], per_node(sm[2][:, 0:NT]), ALU.is_equal))
                        if first:
                            rest = view[6]
                            link(dve.scalar_tensor_tensor(out=sm[6][:], in0=sm[3][:], scalar=-4.0, in1=sm[0][:],
                                                          op0=ALU.mult, op1=ALU.add))
                    link(dve.tensor_tensor(sm[3][:], sm[3][:], sm[4][:], ALU.add))
                    link(dve.tensor_tensor(sm[0][:], sm[0][:], sm[3][:], ALU.mult))
                    if shares:
                        link(dve.tensor_reduce(sm[2][:, 0:NT], view[0], AX.X, ALU.add))
                        link(dve.reciprocal(sm[2][:, 0:NT], sm[2][:, 0:NT]))
                        link(dve.tensor_tensor(view[0], view[0], per_node(sm[2][:, 0:NT]), ALU.mult))
                    V(dve.tensor_copy(chosen[:, 0:NT, :], view[3]))
                    V(dve.memset(chosen[:, NT, :], 0.0))
                    V(dve.memset(choice_sum[:, 0, :], 0.0))
                    link(dve.tensor_copy(choice_sum[:, 1, :], view[3][:, 0, :]))
                    for m in range(1, NT):
                        link(dve.tensor_tensor(choice_sum[:, m + 1, :], choice_sum[:, m, :], view[3][:, m, :], ALU.add))
                dve.tensor_copy(CW[:].rearrange("p e t -> p t e"), view[0]).then_inc(cw_ready, 1)
                if top2:
                    ps = x_full_slot()
                    V(dve.tensor_copy(n_chosen, ps[:, NT * E:(NT + 1) * E]))
                    x_emptied(dve.scalar_tensor_tensor(out=rank_p1, in0=ps[0:P, 0:NT * E].rearrange("p (t e) -> p t e", e=E),
                                                       scalar=1.0, in1=view[3], op0=ALU.add, op1=ALU.mult))
                for lo, n_ in ((0, 4 * P), (4 * P, P)):
                    ps = x_full_slot()
                    x_emptied(dve.tensor_copy(CWT[:, lo:lo + n_], ps[0:E, 0:n_]))
                if not top2:
                    add_rows(X, X)

            def across(a, n):
                return a.unsqueeze(2).to_broadcast([128, a.shape[1], n])

            def along(a, n):
                return a.unsqueeze(1).to_broadcast([128, n, a.shape[1]])

            def plan_items(q):
                count = 2 * PAIRS + 1
                dve.wait_ge(x_free, xr.n)
                settle()
                V(dve.tensor_scalar(rank.rearrange("p e t -> p t e"), rank_p1, -1.0, None, ALU.add))
                link(dve.tensor_tensor(by_tile, across(n_chosen, NT), along(tile_end[:], E), ALU.is_gt))
                link(dve.tensor_reduce(n_tiles, by_tile, AX.X, ALU.add))
                link(dve.tensor_tensor(by_expert, along(n_tiles, E), upto[:], ALU.mult))
                link(dve.tensor_reduce(e_end, by_expert, AX.X, ALU.add))
                V(dve.tensor_tensor(e_start, e_end, n_tiles, ALU.subtract))
                V(dve.tensor_scalar(by_pair, pair_no[:], e_end[:, E - 1:E], None, ALU.is_lt))
                link(dve.tensor_tensor(by_item, along(e_end, count), across(item_no[:], E), ALU.is_le))
                V(dve.tensor_reduce(item_e, by_item, AX.X, ALU.add))
                V(dve.tensor_reduce(n_pairs, by_pair, AX.X, ALU.add))
                link(dve.tensor_tensor(by_item2, along(e_start, count), across(item_no[:], E), ALU.is_le))
                V(dve.tensor_scalar(plan[:, 0:count], item_e[0:1, :], float(E - 1), None, ALU.min))
                V(dve.tensor_copy(plan[:, count:count + 1], n_pairs[0:1, :]))
                link(dve.tensor_tensor(by_item2, by_item2, along(e_start, count), ALU.mult))
                link(dve.tensor_reduce(item_start, by_item2, AX.X, ALU.max))
                link(dve.tensor_tensor(item_off, item_no[:], item_start, ALU.subtract))
                link(dve.tensor_scalar(item_off, item_off, float(S), None, ALU.mult))
                announce(q.plan)

            def add_items(q, norm=False):
                pairs = dve.value_load(plan[0:1, 2 * PAIRS + 1:2 * PAIRS + 2], min_val=1, max_val=PAIRS)
                own = Count()

                def own_step(ins):
                    ins.then_inc(q.step, 1)
                    own.n += 1
                    dve.wait_ge(q.step, own.at())

                def fill_slots(b, e, at):
                    own_step(dve.tensor_scalar(rank_item[b].unsqueeze(1), rank[:, bass.ds(e, 1), :], item_off[0:P, at],
                                               None, ALU.subtract))
                    for j in range(NT):
                        ins = dve.tensor_scalar(hot_in[b][:, j, :], slot_no[:], rank_item[b][:, j:j + 1], None, ALU.is_equal)
                    ins.then_inc(q.hot, 1)

                def expert(at):
                    return dve.value_load(plan[0:1, at], min_val=0, max_val=E - 1)

                dve.nop().then_inc(q.o_free, 3)
                fill_slots(0, expert(slice(0, 1)), slice(0, 1))
                if norm:
                    layer_norm(XN, XN)
                add_rows(X, X)
                with dve.Fori(0, pairs) as i:
                    own.enter(i, 2 * 2)
                    for b in range(2):
                        e = expert(bass.ds(i * 2 + b, 1))
                        after = bass.ds(i * 2 + (b + 1), 1)
                        e_next = expert(after)
                        dve.wait_ge(q.hot_full, i * 2 + (b + 1))
                        fill_slots(1 - b, e_next, after)
                        dve.wait_ge(q.y_full, i * 2 + (b + 3))
                        own_step(dve.tensor_copy(y_item[:, 0, :], psX[:, 1, 0:D]))
                        dve.tensor_tensor(y_item[:, 1, :], psX[:, 1, 0:D], y_item[:, 0, :], ALU.subtract).then_inc(q.y_ready, 1)
                        for j in range(NT):
                            bank = i * 6 + (b * 3 + j // 2 + 1)
                            if j % 2 == 0:
                                dve.wait_ge(q.o_full, bank)
                                dve.wait_ge(q.o_free, bank)
                            ins = dve.scalar_tensor_tensor(out=X[:, j, :], in0=tile_out(j), scalar=CW[:, bass.ds(e, 1), j],
                                                           in1=X[:, j, :], op0=ALU.mult, op1=ALU.add)
                            if j in (1, 3, 4):
                                ins.then_inc(q.o_free, 1)
                dve.wait_ge(q.o_free, pairs * 6 + 3)

            def add_experts():
                with dve.Fori(0, E // 2) as i:
                    t.enter(i, 2 * NT)
                    for b in range(2):
                        for m in range(NT):
                            ps = t_full_slot()
                            dve.wait_ge(t_free, t.at(-NT + 1))
                            t_emptied(dve.scalar_tensor_tensor(out=X[:, m, :], in0=ps[0:P, 0:D],
                                                               scalar=CW[:, bass.ds(i * 2 + b, 1), m],
                                                               in1=X[:, m, :], op0=ALU.mult, op1=ALU.add))
                    t.leave(E // 2)

            def add_rows(a, b, norm=False):
                for i in range(NT):
                    ps = t_full_slot()
                    t_emptied(dve.tensor_tensor(a[:, i, 0:D], ps[0:P, 0:D], b[:, i, :], ALU.add))
                    if norm and i:
                        dve.wait_ge(t_free, t.n - 1)
                        V(dve.bn_stats(stats[:, i - 1, :], a[:, i - 1, 0:D]))
                if norm:
                    t_settle()
                    V(dve.bn_stats(stats[:, NT - 1, :], a[:, NT - 1, 0:D]))

            dve.wait_ge(consts, 1)
            dve.wait_ge(ld_idx, 32)
            link(dve.tensor_copy(idx_float, idx[:]))
            link(dve.tensor_reduce(ends[:, 0:1], idx_float[:, 1, :], AX.X, ALU.min))
            dve.tensor_reduce(ends[:, 1:2], idx_float[:, 1, :], AX.X, ALU.max).then_inc(idx_f, 1)
            ps = x_full_slot()
            for w in range(2):
                V(dve.tensor_copy(idxT[:, w, 0:G, :].rearrange("p g r -> p r g"),
                                  ps[0:P, w * R * G:(w + 1) * R * G].rearrange("p (r g) -> p r g", g=G)))
            x_emptied(dve.tensor_copy(endsT[:].rearrange("p a g -> p (a g)"), ps[0:1, 2 * R * G:(2 * R + 2) * G]))
            dve.wait_ge(x_free, xr.n)
            high, low = (endsT[:, w, :].unsqueeze(1).to_broadcast([1, NT, G]) for w in (1, 0))
            held = span[:, :, 0, :]
            V(dve.tensor_tensor(held, high, tile_start[:], ALU.is_ge))
            link(dve.scalar_tensor_tensor(out=span[:, :, 1, :], in0=low, scalar=float(-P), in1=tile_start[:],
                                          op0=ALU.add, op1=ALU.is_lt))
            link(dve.tensor_tensor(held, held, span[:, :, 1, :], ALU.mult))
            link(dve.tensor_tensor(span[:, :, 1, :], held, group_no[:, 1, :].unsqueeze(1).to_broadcast([1, NT, G]), ALU.mult))
            link(dve.tensor_tensor(held, held, group_no[:, 0, :].unsqueeze(1).to_broadcast([1, NT, G]), ALU.mult))
            link(dve.tensor_reduce(bounds[:, 0, :], span[:, :, 0, :], AX.X, ALU.max))
            link(dve.tensor_scalar(bounds[:, 0, :], bounds[:, 0, :], -1.0, float(G), ALU.mult, ALU.add))
            link(dve.tensor_scalar(bounds[:, 0, :], bounds[:, 0, :], float(G - 1), None, ALU.min))
            link(dve.tensor_reduce(last[:], span[:, :, 1, :], AX.X, ALU.max))
            link(dve.tensor_tensor(bounds[:, 1, :], last[:], bounds[:, 0, :], ALU.subtract))
            link(dve.tensor_scalar(bounds[:, 1, :], bounds[:, 1, :], 1.0, None, ALU.max))
            link(dve.memset(bounds[:, 2, 0:1], 0.0))
            for m in range(1, NT):
                link(dve.tensor_tensor(bounds[:, 2, m:m + 1], bounds[:, 2, m - 1:m], bounds[:, 1, m - 1:m], ALU.add))
            dve.tensor_copy(bounds_i[:], bounds[:]).then_inc(bounds_ready, 1)

            dve.wait_ge(ld_x, 16)
            layer_norm(X, XN)
            turned_to(XT)
            dve.wait_ge(bounds_ready, 1)
            first = [dve.value_load(bounds_i[0:1, 0, m:m + 1], min_val=0, max_val=G - 1) for m in range(NT)]
            count = [dve.value_load(bounds_i[0:1, 1, m:m + 1], min_val=1, max_val=G) for m in range(NT)]
            before = [dve.value_load(bounds_i[0:1, 2, m:m + 1], min_val=0, max_val=G * NT) for m in range(NT)]
            for m in range(NT):
                with dve.Fori(0, count[m]) as j:
                    for r in range(R):
                        if r % 2 == 0:
                            dve.wait_ge(hot_used, (before[m] + j) * 2 + (r // 2 + 1))
                        dve.tensor_scalar(hot_src[:, r, :], iota[:], idxT[:, 0, bass.ds(first[m] + j, 1), r],
                                          None, ALU.is_equal)
                        ins = dve.tensor_scalar(hot_dst[:, r, 0:P], iota[:, m * P:m * P + P],
                                                idxT[:, 1, bass.ds(first[m] + j, 1), r], None, ALU.is_equal)
                        if r % 2:
                            ins.then_inc(hot_ready, 1)
            heads = [s[:].rearrange("p (t h) -> p t h", h=H8) for s in sm]

            def by_head(a):
                return a.rearrange("p t (h c) -> p t h c", c=HC)

            def per_head(a):
                return a.unsqueeze(3).to_broadcast([P, NT, H8, HC])

            dve.wait_ge(consts, 2)
            dve.wait_ge(xn_ready, NT)
            link(dve.tensor_reduce(heads[0], by_head(XN[:, :, 0:D]), AX.X, ALU.add))
            link(dve.tensor_scalar(sm[0][:], sm[0][:], 1.0 / HC, None, ALU.mult))
            link(dve.tensor_tensor(by_head(y0[:]), by_head(XN[:, :, 0:D]), per_head(heads[0]), ALU.subtract))
            link(dve.tensor_tensor(sq0[:], y0[:], y0[:], ALU.mult))
            dve.tensor_reduce(heads[1], by_head(sq0[:]), AX.X, ALU.add).then_inc(l0_std, 1)
            dve.wait_ge(l0_std_r, 1)
            link(dve.tensor_scalar(sm[1][:], sm[1][:], 1e-5, None, ALU.add))
            link(dve.reciprocal(sm[1][:], sm[1][:]))
            link(dve.tensor_tensor(by_head(y0[:]), by_head(y0[:]), per_head(heads[1]), ALU.mult))
            dve.wait_ge(ld_rows, 16)
            V(dve.tensor_tensor(k0[:], y0[:], row("l0_kw"), ALU.mult))
            link(dve.tensor_tensor(v0[:], y0[:], row("l0_vw"), ALU.mult))
            link(dve.tensor_tensor(k0[:], k0[:], row("l0_kb"), ALU.add))
            dve.tensor_tensor(v0[:], v0[:], row("l0_vb"), ALU.add).then_inc(l0_kv, 1)
            for m in range(NT):
                ps = t_full_slot()
                link(dve.tensor_scalar(inv_deg[:, m:m + 1], ps[0:P, D:D + 1], 1.0, None, ALU.max))
                link(dve.reciprocal(inv_deg[:, m:m + 1], inv_deg[:, m:m + 1]))
                t_emptied(dve.tensor_scalar(ag[:, m, :], ps[0:P, 0:D], inv_deg[:, m:m + 1], None, ALU.mult))
            for k in range(6):
                V(dve.tensor_scalar(inv_deg_k[:, k, :], inv_deg[:], 1.0 / (k + 1), None, ALU.mult))
            turned_to(agT)
            ps = t_full_slot()
            dve.wait_ge(ld_small[0], 16)
            link(dve.tensor_copy(wc[:], W("l0_wr")))
            for c in range(KC):
                at = wc[:, c, c * 128:c * 128 + 128]
                link(dve.tensor_tensor(at, at, ident[:], ALU.add))
                ins = dve.scalar_tensor_tensor(out=kv0[:, c, :], in0=ps[:, c * 128:c * 128 + 128], scalar=1.0 / N,
                                               in1=headmask[:], op0=ALU.mult, op1=ALU.mult)
                V(ins) if c == 0 else t_emptied(ins)
            settle()
            t_settle()
            for c in range(KC):
                at = wc[:, c, c * 128:c * 128 + 128]
                ins = dve.tensor_tensor(at, at, kv0[:, c, :], ALU.add)
            ins.then_inc(l0_w, 1)
            dve.wait_ge(xb_ready, 1)
            add_rows(X, XB, norm=True)
            announce(x_ready)
            layer_norm(X, XN, begun=True)
            turned_to(XT)
            router(1, "l0_gb", top2=True)
            plan_items(items[0])
            add_items(items[0])
            announce(x_ready)
            layer_norm(X, XN)
            turned_to(XT)
            dve.wait_ge(ld_cols, 32)
            V(dve.tensor_scalar(v12[:, 0, :], col("v1"), 1e-3, None, ALU.add))
            V(dve.tensor_scalar(v12[:, 1, :], col("v2"), 1e-3, None, ALU.add))
            announce(bn_v)
            add_rows(u_pre, row("l1_bin"))
            announce(l1_pre)
            for i in range(NT):
                ps = t_full_slot()
                dve.tensor_scalar(k_neg[:, i, :], ps[0:P, 0:D], 0.0, None, ALU.min).then_inc(l1_kmin, 1)
                V(dve.tensor_scalar(k1[:, i, :], ps[0:P, 0:D], 0.0, None, ALU.max))
                t_emptied(dve.tensor_copy(v1m[:, i, :], ps[0:P, D:2 * D]))
            settle()
            dve.wait_ge(l1_kexp, 1)
            dve.tensor_tensor(k1[:], k1[:], k_neg[:], ALU.add).then_inc(l1_k, 1)
            dve.wait_ge(l1_q, 1)
            dve.tensor_tensor(q_pos[:], q_pos[:], q_neg[:], ALU.add).then_inc(l1_qT, 1)
            ps = t_full_slot()
            for c in range(KC):
                V(dve.tensor_scalar(bd[:, c, 128:132], headcols[:], ps[:, D + c:D + c + 1], None, ALU.mult))
                ins = dve.tensor_tensor(bd[:, c, 0:128], ps[:, c * 128:c * 128 + 128], headmask[:], ALU.mult)
                V(ins) if c == 0 else t_emptied(ins)
            announce(l1_bd)
            for i in range(NT):
                ps = t_full_slot()
                p3 = ps[0:P, 0:KC * 132].rearrange("p (c n) -> p c n", c=KC)
                z = sm[i][:, 0:8].rearrange("p (c h) -> p c h", c=KC)
                link(dve.tensor_scalar(z, p3[:, :, 128:132], 1e-6, None, ALU.add))
                link(dve.reciprocal(sm[i][:, 0:8], sm[i][:, 0:8]))
                for c in range(KC):
                    ins = dve.tensor_tensor(mix[:, i, c * 128:c * 128 + 128].rearrange("p (h e) -> p h e", e=HC),
                                            p3[:, c, 0:128].rearrange("p (h e) -> p h e", e=HC),
                                            z[:, c, :].unsqueeze(2).to_broadcast([P, 4, HC]), ALU.mult)
                    V(ins) if c == 0 else t_emptied(ins)
            t_settle()
            settle()
            link(dve.tensor_tensor(mix[:], mix[:], XN[:, :, 0:D], ALU.add))
            layer_norm(mix, x1m, None)
            link(dve.tensor_tensor(x1m[:], x1m[:], row("l1_g1"), ALU.mult))
            dve.tensor_tensor(x1m[:], x1m[:], row("l1_b1"), ALU.add).then_inc(l1_x1, 1)
            V(dve.memset(x1T[:, :, N:TP], 0.0))
            turned_to(x1T)
            dve.wait_ge(bn_r, 1)
            for w, s, o in ((0, s1, o1), (1, s2, o2)):
                V(dve.tensor_tensor(s[:], v12[:, w, :], col(f"g{w + 1}"), ALU.mult))
                link(dve.tensor_tensor(o[:], col(f"b{w + 1}"), col(f"m{w + 1}"), ALU.subtract))
                link(dve.tensor_tensor(o[:], o[:], s[:], ALU.mult))
                link(dve.tensor_tensor(o[:], o[:], col(f"be{w + 1}"), ALU.add))
            announce(bn_ready)
            dve.wait_ge(l1_x1b, 1)
            add_rows(mix, x1b, norm=True)
            layer_norm(mix, mix, None, begun=True)
            link(dve.tensor_tensor(mix[:], mix[:], row("l1_g2"), ALU.mult))
            link(dve.tensor_tensor(mix[:], mix[:], row("l1_be2"), ALU.add))
            dve.wait_ge(xb_ready, 2)
            link(dve.tensor_tensor(XB[:], XB[:], mix[:], ALU.add))
            with dve.Fori(0, 3) as i:
                t.enter(i, 2 * NT)
                for b in range(2):
                    for m in range(NT):
                        ps = t_full_slot()
                        if m == 0:
                            dve.wait_ge(l1_sum, i * 2 + (b + 1))
                        ins = dve.tensor_scalar(term[1 - b][:, m, :], ps[0:P, 0:D],
                                                inv_deg_k[:, bass.ds(i * 2 + b, 1), m], None, ALU.mult)
                        t_emptied(ins)
                    dve.wait_ge(t_free, t.at())
                    dve.nop().then_inc(l1_term, 1)
                t.leave(3)
            turned_to(totalT)
            add_rows(X, XB, norm=True)
            announce(x_ready)
            layer_norm(X, XN, begun=True)
            turned_to(XT)
            router(2, "l1_br")
            add_experts()
            announce(x_ready)
            layer_norm(X, XN)
            turned_to(XT)
            for i in range(NT):
                ps = t_full_slot()
                t_emptied(dve.tensor_copy(he[:, i, :, 0:HC], ps[0:P, 0:D].rearrange("p (h c) -> p h c", c=HC)))
            t_settle()
            for w, name in ((0, "l2_as"), (1, "l2_ad")):
                a, b = ROWS[name]
                for i in range(NT):
                    V(dve.tensor_tensor(hm[:, i, :].rearrange("p (h c) -> p h c", c=HC), he[:, i, :, 0:HC],
                                        w_rows[:, a:b].rearrange("p (h c) -> p h c", c=HC), ALU.mult))
                settle()
                V(dve.tensor_reduce(hsum[:, w], by_head(hm[:]), AX.X, ALU.add))
                settle()
            V(dve.tensor_scalar(as2[:], hsum[:, 0], 0.2, None, ALU.mult))
            V(dve.tensor_scalar(as8[:], hsum[:, 0], 0.8, None, ALU.mult))
            V(dve.tensor_copy(ad_t[:], ad_h))
            announce(l2_ab)
            for tiles, lo in (((0, 1, 2, 3), 0), ((4,), 512)):
                ps = t_full_slot()
                t_emptied(dve.tensor_copy(v2m[:, lo:lo + len(tiles) * 128], ps[0:P, 0:len(tiles) * 128]))
            for lo, n_ in ((0, 4 * P), (4 * P, P)):
                ps = x_full_slot()
                x_emptied(dve.tensor_copy(asT[:, lo:lo + n_], ps[0:H8, 0:n_]))
            dve.wait_ge(f_free, F_K2)
            link(dve.tensor_reduce(kcol[:, 2:3], k2T[:, 0:N], AX.X, ALU.max))
            dve.tensor_scalar(kcol[:, 0:1], kcol[:, 2:3], -1.0, None, ALU.mult).then_inc(l2_kmax, 1)
            for tiles, lo in (((0, 1, 2, 3), 0), ((4,), 512)):
                ps = x_full_slot()
                x_emptied(dve.tensor_copy(k2m[:, lo:lo + len(tiles) * 128], ps[0:P, 0:len(tiles) * 128]))
            ps = t_full_slot()
            t_emptied(dve.tensor_tensor(ctT, ps[:, 0:128], headmask[:], ALU.mult))
            link(dve.reciprocal(kcol[:, 3:4], kcol[:, 1:2]))
            ps = t_full_slot()
            t_emptied(dve.tensor_scalar(gw2, ps[:, 0:D], kcol[:, 3:4], HC ** -0.5, ALU.mult, ALU.mult))
            dve.wait_ge(xb_ready, 3)
            add_rows(XB, XB)
            t_settle()
            for m in range(NT):
                V(dve.tensor_scalar(no_edge[:, m, :], A[:, m, :], 0.0, NO_EDGE, ALU.is_equal, ALU.mult))
            settle()
            dve.wait_ge(f_free, F_K2 + H8)

            def head_row(h):
                V(dve.tensor_copy(a_now[:], a_row[:, h, 0:N].rearrange("p a n -> p (a n)")))
                settle()
                dve.memset(kcol[:, 7:8], 0.0)

            def highest(m):
                V(dve.tensor_tensor_reduce(out=masked_row[m % 2], in0=a_now[:], in1=no_edge[:, m, :],
                                           scale=1.0, scalar=-3e38, op0=ALU.add, op1=ALU.max,
                                           accum_out=mx[:, m:m + 1]))

            def shifts(h):
                adh, zh, gh, sh = (y[:, h, :].rearrange("p a n -> p (a n)") for y in (ad_h, z2, gm, shift))
                settle()
                link(dve.tensor_tensor(zh, mx[:], adh, ALU.add))
                link(dve.scalar_tensor_tensor(out=gh, in0=zh, scalar=0.2, in1=zh, op0=ALU.mult, op1=ALU.max))
                dve.scalar_tensor_tensor(out=sh, in0=adh, scalar=0.2, in1=gh, op0=ALU.mult, op1=ALU.subtract)\
                   .then_inc(g_shift, 1)

            def edges_times(at, n):
                settle()
                j = TILES[n]
                dve.wait_ge(g_exp, at * NT + (NT + n + 1))
                dve.scalar_tensor_tensor(out=e_score[:, j, :], in0=e_score[:, j, :], scalar=1.0, in1=AT[:, j, :],
                                         op0=ALU.min, op1=ALU.mult).then_inc(g_p, 1)

            def head(h, at, following=None):
                for n, j in enumerate(V_TILES):
                    dve.wait_ge(g_shift_row, at + 1)
                    dve.wait_ge(g_relu, at * NT + (j + 1))
                    dve.tensor_tensor(score[:, j, :], score[:, j, :], shift_row, ALU.add).then_inc(g_sum_v, 1)
                if following is not None:
                    head_row(following)
                reduced = 0
                for step in "R0R1R2R34R":
                    if step != "R":
                        edges_times(at, int(step))
                    elif following is not None:
                        highest(reduced)
                        reduced += 1
                if following is not None:
                    shifts(following)
                dve.wait_ge(g_agg, at * NT + 2 * NT)
                dve.tensor_copy(out_rows, wide(psT[0:HC + 1])).then_inc(g_out, 1)
                dve.wait_ge(g_turn, at + 1)
                p3 = psX[0:P, 0, 0:NT * (HC + 1)].rearrange("p (m n) -> p m n", m=NT)
                link(dve.tensor_scalar(den[:], p3[:, :, HC], 1e-16, None, ALU.add))
                link(dve.reciprocal(den[:], den[:]))
                dve.tensor_tensor(ACC[:].rearrange("p t (h c) -> p t h c", c=HC)[:, :, h, :].rearrange("p t a c -> p t (a c)"),
                                  p3[:, :, 0:HC], den[:].unsqueeze(2).to_broadcast([P, NT, HC]), ALU.mult).then_inc(g_norm, 1)

            dve.nop().then_inc(g_norm, 1)
            for h in range(2):
                head_row(bass.ds(h, 1))
                for m in range(NT):
                    highest(m)
                    settle()
                shifts(bass.ds(h, 1))
            with dve.Fori(0, H8 - 2) as i:
                v.enter(i, NT + 5)
                head(bass.ds(i, 1), i, bass.ds(i + 2, 1))
                v.leave(H8 - 2)
            for h in (H8 - 2, H8 - 1):
                head(bass.ds(h, 1), h)
            dve.wait_ge(g_norm, H8 + 1)
            link(dve.tensor_tensor(ACC[:], ACC[:], row("l2_bias"), ALU.add))
            link(dve.tensor_scalar(ACC[:], ACC[:], 0.0, None, ALU.max))
            dve.tensor_tensor(X[:], XB[:], ACC[:], ALU.add).then_inc(x_ready, 1)
            dve.wait_ge(x_ready, 5)
            layer_norm(X, XN)
            turned_to(XT)
            dve.wait_ge(xb_ready, 4)
            add_rows(X, XB, norm=True)
            announce(x_ready)
            layer_norm(X, XN, begun=True)
            turned_to(XT)
            a, b = ROWS["l3_bqk"]
            for i in range(NT):
                ps = t_full_slot()
                t_emptied(dve.tensor_tensor(qk[:, i, :], ps[0:P, :], w_rows[:, a:b], ALU.add))
            t_settle()
            link(dve.tensor_reduce(sm[0][:, 0:2 * NT], qk[:].rearrange("p t (w n) -> p (t w) n", n=D), AX.X, ALU.add))
            dve.tensor_scalar(sm[0][:, 0:2 * NT], sm[0][:, 0:2 * NT], -1.0 / D, None, ALU.mult).then_inc(l3_qk, 1)
            for i in range(NT):
                ps = t_full_slot()
                t_emptied(dve.tensor_copy(y3[:, i, :], ps[0:P, 0:D]))
            announce(l3_y1)
            add_rows(v3, row("l3_bv"))
            dve.wait_ge(l3_sq, 1)
            link(dve.tensor_scalar(sm[1][:, 0:2 * NT], sm[1][:, 0:2 * NT], 1e-7, None, ALU.add))
            link(dve.reciprocal(sm[1][:, 0:2 * NT], sm[1][:, 0:2 * NT]))
            for i in range(NT):
                for w in range(2):
                    V(dve.tensor_scalar(qk2[:, i, w * D:w * D + D], qk2[:, i, w * D:w * D + D],
                                        sm[1][:, 2 * i + w:2 * i + w + 1], None, ALU.mult))
            announce(l3_qn)
            for i in range(NT):
                ps = t_full_slot()
                t_emptied(dve.tensor_scalar(gnn3[:, i, :], ps[0:P, 0:D], 0.0, None, ALU.max))
            announce(l3_gnn)
            dve.wait_ge(l3_nr, 1)
            link(dve.tensor_scalar(sm[4][:, 0:NT], sm[4][:, 0:NT], 1e-12, None, ALU.max))
            link(dve.reciprocal(sm[4][:, 0:NT], sm[4][:, 0:NT]))
            for i in range(NT):
                ins = dve.tensor_scalar(qk2[:, i, 0:D], qk2[:, i, 0:D], sm[4][:, i:i + 1], None, ALU.mult)
            ins.then_inc(l3_q, 1)
            ps = t_full_slot()
            t_emptied(dve.tensor_copy(kcol[:, 0:KC], ps[:, 0:KC]))
            announce(l3_kn2)
            ps = t_full_slot()
            t_emptied(dve.tensor_copy(kvT[:].rearrange("p c n -> p (c n)"), ps[:]))
            dve.wait_ge(l3_knr, 1)
            link(dve.tensor_scalar(kcol[:, 0:KC], kcol[:, 0:KC], 1e-12, None, ALU.max))
            link(dve.reciprocal(kcol[:, 0:KC], kcol[:, 0:KC]))
            ps = t_full_slot()
            V(dve.tensor_scalar(gw3[:, 0, :], ps[:, 0:D], kcol[:, 0:1], N ** -0.5, ALU.mult, ALU.mult))
            t_emptied(dve.tensor_scalar(gw3[:, 1, :], ps[:, D:2 * D], kcol[:, 1:2], N ** -0.5, ALU.mult, ALU.mult))
            announce(l3_gw)
            turned_to(qT3)
            dve.wait_ge(xb_ready, 6)
            add_rows(X, XB, norm=True)
            announce(x_ready)
            layer_norm(X, XN, begun=True)
            turned_to(XT)
            router(3, "l3_br", top2=True, shares=True)
            plan_items(items[1])
            add_items(items[1], norm=True)
            announce(x_ready)


_INPUTS = ["x", "src", "dst"]


def kernel(**inputs):
    import numpy as _np
    import concourse.bacc as _bacc
    from concourse import mybir as _mybir
    from concourse.bass_utils import run_bass_kernel_spmd as _run

    a = {k: _np.asarray(v) for k, v in inputs.items()}

    def chunks(w):
        return w.reshape(-1, 128, w.shape[-1]).transpose(1, 0, 2).reshape(128, -1)

    def packed(table, parts):
        assert list(parts) == [n for n in table if n != "end"]
        return _np.ascontiguousarray(_np.concatenate(list(parts.values()), axis=-1))

    def columns(v):
        return v.reshape(-1, 128).T

    small = packed(SMALL, {
        "l0_wl": chunks(a["L0_gnn_W_l"].T), "l0_wr": chunks(a["L0_gnn_W_r"].T), "l0_gate": chunks(a["L0_ffn_gate_w"]),
        "l1_win": chunks(a["L1_gnn_W_in"].T), "l1_qkv": chunks(a["L1_mix_Wqkv"].T), "l1_w1": chunks(a["L1_mix_W1"].T),
        "l1_w2": chunks(a["L1_mix_W2"].T), "l1_wout": chunks(a["L1_gnn_W_out"].T), "l1_wr": chunks(a["L1_ffn_Wr"]),
        "l2_w": chunks(a["L2_gnn_W"].reshape(D, D)), "l2_qkv": chunks(a["L2_mix_W_qkv"]),
        "l2_wout": chunks(a["L2_mix_W_out"]), "l2_ffn": chunks(a["L2_ffn_weight"].T),
        "l3_w0": chunks(a["L3_gnn_w0"]), "l3_w1": chunks(a["L3_gnn_w1"]), "l3_qkv": chunks(a["L3_mix_W_qkv"]),
        "l3_wout": chunks(a["L3_mix_W_out"]), "l3_wr": chunks(a["L3_ffn_Wr"])})
    bqkv = a["L3_mix_b_qkv"]
    rows = packed(ROWS, {
        "l0_br": a["L0_gnn_b_r"], "l0_kw": a["L0_mix_kln_weight"].reshape(-1), "l0_kb": a["L0_mix_kln_bias"].reshape(-1),
        "l0_vw": a["L0_mix_vln_weight"].reshape(-1), "l0_vb": a["L0_mix_vln_bias"].reshape(-1),
        "l0_gb": a["L0_ffn_gate_b"], "l1_bin": a["L1_gnn_b_in"], "l1_bout": a["L1_gnn_b_out"],
        "l1_g1": a["L1_mix_ln1_g"], "l1_b1": a["L1_mix_ln1_b"], "l1_b2": a["L1_mix_b2"], "l1_g2": a["L1_mix_ln2_g"],
        "l1_be2": a["L1_mix_ln2_b"], "l1_br": a["L1_ffn_br"], "l2_as": a["L2_gnn_att_src"].reshape(-1),
        "l2_ad": a["L2_gnn_att_dst"].reshape(-1), "l2_bias": a["L2_gnn_bias"], "l2_bout": a["L2_mix_b_out"],
        "l2_ffnb": a["L2_ffn_bias"], "l3_bqk": bqkv[:2 * D], "l3_bv": bqkv[2 * D:], "l3_bout": a["L3_mix_b_out"],
        "l3_br": a["L3_ffn_br"]})
    cols = packed(COLS, {
        "l0_b1": columns(a["L0_ffn_b1"]), "l1_mb1": columns(a["L1_mix_b1"]),
        "b1": columns(a["L1_ffn_b1"]), "g1": columns(a["L1_ffn_g1"]), "be1": columns(a["L1_ffn_be1"]),
        "m1": columns(a["L1_ffn_m1"]), "v1": columns(a["L1_ffn_v1"]),
        "b2": columns(a["L1_ffn_b2"]), "g2": columns(a["L1_ffn_g2"]), "be2": columns(a["L1_ffn_be2"]),
        "m2": columns(a["L1_ffn_m2"]), "v2": columns(a["L1_ffn_v2"]), "l3_bv": columns(bqkv[2 * D:]),
        "l3_g": columns(a["L3_ffn_ln_g"]), "l3_b": columns(a["L3_ffn_ln_b"]), "l3_b1": columns(a["L3_ffn_b1"])})
    eb2 = _np.ascontiguousarray(_np.stack([a["L0_ffn_b2"], a["L1_ffn_bo"], a["L3_ffn_b2"]], axis=1))

    def experts(*layers):
        return _np.ascontiguousarray(_np.stack([_np.concatenate([chunks(w[e]) for w in layers], axis=1) for e in range(E)]))

    arrays = {"x": a["x"], "src": a["src"], "dst": a["dst"], "small": small, "rows": rows, "cols": cols, "eb2": eb2,
              "ffn0": experts(a["L0_ffn_W1"], a["L0_ffn_W2"]),
              "ffn1": experts(a["L1_ffn_W1"], a["L1_ffn_W2"], a["L1_ffn_Wo"]),
              "ffn3": experts(a["L3_ffn_W1"], a["L3_ffn_W2"])}
    arrays = {f"in_{k}": _np.ascontiguousarray(v) for k, v in arrays.items()}
    nc = _bacc.Bacc("TRN2", target_bir_lowering=False, num_devices=1)
    args = [nc.dram_tensor(k, v.shape, _mybir.dt.from_np(v.dtype), kind="ExternalInput").ap() for k, v in arrays.items()]
    args.append(nc.dram_tensor("out_x", (N, D), F32, kind="ExternalOutput").ap())
    gps_network(nc, *args)
    r = _run(nc, [arrays], core_ids=[0])
    return r.results[0]["out_x"]
```
